# Optimizing a Trainium2 kernel written in Bass

```python
import numpy as np
import jax
import jax.numpy as jnp

def _softmax(x, axis=-1):
    return jax.nn.softmax(x, axis=axis)

def _gelu(x):
    return jax.nn.gelu(x, approximate=True)

def _silu(x):
    return jax.nn.silu(x)

def _sigmoid(x):
    return jax.nn.sigmoid(x)

def _layernorm(x, axis=-1, eps=1e-05):
    m = jnp.mean(x, axis=axis, keepdims=True)
    v = jnp.var(x, axis=axis, keepdims=True)
    return (x - m) / jnp.sqrt(v + eps)

def _scatter_add(tgt, idx, src, axis=0):
    return tgt.at[idx].add(src)

def _segment_sum(src, seg, n):
    return jax.ops.segment_sum(src, seg, n)
kernel_name = 'mk_gnn_resnorm_d4_gnn_r8_070122'

def setup_inputs(seed: int=0):
    np.random.seed(seed)
    _w = jnp.asarray

    def _rec_inputs():
        import jax
        import jax.numpy as jnp
        _gk = jax.random.key(seed)
        x = -0.0003713 + 1 * jax.random.normal(jax.random.fold_in(_gk, 1), (12500, 128), jnp.float32)
        _s = jax.random.randint(jax.random.fold_in(_gk, 2), (100000,), 0, 12500, jnp.int32)
        _d = jax.random.randint(jax.random.fold_in(_gk, 3), (100000,), 0, 12500, jnp.int32)
        _loop = jnp.arange(12500, dtype=jnp.int32)
        src = jnp.concatenate([_s, _d, _loop])
        dst = jnp.concatenate([_d, _s, _loop])
        _o = jnp.argsort(dst, stable=True)
        src = src[_o]
        dst = dst[_o]
        edge_attr_16 = 0.000216709 + 1.00012 * jax.random.normal(jax.random.fold_in(_gk, 12), (212500, 16), jnp.float32)
        edge_weight = jax.random.uniform(jax.random.fold_in(_gk, 14), (212500,), jnp.float32, 0.0, 1)
        node_vec = jax.random.uniform(jax.random.fold_in(_gk, 15), (12500,), jnp.float32, 0.0, 0.999993)
        return (x, src, dst, edge_attr_16, edge_weight, node_vec)
    x, src, dst, edge_attr_16, edge_weight, node_vec = _rec_inputs()

    def _L0_gnn_setup():
        import jax, jax.numpy as jnp
        import numpy as np
        N = 12500
        E = 200000
        D_IN = 128
        D_HID = 128
        D_OUT = 128
        BN_EPS = 1e-05
        LEAKY_SLOPE = 0.01

        def _graph_conv(h, s, d, W, b, norm_src, norm_dst):
            h = h * norm_src
            m = jax.ops.segment_sum(h[s], d, num_segments=N)
            m = m * norm_dst
            return m @ W + b
        key = jax.random.key(seed)
        ks = jax.random.split(key, 8)
        x = jax.random.normal(ks[0], (N, D_IN), dtype=jnp.float32)
        src = jax.random.randint(ks[1], (E,), 0, N, dtype=jnp.int32)
        dst = jax.random.randint(ks[2], (E,), 0, N, dtype=jnp.int32)
        W1 = jax.random.normal(ks[3], (D_IN, D_HID), dtype=jnp.float32) * (1.0 / np.sqrt(D_IN))
        b1 = jnp.zeros((D_HID,), jnp.float32)
        W2 = jax.random.normal(ks[4], (D_HID, D_OUT), dtype=jnp.float32) * (1.0 / np.sqrt(D_HID))
        b2 = jnp.zeros((D_OUT,), jnp.float32)
        gamma = jnp.ones((D_HID,), jnp.float32)
        beta = jnp.zeros((D_HID,), jnp.float32)
        run_mean = jax.random.normal(ks[5], (D_HID,), jnp.float32) * 0.1
        run_var = jax.random.uniform(ks[6], (D_HID,), jnp.float32, 0.5, 1.5)
        return {'x': x, 'src': src, 'dst': dst, 'W1': W1, 'b1': b1, 'W2': W2, 'b2': b2, 'gamma': gamma, 'beta': beta, 'run_mean': run_mean, 'run_var': run_var}
    _L0_gnn_all = _L0_gnn_setup()
    _L0_gnn_in = {k: v for k, v in _L0_gnn_all.items() if k in ('W1', 'b1', 'W2', 'b2', 'gamma', 'beta', 'run_mean', 'run_var')}
    del _L0_gnn_all

    def _L1_gnn_setup():
        import jax, jax.numpy as jnp
        import numpy as np
        N_NODES = 12500
        N_EDGES = 200000
        D_IN = 128
        D_OUT = 128
        key = jax.random.key(seed)
        k1, k2, k3, k4, k5, k6 = jax.random.split(key, 6)
        x = jax.random.normal(k1, (N_NODES, D_IN), dtype=jnp.float32)
        W = jax.random.normal(k2, (D_OUT, D_IN), dtype=jnp.float32) * (1.0 / np.sqrt(D_IN))
        b = jax.random.normal(k3, (D_OUT,), dtype=jnp.float32) * 0.01
        edge_weight = jax.random.uniform(k4, (N_EDGES,), dtype=jnp.float32)
        edge_src = jax.random.randint(k5, (N_EDGES,), 0, N_NODES, dtype=jnp.int32)
        edge_dst = jax.random.randint(k6, (N_EDGES,), 0, N_NODES, dtype=jnp.int32)
        return {'x': x, 'W': W, 'b': b, 'edge_weight': edge_weight, 'edge_src': edge_src, 'edge_dst': edge_dst}
    _L1_gnn_all = _L1_gnn_setup()
    _L1_gnn_in = {k: v for k, v in _L1_gnn_all.items() if k in ('W', 'b')}
    del _L1_gnn_all

    def _L2_gnn_setup():
        import jax, jax.numpy as jnp
        import numpy as np
        N_NODES = 5000
        N_EDGES = 80000
        D_IN = 128
        UNITS = 128
        EPS_NORM = 1e-08
        EPS_ATT = 1e-08
        key = jax.random.key(seed)
        k1, k2, k3 = jax.random.split(key, 3)
        node_states = jax.random.normal(k1, (N_NODES, D_IN), dtype=jnp.float32)
        edges = jax.random.randint(k2, (N_EDGES, 2), 0, N_NODES, dtype=jnp.int64)
        kernel = jax.random.normal(k3, (D_IN, UNITS), dtype=jnp.float32) * (1.0 / np.sqrt(D_IN))
        return {'node_states': node_states, 'edges': edges, 'kernel': kernel}
    _L2_gnn_all = _L2_gnn_setup()
    _L2_gnn_in = {k: v for k, v in _L2_gnn_all.items() if k in ('kernel',)}
    del _L2_gnn_all

    def _L3_gnn_setup():
        import jax, jax.numpy as jnp
        import numpy as np
        N_NODES = 12500
        N_EDGES = 200000
        IN_DIM = 128
        HID = 256
        HEADS = 4
        DH = HID // HEADS
        OUT_DIM = 128
        key = jax.random.key(seed)
        ks = jax.random.split(key, 16)
        s = 0.02
        return {'src': jax.random.randint(ks[0], (N_EDGES,), 0, N_NODES), 'dst': jax.random.randint(ks[1], (N_EDGES,), 0, N_NODES), 'node_feats': jax.random.normal(ks[2], (N_NODES, IN_DIM), jnp.float32), 'edge_feats': jax.random.normal(ks[3], (N_EDGES, 16), jnp.float32), 'timestamps': jax.random.uniform(ks[4], (N_NODES,), jnp.float32), 'W_t': jax.random.normal(ks[5], (HID, 1), jnp.float32) * s, 'b_t': jnp.zeros((HID,), jnp.float32), 'W_fc': jax.random.normal(ks[6], (HID, IN_DIM), jnp.float32) * s, 'attn_l': jax.random.normal(ks[7], (HEADS, DH), jnp.float32) * s, 'attn_r': jax.random.normal(ks[8], (HEADS, DH), jnp.float32) * s, 'bias_gat': jnp.zeros((HID,), jnp.float32), 'W_ih': jax.random.normal(ks[9], (3 * HID, HID), jnp.float32) * s, 'W_hh': jax.random.normal(ks[10], (3 * HID, HID), jnp.float32) * s, 'b_ih': jnp.zeros((3 * HID,), jnp.float32), 'b_hh': jnp.zeros((3 * HID,), jnp.float32), 'W_out': jax.random.normal(ks[11], (OUT_DIM, HID), jnp.float32) * s, 'b_out': jnp.zeros((OUT_DIM,), jnp.float32)}
    _L3_gnn_all = _L3_gnn_setup()
    _L3_gnn_in = {k: v for k, v in _L3_gnn_all.items() if k in ('W_t', 'b_t', 'W_fc', 'attn_l', 'attn_r', 'bias_gat', 'W_ih', 'W_hh', 'b_ih', 'b_hh', 'W_out', 'b_out')}
    del _L3_gnn_all
    return {'x': x, 'src': src, 'dst': dst, 'edge_attr_16': edge_attr_16, 'edge_weight': edge_weight, 'node_vec': node_vec, 'L0_gnn_W1': _L0_gnn_in['W1'], 'L0_gnn_b1': _L0_gnn_in['b1'], 'L0_gnn_W2': _L0_gnn_in['W2'], 'L0_gnn_b2': _L0_gnn_in['b2'], 'L0_gnn_gamma': _L0_gnn_in['gamma'], 'L0_gnn_beta': _L0_gnn_in['beta'], 'L0_gnn_run_mean': _L0_gnn_in['run_mean'], 'L0_gnn_run_var': _L0_gnn_in['run_var'], 'L1_gnn_W': _L1_gnn_in['W'], 'L1_gnn_b': _L1_gnn_in['b'], 'L2_gnn_kernel': _L2_gnn_in['kernel'], 'L3_gnn_W_t': _L3_gnn_in['W_t'], 'L3_gnn_b_t': _L3_gnn_in['b_t'], 'L3_gnn_W_fc': _L3_gnn_in['W_fc'], 'L3_gnn_attn_l': _L3_gnn_in['attn_l'], 'L3_gnn_attn_r': _L3_gnn_in['attn_r'], 'L3_gnn_bias_gat': _L3_gnn_in['bias_gat'], 'L3_gnn_W_ih': _L3_gnn_in['W_ih'], 'L3_gnn_W_hh': _L3_gnn_in['W_hh'], 'L3_gnn_b_ih': _L3_gnn_in['b_ih'], 'L3_gnn_b_hh': _L3_gnn_in['b_hh'], 'L3_gnn_W_out': _L3_gnn_in['W_out'], 'L3_gnn_b_out': _L3_gnn_in['b_out']}

def reference(x, src, dst, edge_attr_16, edge_weight, node_vec, L0_gnn_W1, L0_gnn_b1, L0_gnn_W2, L0_gnn_b2, L0_gnn_gamma, L0_gnn_beta, L0_gnn_run_mean, L0_gnn_run_var, L1_gnn_W, L1_gnn_b, L2_gnn_kernel, L3_gnn_W_t, L3_gnn_b_t, L3_gnn_W_fc, L3_gnn_attn_l, L3_gnn_attn_r, L3_gnn_bias_gat, L3_gnn_W_ih, L3_gnn_W_hh, L3_gnn_b_ih, L3_gnn_b_hh, L3_gnn_W_out, L3_gnn_b_out):
    import jax
    import jax.numpy as jnp

    def _L0_gnn_ref(x, src, dst, W1, b1, W2, b2, gamma, beta, run_mean, run_var):
        import jax, jax.numpy as jnp
        import numpy as np
        N = 12500
        E = 200000
        D_IN = 128
        D_HID = 128
        D_OUT = 128
        BN_EPS = 1e-05
        LEAKY_SLOPE = 0.01

        def _graph_conv(h, s, d, W, b, norm_src, norm_dst):
            h = h * norm_src
            m = jax.ops.segment_sum(h[s], d, num_segments=N)
            m = m * norm_dst
            return m @ W + b
        loop = jnp.arange(N, dtype=src.dtype)
        s = jnp.concatenate([src, loop])
        d = jnp.concatenate([dst, loop])
        ones = jnp.ones(s.shape[0], jnp.float32)
        out_deg = jnp.maximum(jax.ops.segment_sum(ones, s, num_segments=N), 1.0)
        in_deg = jnp.maximum(jax.ops.segment_sum(ones, d, num_segments=N), 1.0)
        norm_src = (out_deg ** (-0.5))[:, None]
        norm_dst = (in_deg ** (-0.5))[:, None]
        h = _graph_conv(x, s, d, W1, b1, norm_src, norm_dst)
        h = (h - run_mean) * jax.lax.rsqrt(run_var + BN_EPS) * gamma + beta
        h = jnp.where(h > 0, h, LEAKY_SLOPE * h)
        h = _graph_conv(h, s, d, W2, b2, norm_src, norm_dst)
        return h

    def _L1_gnn_ref(x, W, b, edge_weight, edge_src, edge_dst):
        import jax, jax.numpy as jnp
        import numpy as np
        N_NODES = 12500
        N_EDGES = 200000
        D_IN = 128
        D_OUT = 128
        h = jnp.einsum('nd,od->no', x, W) + b
        msgs = edge_weight[:, None] * h[edge_src]
        agg = jax.ops.segment_sum(msgs, edge_dst, num_segments=N_NODES)
        return jax.nn.relu(agg)

    def _L2_gnn_ref(node_states, edges, kernel):
        import jax, jax.numpy as jnp
        import numpy as np
        N_NODES = 5000
        N_EDGES = 80000
        D_IN = 128
        UNITS = 128
        EPS_NORM = 1e-08
        EPS_ATT = 1e-08
        num_nodes = node_states.shape[0]
        tgt = edges[:, 0]
        src = edges[:, 1]
        h = node_states @ kernel
        h_tgt = h[tgt]
        h_src = h[src]

        def l2norm(x):
            n = jnp.sqrt(jnp.maximum(jnp.sum(x * x, axis=-1, keepdims=True), EPS_NORM * EPS_NORM))
            return x / n
        cos = jnp.sum(l2norm(h_tgt) * l2norm(h_src), axis=-1)
        seg_max = jax.ops.segment_max(cos, tgt, num_segments=num_nodes)
        exp_sim = jnp.exp(cos - seg_max[tgt])
        att_sum = jax.ops.segment_sum(exp_sim, tgt, num_segments=num_nodes)
        attn = exp_sim / (att_sum[tgt] + EPS_ATT)
        out = jax.ops.segment_sum(h_src * attn[:, None], tgt, num_segments=num_nodes)
        return out

    def _L3_gnn_ref(src, dst, node_feats, edge_feats, timestamps, W_t, b_t, W_fc, attn_l, attn_r, bias_gat, W_ih, W_hh, b_ih, b_hh, W_out, b_out):
        import jax, jax.numpy as jnp
        import numpy as np
        N_NODES = 12500
        N_EDGES = 200000
        IN_DIM = 128
        HID = 256
        HEADS = 4
        DH = HID // HEADS
        OUT_DIM = 128
        t_emb = timestamps[:, None] * W_t[:, 0][None, :] + b_t
        feat = (node_feats @ W_fc.T).reshape(-1, HEADS, DH)
        el = jnp.einsum('nhd,hd->nh', feat, attn_l)
        er = jnp.einsum('nhd,hd->nh', feat, attn_r)
        e = jax.nn.leaky_relu(el[src] + er[dst], negative_slope=0.2)
        e_max = jax.ops.segment_max(e, dst, num_segments=N_NODES)
        ee = jnp.exp(e - e_max[dst])
        denom = jax.ops.segment_sum(ee, dst, num_segments=N_NODES)
        alpha = ee / denom[dst]
        msg = alpha[:, :, None] * feat[src]
        rst = jax.ops.segment_sum(msg, dst, num_segments=N_NODES)
        rst = rst + bias_gat.reshape(HEADS, DH)
        h = rst.reshape(-1, HID)
        hx = jnp.zeros_like(h)
        gi = h @ W_ih.T + b_ih
        gh = hx @ W_hh.T + b_hh
        i_r, i_z, i_n = jnp.split(gi, 3, axis=-1)
        h_r, h_z, h_n = jnp.split(gh, 3, axis=-1)
        r = jax.nn.sigmoid(i_r + h_r)
        z = jax.nn.sigmoid(i_z + h_z)
        n = jnp.tanh(i_n + r * h_n)
        h_mem = (1.0 - z) * n + z * hx
        return h_mem @ W_out.T + b_out
    edge_index_t = jnp.stack([src, dst], axis=1)
    x = _layernorm(x + _L0_gnn_ref(x, src, dst, L0_gnn_W1, L0_gnn_b1, L0_gnn_W2, L0_gnn_b2, L0_gnn_gamma, L0_gnn_beta, L0_gnn_run_mean, L0_gnn_run_var), axis=-1)
    x = _layernorm(x + _L1_gnn_ref(x, L1_gnn_W, L1_gnn_b, edge_weight, src, dst), axis=-1)
    x = _layernorm(x + _L2_gnn_ref(x, edge_index_t, L2_gnn_kernel), axis=-1)
    x = _layernorm(x + _L3_gnn_ref(src, dst, x, edge_attr_16, node_vec, L3_gnn_W_t, L3_gnn_b_t, L3_gnn_W_fc, L3_gnn_attn_l, L3_gnn_attn_r, L3_gnn_bias_gat, L3_gnn_W_ih, L3_gnn_W_hh, L3_gnn_b_ih, L3_gnn_b_hh, L3_gnn_W_out, L3_gnn_b_out), axis=-1)
    return x

_drawn_inputs = setup_inputs


def setup_inputs(seed=0):
    import zlib

    import numpy as np

    out = dict(_drawn_inputs(seed))
    spreads = {'L0_gnn_b1': (0.0, 0.1),
     'L0_gnn_b2': (0.0, 0.1),
     'L0_gnn_gamma': (1.0, 0.2),
     'L0_gnn_beta': (0.0, 0.1),
     'L3_gnn_b_t': (0.0, 0.1),
     'L3_gnn_bias_gat': (0.0, 0.8),
     'L3_gnn_b_ih': (0.0, 0.567),
     'L3_gnn_b_hh': (0.0, 0.8),
     'L3_gnn_b_out': (0.0, 0.1)}
    factors = {'L3_gnn_W_fc': 8.0,
     'L3_gnn_attn_l': 8.0,
     'L3_gnn_attn_r': 8.0,
     'L3_gnn_W_ih': 7.383,
     'L3_gnn_W_out': 3.498}
    for name, (base, spread) in spreads.items():
        noise = np.random.default_rng([zlib.crc32(name.encode()), seed]).standard_normal(out[name].shape)
        drawn = base * np.exp(spread * noise) if base else spread * noise
        out[name] = jnp.asarray(drawn.astype(out[name].dtype))
    for name, factor in factors.items():
        out[name] = (out[name] * factor).astype(out[name].dtype)
    return out
```

```python
from contextlib import ExitStack

import concourse.bass as bass
from concourse import mybir

ALU = mybir.AluOpType
ACT = mybir.ActivationFunctionType
AX = mybir.AxisListType
F32 = mybir.dt.float32
BF16 = mybir.dt.bfloat16
I32 = mybir.dt.int32

P = 128
N = 12500
E = 212500
D = 128
HEADS = 4
HID = 256
DH = HID // HEADS
GATES = 3 * HID
GC = GATES // P
KC = HID // P

NB = -(-N // P)
LAST = N - (NB - 1) * P
NR = NB * P
NK = NB + 1

EC = -(-E // P)
EL = E - (P - 1) * EC
SU = 11
ST = EC // SU
SG = ((0, 6), (6, 5))
NO_EDGE = NB * P
FAR = float(1 << 26)
NO_LANE = 999.0

U = 16
HU = U // 2
KT = -(-((E + NB * (P - 1)) // P) // U) * U
T = KT // U
RW = 4

NT = NB // 2
W_COS = D + 2
W_GAT = HID + HEADS
EPS_LN = 1e-5
EPS_BN = 1e-5
EPS_ATT = 1e-8
assert ST * SU == EC and NT * 2 == NB


class Signal:

    def __init__(self, handle):
        self.handle = handle
        self.start = 0

    def at(self, n):
        return n + self.start

    def phase_over(self, n):
        self.start += n


class Chain:

    def __init__(self, eng, steps, per_turn):
        self.eng, self.steps, self.per_turn = eng, steps, per_turn

    def turn(self, t):
        self.t, self.n = t, 0

    def link(self, ins):
        self.n += 1
        assert self.n <= self.per_turn
        ins.then_inc(self.steps.handle, 1)
        self.eng.wait_ge(self.steps.handle, self.steps.at(self.t * self.per_turn + self.n))


def turns(eng, count, body):
    body(0, True)
    with eng.Fori(1, count) as t:
        body(t, False)


def program(nc, x, src, dst, edge_weight, W1, b1, W2, b2, gamma, beta, run_mean, run_var, W_msg, b_msg, W_cos,
            W_fc, attn_l, attn_r, bias_gat, W_ih, b_ih, b_hh, W_out, b_out, out):
    ctx = ExitStack()
    with ctx:
        def sb(name, shape, dt=F32, scope=ctx):
            return scope.enter_context(nc.sbuf_tensor(name, shape, dt))

        def signal(name):
            return Signal(ctx.enter_context(nc.semaphore(name)))

        bank = [ctx.enter_context(nc.psum_tensor(f"bank{i}", [P, 512], F32)) for i in range(8)]

        waits_passed = signal("waits_passed")

        rows_conv = [nc.dram_tensor(f"rows_conv{i}", [NR, D], F32).ap() for i in range(2)]
        rows_msg = nc.dram_tensor("rows_msg", [NR, D], F32).ap()
        rows_cos = nc.dram_tensor("rows_cos", [NR, W_COS], F32).ap()
        rows_gat = nc.dram_tensor("rows_gat", [NR, W_GAT], F32).ap()
        records = {k: nc.dram_tensor(f"records_{k}", [P * KT, RW], I32).ap() for k in ("dst", "src")}
        tile_block = {k: nc.dram_tensor(f"tile_block_{k}", [1, KT], I32).ap() for k in ("dst", "src")}

        ident = sb("ident", [P, P])
        iota = sb("iota", [P, P])
        ones = sb("ones", [P, P])
        w1 = sb("w1", [P, D])
        w2 = sb("w2", [P, D])
        w_msgT = sb("w_msgT", [P, D])
        w_cos = sb("w_cos", [P, D])
        w_gat = sb("w_gat", [P, HID + 2 * HEADS])
        w_ihT = sb("w_ihT", [P, KC, GATES])
        w_outT = sb("w_outT", [P, KC, D])
        bn_scale = sb("bn_scale", [P, D])
        bn_shift = sb("bn_shift", [P, D])
        b2_row = sb("b2_row", [P, D])
        b_msg_row = sb("b_msg_row", [P, D])
        bias_gat_row = sb("bias_gat_row", [P, HID])
        b_out_row = sb("b_out_row", [P, D])
        b_gate = sb("b_gate", [P, GC])
        b_hid_n = sb("b_hid_n", [P, KC])
        norm = {k: sb(f"norm_{k}", [P, NB]) for k in ("dst", "src")}

        load_weights(nc, ctx, locals())
        sort_edges(nc, ctx, locals())
        layers(nc, ctx, locals())


def row_of(ap):
    return ap.rearrange("(a d) -> a d", a=1).broadcast_to([P, ap.shape[0]])


def load_weights(nc, ctx, v):
    (bank, ident, iota, ones, w1, w2, w_msgT, w_cos, w_gat, w_ihT, w_outT, bn_scale, bn_shift, b2_row, b_msg_row,
     bias_gat_row, b_out_row, b_gate, b_hid_n) = (v[k] for k in (
         "bank", "ident", "iota", "ones", "w1", "w2", "w_msgT", "w_cos", "w_gat", "w_ihT", "w_outT", "bn_scale",
         "bn_shift", "b2_row", "b_msg_row", "bias_gat_row", "b_out_row", "b_gate", "b_hid_n"))
    signal = v["signal"]
    with ExitStack() as scope:
        def sb(name, shape, dt=F32):
            return v["sb"](name, shape, dt, scope)

        iota_i = sb("iota_i", [P, P], I32)
        msg_in = sb("msg_in", [P, D])
        fc_in = sb("fc_in", [P, KC, D])
        ih_in = sb("ih_in", [P, GC, HID])
        out_in = sb("out_in", [P, HID])
        attn = sb("attn", [P, KC, 2 * HEADS])
        rows = {k: sb(f"row_{k}", [P, D]) for k in ("b1", "gamma", "beta", "mean", "var")}
        b_hh_col = sb("b_hh_col", [P, GC])

        weights_in = signal("weights_in")
        attn_zero = signal("attn_zero")
        attn_in = signal("attn_in")
        consts_set = signal("consts_set")
        iota_set = signal("iota_set")
        turned = signal("turned")
        kept = signal("kept")
        var_eps = signal("var_eps")
        var_root = signal("var_root")
        chain = signal("chain_weights")
        loads = [
            (w1[:, :], v["W1"]), (w2[:, :], v["W2"]), (msg_in[:, :], v["W_msg"]), (w_cos[:, :], v["W_cos"]),
            (fc_in[:, :, :], v["W_fc"].rearrange("(c p) d -> p c d", p=P)),
            (ih_in[:, :, :], v["W_ih"].rearrange("(c p) k -> p c k", p=P)), (out_in[:, :], v["W_out"]),
            (rows["b1"][:, :], row_of(v["b1"])), (rows["gamma"][:, :], row_of(v["gamma"])),
            (rows["beta"][:, :], row_of(v["beta"])), (rows["mean"][:, :], row_of(v["run_mean"])),
            (rows["var"][:, :], row_of(v["run_var"])), (b2_row[:, :], row_of(v["b2"])),
            (b_msg_row[:, :], row_of(v["b_msg"])), (bias_gat_row[:, :], row_of(v["bias_gat"])),
            (b_out_row[:, :], row_of(v["b_out"])),
            (b_gate[:, :], v["b_ih"].rearrange("(c p) -> p c", p=P)),
            (b_hh_col[:, :], v["b_hh"].rearrange("(c p) -> p c", p=P)),
        ]
        turns_of = [(msg_in[:, :], w_msgT[:, :])]
        turns_of += [(fc_in[:, c, :], w_gat[:, c * P:(c + 1) * P]) for c in range(KC)]
        turns_of += [(ih_in[:, g, c * P:(c + 1) * P], w_ihT[:, c, g * P:(g + 1) * P]) for g in range(GC) for c in range(KC)]
        turns_of += [(out_in[:, c * P:(c + 1) * P], w_outT[:, c, :]) for c in range(KC)]

        with nc.Block() as block:
            @block.sync
            def _(sp):
                with nc.allow_non_contiguous_dma(reason="biases, a few hundred words, once"):
                    for to, of in loads:
                        sp.dma_start(to, of).then_inc(weights_in.handle, 16)
                    sp.wait_ge(attn_zero.handle, attn_zero.at(1))
                    for n, a in enumerate((v["attn_l"], v["attn_r"])):
                        for h in range(HEADS):
                            lanes = slice(h % 2 * DH, h % 2 * DH + DH)
                            column = n * HEADS + h
                            sp.dma_start(attn[lanes, h // 2, column:column + 1],
                                         a[h:h + 1, :].rearrange("a d -> d a")).then_inc(attn_in.handle, 16)

            @block.gpsimd
            def _(pool):
                pool.iota(iota_i[:, :], pattern=[[1, P]], base=0, channel_multiplier=0).then_inc(iota_set.handle, 1)
                pool.memset(ident[:, :], 0.0).then_inc(consts_set.handle, 1)
                pool.wait_ge(consts_set.handle, consts_set.at(1))
                pool.affine_select(out=ident[:, :], in_=ident[:, :], compare_op=ALU.not_equal, fill=1.0, base=0,
                                   pattern=[[-1, P]], channel_multiplier=1).then_inc(consts_set.handle, 1)

            @block.tensor
            def _(pe):
                pe.wait_ge(consts_set.handle, consts_set.at(2))
                pe.wait_ge(weights_in.handle, weights_in.at(16 * len(loads)))
                for i, (of, _) in enumerate(turns_of):
                    if i >= 4:
                        pe.wait_ge(kept.handle, kept.at(i - 3))
                    pe.transpose(bank[i % 4][:, 0:P], of, ident[:, :]).then_inc(turned.handle, 1)
                pe.wait_ge(attn_in.handle, attn_in.at(16 * 2 * HEADS))
                for c in range(KC):
                    ins = pe.matmul(bank[4][:, 0:2 * HEADS], fc_in[:, c, :], attn[:, c, :], start=(c == 0),
                                    stop=(c == KC - 1))
                ins.then_inc(turned.handle, 1)

            @block.vector
            def _(dve):
                links = Chain(dve, chain, 8)
                links.turn(0)
                dve.memset(attn[:, :, :], 0.0).then_inc(attn_zero.handle, 1)
                dve.memset(ones[:, :], 1.0)
                dve.wait_ge(iota_set.handle, iota_set.at(1))
                dve.tensor_copy(iota[:, :], iota_i[:, :])
                dve.wait_ge(weights_in.handle, weights_in.at(16 * len(loads)))
                dve.tensor_scalar(rows["var"][:, :], rows["var"][:, :], EPS_BN, None, ALU.add).then_inc(var_eps.handle, 1)
                dve.wait_ge(var_root.handle, var_root.at(1))
                links.link(dve.reciprocal(rows["var"][:, :], rows["var"][:, :]))
                links.link(dve.tensor_tensor(bn_scale[:, :], rows["var"][:, :], rows["gamma"][:, :], ALU.mult))
                links.link(dve.tensor_tensor(rows["b1"][:, :], rows["b1"][:, :], rows["mean"][:, :], ALU.subtract))
                links.link(dve.tensor_tensor(rows["b1"][:, :], rows["b1"][:, :], bn_scale[:, :], ALU.mult))
                links.link(dve.tensor_tensor(bn_shift[:, :], rows["b1"][:, :], rows["beta"][:, :], ALU.add))
                links.link(dve.tensor_copy(b_hid_n[:, :], b_hh_col[:, 2 * KC:3 * KC]))
                links.link(dve.tensor_tensor(b_gate[:, 0:2 * KC], b_gate[:, 0:2 * KC], b_hh_col[:, 0:2 * KC], ALU.add))
                links.link(dve.tensor_scalar(b_gate[:, KC:2 * KC], b_gate[:, KC:2 * KC], -1.0, None, ALU.mult))
                for i, (_, to) in enumerate(turns_of):
                    dve.wait_ge(turned.handle, turned.at(i + 1))
                    dve.tensor_copy(to, bank[i % 4][:, 0:P]).then_inc(kept.handle, 1)
                dve.wait_ge(turned.handle, turned.at(len(turns_of) + 1))
                dve.tensor_copy(w_gat[:, HID:], bank[4][:, 0:2 * HEADS]).then_inc(kept.handle, 1)
                dve.wait_ge(kept.handle, kept.at(len(turns_of) + 1))

            @block.scalar
            def _(act):
                act.wait_ge(var_eps.handle, var_eps.at(1))
                act.activation(rows["var"][:, :], rows["var"][:, :], ACT.Sqrt).then_inc(var_root.handle, 1)


def sort_edges(nc, ctx, v):
    bank, ident, iota, ones, norm, records, tile_block, waits_passed = (
        v[k] for k in ("bank", "ident", "iota", "ones", "norm", "records", "tile_block", "waits_passed"))
    signal = v["signal"]
    keys = ("dst", "src")
    other = {"dst": "src", "src": "dst"}
    with ExitStack() as scope:
        def sb(name, shape, dt=F32):
            return v["sb"](name, shape, dt, scope)

        ends = {k: sb(f"ends_{k}", [P, EC], I32) for k in keys}
        weight = sb("weight", [P, EC])
        hi = {k: sb(f"hi_{k}", [P, EC]) for k in keys}
        lo = {k: sb(f"lo_{k}", [P, EC]) for k in keys}
        bits = sb("bits", [P, EC], I32)
        hot_hi = {k: [sb(f"hot_hi_{k}{g}", [P, n, 100], BF16) for g, (_, n) in enumerate(SG)] for k in keys}
        hot_lo = {k: [sb(f"hot_lo_{k}{g}", [P, n, P], BF16) for g, (_, n) in enumerate(SG)] for k in keys}
        before = sb("before", [P, P])
        before_h = sb("before_h", [P, P], BF16)
        rest_h = sb("rest_h", [P, P], BF16)
        lane_i = sb("lane_i", [P, 1], I32)
        far = sb("far", [P, 1])
        tile_i = sb("tile_i", [P, KT], I32)
        tile_f = sb("tile_f", [P, KT])
        begun = sb("begun", [P, KT])
        block_row = {k: sb(f"block_row_{k}", [1, KT], I32) for k in keys}
        count = {k: sb(f"count_{k}", [P, P]) for k in keys}
        total = {k: sb(f"total_{k}", [P, 1]) for k in keys}
        total_i = {k: sb(f"total_i_{k}", [P, 1], I32) for k in keys}
        n_tiles = {k: sb(f"n_tiles_{k}", [P, 1]) for k in keys}
        first_tile = {k: sb(f"first_tile_{k}", [P, 1]) for k in keys}
        first_place = {k: sb(f"first_place_{k}", [P, 1]) for k in keys}
        place_diag = {k: sb(f"place_diag_{k}", [P, NK]) for k in keys}
        no_records = sb("no_records", [P, KT, RW], I32)

        zeroed = signal("zeroed")
        edges_in = signal("edges_in")
        index_set = signal("index_set")
        blank_set = signal("blank_set")
        blank_out = signal("blank_out")
        counted = signal("counted")
        hot_set = signal("hot_set")
        hot_used = signal("hot_used")
        chain = signal("chain_sort")
        turned = signal("sort_turned")
        begun_set = signal("begun_set")
        block_sum = signal("block_sum")
        block_kept = signal("block_kept")
        degree_in = signal("degree_in")
        degree_root = signal("degree_root")
        blocks_out = signal("blocks_out")
        consts = signal("sort_consts")

        CH = KT // 4
        with nc.Block() as block:
            @block.sync
            def _(sp):
                sp.wait_ge(zeroed.handle, zeroed.at(1))
                for to, of in ((ends["dst"], v["dst"]), (ends["src"], v["src"]), (weight, v["edge_weight"])):
                    sp.dma_start(to[0:P - 1, :], of[0:(P - 1) * EC].rearrange("(p c) -> p c", c=EC)).then_inc(edges_in.handle, 16)
                    sp.dma_start(to[P - 1:P, 0:EL], of[(P - 1) * EC:E].rearrange("(p c) -> p c", p=1)).then_inc(edges_in.handle, 16)
                sp.wait_ge(blank_set.handle, blank_set.at(1))
                for k in keys:
                    sp.dma_start(records[k].rearrange("(p c) w -> p c w", c=KT), no_records[:, :, :]).then_inc(blank_out.handle, 16)
                sp.wait_ge(blank_out.handle, blank_out.at(32))

            @block.gpsimd
            def _(pool):
                pool.memset(before[:, :], 0.0).then_inc(consts.handle, 1)
                pool.wait_ge(consts.handle, consts.at(1))
                pool.affine_select(out=before[:, :], in_=before[:, :], compare_op=ALU.is_ge, fill=1.0, base=0,
                                   pattern=[[-1, P]], channel_multiplier=1).then_inc(index_set.handle, 1)
                pool.iota(lane_i[:, :], pattern=[[0, 1]], base=0, channel_multiplier=1).then_inc(index_set.handle, 1)
                pool.iota(tile_i[:, :], pattern=[[1, KT]], base=0, channel_multiplier=0).then_inc(index_set.handle, 1)

            @block.vector
            def _(dve):
                for k in keys:
                    dve.memset(ends[k][:, :], NO_EDGE)
                dve.memset(weight[:, :], 0.0).then_inc(zeroed.handle, 1)
                links = Chain(dve, chain, 3 + 8)
                links.turn(0)
                links.link(dve.memset(no_records[:, :, :], 0))
                dve.memset(no_records[:, :, 1:2].bitcast(F32), NO_LANE).then_inc(blank_set.handle, 1)
                dve.wait_ge(index_set.handle, index_set.at(3))
                dve.tensor_copy(before_h[:, :], before[:, :])
                dve.tensor_scalar(rest_h[:, :], before[:, :], -1.0, 1.0, ALU.mult, ALU.add)
                dve.tensor_copy(tile_f[:, :], tile_i[:, :])
                links.link(dve.tensor_copy(far[:, :], lane_i[:, :]))
                links.link(dve.tensor_scalar(far[:, :], far[:, :], float(NB), FAR, ALU.is_ge, ALU.mult))
                dve.wait_ge(edges_in.handle, edges_in.at(96))
                for k in keys:
                    links.link(dve.tensor_scalar(bits[:, :], ends[k][:, :], 7, None, ALU.logical_shift_right))
                    links.link(dve.tensor_copy(hi[k][:, :], bits[:, :]))
                    links.link(dve.tensor_scalar(bits[:, :], ends[k][:, :], 127, None, ALU.bitwise_and))
                    links.link(dve.tensor_copy(lo[k][:, :], bits[:, :]))

                def body(t, first):
                    for g, (c0, n) in enumerate(SG):
                        if not first:
                            dve.wait_ge(hot_used.handle, hot_used.at(t * 2 + g - 1))
                        cols = bass.ds(t * SU + c0, n)
                        for k in keys:
                            dve.tensor_tensor(hot_hi[k][g][:, :, :], hi[k][:, cols].unsqueeze(2).to_broadcast([P, n, 100]),
                                              iota[:, 0:100].unsqueeze(1).to_broadcast([P, n, 100]), ALU.is_equal)
                            ins = dve.tensor_tensor(hot_lo[k][g][:, :, :], lo[k][:, cols].unsqueeze(2).to_broadcast([P, n, P]),
                                                    iota[:, :].unsqueeze(1).to_broadcast([P, n, P]), ALU.is_equal)
                        ins.then_inc(hot_set.handle, 1)

                turns(dve, ST, body)

            @block.tensor
            def _(pe):
                def body(t, first):
                    for g, (_, n) in enumerate(SG):
                        pe.wait_ge(hot_set.handle, hot_set.at(t * 2 + g + 1))
                        for b, k in enumerate(keys):
                            for j in range(n):
                                ins = pe.matmul(bank[b][0:NK, 0:P], hot_hi[k][g][:, j, 0:NK], hot_lo[k][g][:, j, :],
                                                start=first and g == 0 and j == 0, stop=True, skip_group_check=True)
                        ins.then_inc(hot_used.handle, 1)

                turns(pe, ST, body)
        chain.phase_over(3 + 8)
        hot_set.phase_over(2 * ST)
        hot_used.phase_over(2 * ST)

        with nc.Block() as block:
            @block.vector
            def _(dve):
                links = Chain(dve, chain, 17)
                links.turn(0)
                for b, k in enumerate(keys):
                    links.link(dve.tensor_copy(count[k][0:NK, :], bank[b][0:NK, 0:P]))
                    links.link(dve.tensor_reduce(total[k][0:NK, :], count[k][0:NK, :], AX.X, ALU.add))
                    links.link(dve.tensor_scalar(total[k][0:NK, :], total[k][0:NK, :], float(P - 1), None, ALU.add))
                    links.link(dve.tensor_copy(total_i[k][0:NK, :], total[k][0:NK, :]))
                    links.link(dve.tensor_scalar(total_i[k][0:NK, :], total_i[k][0:NK, :], 7, None, ALU.logical_shift_right))
                    dve.tensor_copy(n_tiles[k][0:NK, :], total_i[k][0:NK, :]).then_inc(counted.handle, 1)
                for b, k in enumerate(keys):
                    dve.wait_ge(turned.handle, turned.at(b + 1))
                    links.link(dve.tensor_scalar(norm[k][:, :], bank[2][:, 0:NB], 1.0, 1.0, ALU.add, ALU.max))
                    dve.tensor_copy(first_tile[k][0:NK, :], bank[3][0:NK, 0:1]).then_inc(degree_in.handle, 1)
                    dve.wait_ge(degree_in.handle, degree_in.at(3 * b + 1))
                    links.link(dve.tensor_scalar(first_place[k][0:NK, :], first_tile[k][0:NK, :], float(P), None, ALU.mult))
                    dve.tensor_scalar(begun[0:NB, :], tile_f[0:NB, :], first_tile[k][0:NB, :], None, ALU.is_ge).then_inc(begun_set.handle, 1)
                    dve.tensor_tensor(first_place[k][0:NK, :], first_place[k][0:NK, :], far[0:NK, :], ALU.add).then_inc(degree_in.handle, 1)
                    dve.wait_ge(degree_in.handle, degree_in.at(3 * b + 2))
                    dve.tensor_scalar(place_diag[k][0:NK, :], ident[0:NK, 0:NK], first_place[k][0:NK, :], None, ALU.mult)
                    dve.wait_ge(block_sum.handle, block_sum.at(b + 1))
                    for q in range(4):
                        ins = dve.tensor_scalar(block_row[k][:, q * CH:(q + 1) * CH], bank[4 + q][0:1, 0:CH], -1.0, None, ALU.add)
                    ins.then_inc(block_kept.handle, 1)
                    dve.wait_ge(degree_root.handle, degree_root.at(b + 1))
                    dve.reciprocal(norm[k][:, :], norm[k][:, :]).then_inc(degree_in.handle, 1)
                dve.wait_ge(degree_in.handle, degree_in.at(6))

            @block.tensor
            def _(pe):
                for b, k in enumerate(keys):
                    pe.wait_ge(counted.handle, counted.at(b + 1))
                    if b:
                        pe.wait_ge(degree_in.handle, degree_in.at(3 * b - 2))
                    pe.transpose(bank[2][:, 0:NB], count[k][0:NB, :], ident[0:NB, 0:NB])
                    pe.matmul(bank[3][0:NK, 0:1], before[0:NK, 0:NK], n_tiles[k][0:NK, :], start=True, stop=True).then_inc(turned.handle, 1)
                    pe.wait_ge(begun_set.handle, begun_set.at(b + 1))
                    if b:
                        pe.wait_ge(block_kept.handle, block_kept.at(b))
                    for q in range(4):
                        ins = pe.matmul(bank[4 + q][0:1, 0:CH], ones[0:NB, 0:1], begun[0:NB, q * CH:(q + 1) * CH], start=True, stop=True)
                    ins.then_inc(block_sum.handle, 1)

            @block.scalar
            def _(act):
                for b, k in enumerate(keys):
                    act.wait_ge(degree_in.handle, degree_in.at(3 * b + 1))
                    act.activation(norm[k][:, :], norm[k][:, :], ACT.Sqrt).then_inc(degree_root.handle, 1)

            @block.sync
            def _(sp):
                for b, k in enumerate(keys):
                    sp.wait_ge(block_kept.handle, block_kept.at(b + 1))
                    sp.dma_start(tile_block[k], block_row[k][:, :]).then_inc(blocks_out.handle, 16)
                sp.wait_ge(blocks_out.handle, blocks_out.at(32))
        chain.phase_over(14)

        with ExitStack() as inner:
            place = [v["sb"](f"place{g}", [P, n], F32, inner) for g, (_, n) in enumerate(SG)]
            place_i = [v["sb"](f"place_i{g}", [P, n], I32, inner) for g, (_, n) in enumerate(SG)]
            tile_of = [v["sb"](f"tile_of{g}", [P, n], I32, inner) for g, (_, n) in enumerate(SG)]
            row_to = [v["sb"](f"row_to{g}", [P, n], I32, inner) for g, (_, n) in enumerate(SG)]
            record = [v["sb"](f"record{g}", [P, n, RW], I32, inner) for g, (_, n) in enumerate(SG)]
            ranked = v["sb"]("ranked", [P, NK], F32, inner)
            record_clear = signal("record_clear")
            prefix_set = signal("prefix_set")
            place_read = signal("place_read")
            rows_set = signal("rows_set")
            record_set = signal("record_set")
            scattered = [signal(f"scattered{g}") for g in range(2)]
            prefix = bank[0][:, 0:NK]

            for k in keys:
                with nc.Block() as block:
                    @block.tensor
                    def _(pe):
                        pe.matmul(prefix, ones[0:NK, :], place_diag[k][0:NK, :], start=True, stop=True, skip_group_check=True)

                        def body(t, first):
                            for g, (c0, n) in enumerate(SG):
                                pe.wait_ge(hot_set.handle, hot_set.at(t * 2 + g + 1))
                                for j in range(n):
                                    pe.matmul(prefix, before_h[:, :], hot_hi[k][g][:, j, 0:NK], start=False, stop=True,
                                              skip_group_check=True).then_inc(prefix_set.handle, 1)
                                    pe.wait_ge(place_read.handle, place_read.at(t * SU + c0 + j + 1))
                                    ins = pe.matmul(prefix, rest_h[:, :], hot_hi[k][g][:, j, 0:NK], start=False, stop=True,
                                                    skip_group_check=True)
                                ins.then_inc(hot_used.handle, 1)

                        turns(pe, ST, body)

                    @block.vector
                    def _(dve):
                        links = Chain(dve, chain, 4)

                        def body(t, first):
                            links.turn(t)
                            for g, (c0, n) in enumerate(SG):
                                if not first:
                                    dve.wait_ge(hot_used.handle, hot_used.at(t * 2 + g - 1))
                                dve.tensor_tensor(hot_hi[k][g][:, :, :],
                                                  hi[k][:, bass.ds(t * SU + c0, n)].unsqueeze(2).to_broadcast([P, n, 100]),
                                                  iota[:, 0:100].unsqueeze(1).to_broadcast([P, n, 100]),
                                                  ALU.is_equal).then_inc(hot_set.handle, 1)
                            for g, (c0, n) in enumerate(SG):
                                for j in range(n):
                                    dve.wait_ge(prefix_set.handle, prefix_set.at(t * SU + c0 + j + 1))
                                    dve.tensor_tensor_reduce(ranked[:, :], prefix, hot_hi[k][g][:, j, 0:NK], 1.0, 0.0, ALU.mult,
                                                             ALU.add, place[g][:, j:j + 1]).then_inc(place_read.handle, 1)
                                dve.wait_ge(place_read.handle, place_read.at(t * SU + c0 + n))
                                links.link(dve.tensor_copy(place_i[g][:, :], place[g][:, :]))
                                dve.tensor_scalar(tile_of[g][:, :], place_i[g][:, :], 7, None, ALU.logical_shift_right)
                                links.link(dve.tensor_scalar(place_i[g][:, :], place_i[g][:, :], 127, None, ALU.bitwise_and))
                                if not first:
                                    dve.wait_ge(scattered[g].handle, scattered[g].at(t * (16 * n)))
                                dve.scalar_tensor_tensor(out=row_to[g][:, :], in0=place_i[g][:, :], scalar=float(KT),
                                                         in1=tile_of[g][:, :], op0=ALU.mult, op1=ALU.add).then_inc(rows_set.handle, 1)

                        turns(dve, ST, body)

                    @block.scalar
                    def _(act):
                        act.wait_ge(record_clear.handle, record_clear.at(2))

                        def body(t, first):
                            for g, (c0, n) in enumerate(SG):
                                if not first:
                                    act.wait_ge(scattered[g].handle, scattered[g].at(t * (16 * n)))
                                cols = bass.ds(t * SU + c0, n)
                                act.copy(record[g][:, :, 0:1], ends[other[k]][:, cols].unsqueeze(2))
                                act.copy(record[g][:, :, 1:2].bitcast(F32), lo[k][:, cols].unsqueeze(2))
                                act.copy(record[g][:, :, 2:3].bitcast(F32), weight[:, cols].unsqueeze(2)).then_inc(record_set.handle, 1)

                        turns(act, ST, body)

                    @block.gpsimd
                    def _(pool):
                        if k == keys[0]:
                            for g in range(2):
                                pool.memset(record[g][:, :, :], 0).then_inc(record_clear.handle, 1)

                        def body(t, first):
                            for g, (_, n) in enumerate(SG):
                                pool.wait_ge(rows_set.handle, rows_set.at(t * 2 + g + 1))
                                pool.wait_ge(record_set.handle, record_set.at(t * 2 + g + 1))
                                pool.sem_inc(waits_passed.handle, 1)
                                for j in range(n):
                                    pool.indirect_dma_start(
                                        out=records[k], out_offset=bass.IndirectOffsetOnAxis(ap=row_to[g][:, j:j + 1], axis=0),
                                        in_=record[g][:, j, :], in_offset=None, bounds_check=P * KT - 1,
                                        oob_is_err=False).then_inc(scattered[g].handle, 16)

                        turns(pool, ST, body)
                        for g, (_, n) in enumerate(SG):
                            pool.wait_ge(scattered[g].handle, scattered[g].at(16 * n * ST))
                hot_set.phase_over(2 * ST)
                hot_used.phase_over(2 * ST)
                prefix_set.phase_over(EC)
                place_read.phase_over(EC)
                rows_set.phase_over(2 * ST)
                record_set.phase_over(2 * ST)
                chain.phase_over(4 * ST)
                for g, (_, n) in enumerate(SG):
                    scattered[g].phase_over(16 * n * ST)


def layers(nc, ctx, v):
    bank, ident, iota, norm, records, tile_block, waits_passed = (
        v[k] for k in ("bank", "ident", "iota", "norm", "records", "tile_block", "waits_passed"))
    sb, signal = v["sb"], v["signal"]
    x_in, out = v["x"], v["out"]
    FULL = (NB - 1) * P

    nodes = sb("nodes", [P, NB, D])
    sums = sb("sums", [P, NB * W_GAT])
    sums_conv = sums[:, 0:NB * D].rearrange("p (b w) -> p b w", w=D)
    sums_msg = sums_conv
    sums_cos = sums[:, 0:NB * W_COS].rearrange("p (b w) -> p b w", w=W_COS)
    sums_gat = sums[:, :].rearrange("p (b w) -> p b w", w=W_GAT)
    unit = sums[:, NB * W_COS:NB * (W_COS + D)].rearrange("p (b w) -> p b w", w=D)
    target = sb("target", [P, NB, 2 * HEADS])
    stats = sb("stats", [P, NB, 6])
    mean = sb("mean", [P, NB])
    rstd = sb("rstd", [P, NB])
    spread = sb("spread", [P, NB])
    block_row = sb("block_row", [1, KT], I32)

    record_in = [signal(f"record_in{h}") for h in range(2)]
    gathered = [signal(f"gathered{s}") for s in range(U)]
    half_used = signal("half_used")
    hot_set = signal("walk_hot_set")
    product = signal("product")
    added = signal("added")
    hot_turned = signal("hot_turned")
    hot_kept = signal("hot_kept")
    target_set = signal("target_set")
    logit_set = signal("logit_set")
    exp_set = signal("exp_set")
    weighted = signal("weighted")
    blocks_in = signal("blocks_in")
    chain = signal("chain_layers")
    block_staged = signal("block_staged")
    block_product = signal("block_product")
    block_rows = signal("block_rows")
    block_turned = signal("block_turned")
    turned_kept = signal("turned_kept")
    stored = [signal(f"stored{j}") for j in range(2)]
    root_in = signal("root_in")
    root_set = signal("root_set")
    x_loaded = signal("x_loaded")

    def walk(name, key, rows, width, kind):
        n_banks = 4
        with ExitStack() as scope:
            record = [sb(f"{name}_record{h}", [P, HU, RW], I32, scope) for h in range(2)]
            got = sb(f"{name}_got", [P, U, width], F32, scope)
            hot = sb(f"{name}_hot", [P, U, P], F32, scope)
            if kind in ("cos", "gat"):
                hotT = sb(f"{name}_hotT", [P, 4, P], F32, scope)
            if kind == "cos":
                hot_w = sb(f"{name}_hot_w", [P, 4, P], F32, scope)
                scratch = sb(f"{name}_scratch", [P, 2, D], F32, scope)
                cos = sb(f"{name}_cos", [P, U], F32, scope)
                exps = sb(f"{name}_exps", [P, U], F32, scope)
            if kind == "gat":
                logit = sb(f"{name}_logit", [P, 2, 4, HEADS], F32, scope)
                logit2 = sb(f"{name}_logit2", [P, 2, 4, HEADS], F32, scope)
            acc = {"conv": sums_conv, "msg": sums_msg, "cos": sums_cos, "gat": sums_gat}[kind]
            list_v = records[key].rearrange("(p c) w -> p c w", c=KT)

            def lane(h, j):
                return record[h][:, j, 1:2].bitcast(F32)

            def tile_blocks(eng, regs, t, h):
                eng.load(regs, block_row[0:1, bass.ds(t * U + h * HU, HU)])
                return [eng.snap(r, min_val=0, max_val=NB - 1) for r in regs]

            with nc.Block() as block:
                @block.sync
                def _(sp):
                    sp.dma_start(block_row[:, :], tile_block[key]).then_inc(blocks_in.handle, 16)

                    def body(t, first):
                        for h in range(2):
                            if not first:
                                sp.wait_ge(half_used.handle, half_used.at(t * 2 + h - 1))
                            sp.dma_start(record[h][:, :, :], list_v[:, bass.ds(t * U + h * HU, HU), :]).then_inc(record_in[h].handle, 16)

                    turns(sp, T, body)

                @block.gpsimd
                def _(pool):
                    def body(t, first):
                        for h in range(2):
                            pool.wait_ge(record_in[h].handle, record_in[h].at(t * 16 + 16))
                            pool.sem_inc(waits_passed.handle, 1)
                            for j in range(HU):
                                pool.indirect_dma_start(
                                    out=got[:, h * HU + j, :], out_offset=None, in_=rows,
                                    in_offset=bass.IndirectOffsetOnAxis(ap=record[h][:, j, 0:1], axis=0),
                                    bounds_check=N - 1, oob_is_err=False).then_inc(gathered[h * HU + j].handle, 16)

                    turns(pool, T, body)

                @block.tensor
                def _(pe):
                    if kind in ("cos", "gat"):
                        regs = [pe.alloc_register(f"{name}_pe_block{j}") for j in range(HU)]
                        pe.wait_ge(blocks_in.handle, blocks_in.at(16))

                    def body(t, first):
                        blocks = {}

                        def turn_hot(s):
                            if s % HU == 0:
                                pe.wait_ge(hot_set.handle, hot_set.at(t * 2 + s // HU + 1))
                            if not (first and s < 2):
                                pe.wait_ge(hot_kept.handle, hot_kept.at(t * U + s - 1))
                            pe.transpose(bank[s % 2][:, 0:P], hot[:, s, :], ident[:, :]).then_inc(hot_turned.handle, 1)

                        def look_up(s):
                            if s % HU == 0:
                                blocks[s // HU] = tile_blocks(pe, regs, t, s // HU)
                            b = blocks[s // HU][s % HU]
                            pe.wait_ge(hot_kept.handle, hot_kept.at(t * U + s + 1))
                            if kind == "cos":
                                if not (first and s < 2):
                                    pe.wait_ge(logit_set.handle, logit_set.at(t * U + s - 1))
                                pe.matmul(bank[2 + s % 2][:, 0:D], hotT[:, s % 4, :], unit[:, bass.ds(b, 1), :],
                                          start=True, stop=True).then_inc(target_set.handle, 1)
                            else:
                                q = s // 4
                                if s % 4 == 0 and not (first and q < 2):
                                    pe.wait_ge(logit_set.handle, logit_set.at(t * 4 + q - 1))
                                pe.matmul(bank[2 + q % 2][:, s % 4 * 8:s % 4 * 8 + 8], hotT[:, s % 4, :],
                                          target[:, bass.ds(b, 1), :], start=True, stop=True).then_inc(target_set.handle, 1)

                        def multiply(s):
                            if kind == "conv":
                                if s % HU == 0:
                                    pe.wait_ge(hot_set.handle, hot_set.at(t * 2 + s // HU + 1))
                                pe.wait_ge(gathered[s].handle, gathered[s].at(t * 16 + 16))
                                left, right = got[:, s, :], hot[:, s, :]
                            elif kind == "msg":
                                if s % HU == 0:
                                    pe.wait_ge(hot_set.handle, hot_set.at(t * 2 + s // HU + 1))
                                pe.wait_ge(gathered[s].handle, gathered[s].at(t * 16 + 16))
                                left, right = hot[:, s, :], got[:, s, :]
                            elif kind == "cos":
                                pe.wait_ge(weighted.handle, weighted.at(t * U + s + 1))
                                left, right = hot_w[:, s % 4, :], got[:, s, :]
                            else:
                                pe.wait_ge(weighted.handle, weighted.at(t * U + s + 1))
                                left, right = hot[:, s, :], got[:, s, :]
                            if not (first and s < n_banks):
                                pe.wait_ge(added.handle, added.at(t * U + s + 1 - n_banks))
                            cols = right.shape[-1]
                            ins = pe.matmul(bank[4 + s % n_banks][:, 0:cols], left, right, start=True, stop=True)
                            ins.then_inc(product.handle, 1)

                        stages = {"conv": [(multiply, 0)], "msg": [(multiply, 0)],
                                  "cos": [(turn_hot, 0), (look_up, 1), (multiply, 3)],
                                  "gat": [(turn_hot, 0), (look_up, 1), (multiply, 6)]}[kind]
                        for i in range(U + stages[-1][1]):
                            for stage, lag in stages:
                                if 0 <= i - lag < U:
                                    stage(i - lag)

                    turns(pe, T, body)

                @block.vector
                def _(dve):
                    links = Chain(dve, chain, 2 * U // 4)
                    regs = [dve.alloc_register(f"{name}_dve_block{j}") for j in range(HU)]
                    dve.wait_ge(blocks_in.handle, blocks_in.at(16))

                    def body(t, first):
                        blocks = {}
                        links.turn(t)

                        def set_hot(h):
                            dve.wait_ge(record_in[h].handle, record_in[h].at(t * 16 + 16))
                            if kind == "msg":
                                for j in range(HU):
                                    ins = dve.tensor_scalar(hot[:, h * HU + j, :], iota[:, :], lane(h, j),
                                                            record[h][:, j, 2:3].bitcast(F32), ALU.is_equal, ALU.mult)
                            else:
                                lanes = record[h][:, :, 1:2].bitcast(F32)
                                ins = dve.tensor_tensor(hot[:, h * HU:(h + 1) * HU, :], lanes.to_broadcast([P, HU, P]),
                                                        iota[:, :].unsqueeze(1).to_broadcast([P, HU, P]), ALU.is_equal)
                            ins.then_inc(hot_set.handle, 1)

                        def score(s):
                            dve.wait_ge(target_set.handle, target_set.at(t * U + s + 1))
                            dve.wait_ge(gathered[s].handle, gathered[s].at(t * 16 + 16))
                            if not (first and s < 2):
                                dve.wait_ge(logit_set.handle, logit_set.at(t * U + s - 1))
                            dve.tensor_tensor_reduce(scratch[:, s % 2, :], bank[2 + s % 2][:, 0:D], got[:, s, 0:D], 1.0, 0.0,
                                                     ALU.mult, ALU.add, cos[:, s:s + 1]).then_inc(logit_set.handle, 1)

                        def weigh_hot(s):
                            dve.wait_ge(exp_set.handle, exp_set.at(t * U + s + 1))
                            if not (first and s < 4):
                                dve.wait_ge(product.handle, product.at(t * U + s - 3))
                            dve.tensor_scalar(hot_w[:, s % 4, :], hot[:, s, :], exps[:, s:s + 1], None, ALU.mult).then_inc(weighted.handle, 1)

                        def logits(s):
                            if s % 4 != 3:
                                return
                            q = s // 4
                            dve.wait_ge(target_set.handle, target_set.at(t * U + s + 1))
                            for i in range(4):
                                dve.wait_ge(gathered[4 * q + i].handle, gathered[4 * q + i].at(t * 16 + 16))
                            if not (first and q < 2):
                                dve.wait_ge(exp_set.handle, exp_set.at(t * 4 + q - 1))
                            here = bank[2 + q % 2][:, 0:32].rearrange("p (i c) -> p i c", c=8)
                            a, b = logit[:, q % 2, :, :], logit2[:, q % 2, :, :]
                            links.link(dve.tensor_tensor(a, here[:, :, HEADS:], got[:, 4 * q:4 * q + 4, HID:], ALU.add))
                            links.link(dve.scalar_tensor_tensor(out=b, in0=a, scalar=0.2, in1=a, op0=ALU.mult, op1=ALU.max))
                            dve.tensor_tensor(a, b, here[:, :, 0:HEADS], ALU.subtract).then_inc(logit_set.handle, 1)

                        def weigh_rows(s):
                            dve.wait_ge(exp_set.handle, exp_set.at(t * 4 + s // 4 + 1))
                            feat = got[:, s, 0:HID].rearrange("p (h d) -> p h d", h=HEADS)
                            dve.tensor_tensor(feat, feat, got[:, s, HID:].unsqueeze(2).to_broadcast([P, HEADS, DH]),
                                              ALU.mult).then_inc(weighted.handle, 1)

                        def add(s):
                            if s % HU == 0:
                                blocks[s // HU] = tile_blocks(dve, regs, t, s // HU)
                            place = acc[:, bass.ds(blocks[s // HU][s % HU], 1), :]
                            dve.wait_ge(product.handle, product.at(t * U + s + 1))
                            if not (first and s == 0):
                                dve.wait_ge(added.handle, added.at(t * U + s))
                            cols = place.shape[-1]
                            dve.tensor_tensor(place, place, bank[4 + s % n_banks][:, 0:cols].unsqueeze(1), ALU.add).then_inc(added.handle, 1)
                            if s % HU == HU - 1:
                                dve.wait_ge(added.handle, added.at(t * U + s + 1))
                                dve.sem_inc(half_used.handle, 1)

                        stages = {"conv": [(add, 0)], "msg": [(add, 0)],
                                  "cos": [(score, 0), (weigh_hot, 1), (add, 2)],
                                  "gat": [(logits, 0), (weigh_rows, 4), (add, 5)]}[kind]
                        set_hot(0)
                        set_hot(1)
                        for i in range(U + stages[-1][1]):
                            for stage, lag in stages:
                                if 0 <= i - lag < U:
                                    stage(i - lag)

                    turns(dve, T, body)

                if kind in ("cos", "gat"):
                    @block.scalar
                    def _(act):
                        def body(t, first):
                            def keep_hot(s):
                                act.wait_ge(hot_turned.handle, hot_turned.at(t * U + s + 1))
                                if not (first and s < 4):
                                    act.wait_ge(target_set.handle, target_set.at(t * U + s - 3))
                                act.copy(hotT[:, s % 4, :], bank[s % 2][:, 0:P]).then_inc(hot_kept.handle, 1)

                            def exp_cos(s):
                                act.wait_ge(logit_set.handle, logit_set.at(t * U + s + 1))
                                act.activation(exps[:, s:s + 1], cos[:, s:s + 1], ACT.Exp,
                                               scale=got[:, s, D:D + 1]).then_inc(exp_set.handle, 1)

                            def exp_gat(s):
                                if s % 4 == 3:
                                    q = s // 4
                                    act.wait_ge(logit_set.handle, logit_set.at(t * 4 + q + 1))
                                    act.activation(got[:, 4 * q:4 * q + 4, HID:], logit[:, q % 2, :, :],
                                                   ACT.Exp).then_inc(exp_set.handle, 1)

                            stages = [(keep_hot, 0), (exp_cos, 2)] if kind == "cos" else [(keep_hot, 0), (exp_gat, 2)]
                            for i in range(U + stages[-1][1]):
                                for stage, lag in stages:
                                    if 0 <= i - lag < U:
                                        stage(i - lag)

                        turns(act, T, body)
        for s in record_in:
            s.phase_over(16 * T)
        for s in gathered:
            s.phase_over(16 * T)
        blocks_in.phase_over(16)
        half_used.phase_over(2 * T)
        hot_set.phase_over(2 * T)
        product.phase_over(KT)
        added.phase_over(KT)
        if kind in ("cos", "gat"):
            hot_turned.phase_over(KT)
            hot_kept.phase_over(KT)
            target_set.phase_over(KT)
            weighted.phase_over(KT)
            for s in (logit_set, exp_set):
                s.phase_over(KT if kind == "cos" else KT // 4)
        if kind == "gat":
            chain.phase_over(T * (2 * U // 4))

    def normalise_scales():
        with nc.Block() as block:
            @block.vector
            def _(dve):
                links = Chain(dve, chain, 6)
                links.turn(0)
                dve.tensor_tensor(mean[:, :], stats[:, :, 1], stats[:, :, 4], ALU.add)
                dve.tensor_tensor(rstd[:, :], stats[:, :, 1], stats[:, :, 4], ALU.subtract)
                links.link(dve.tensor_tensor(spread[:, :], stats[:, :, 2], stats[:, :, 5], ALU.add))
                links.link(dve.tensor_scalar(mean[:, :], mean[:, :], 0.5, None, ALU.mult))
                links.link(dve.scalar_tensor_tensor(out=rstd[:, :], in0=rstd[:, :], scalar=0.25, in1=rstd[:, :], op0=ALU.mult, op1=ALU.mult))
                links.link(dve.scalar_tensor_tensor(out=spread[:, :], in0=spread[:, :], scalar=1.0 / D, in1=rstd[:, :], op0=ALU.mult, op1=ALU.add))
                dve.tensor_scalar(spread[:, :], spread[:, :], EPS_LN, None, ALU.add).then_inc(root_in.handle, 1)
                dve.wait_ge(root_set.handle, root_set.at(1))
                links.link(dve.reciprocal(rstd[:, :], rstd[:, :]))

            @block.scalar
            def _(act):
                act.wait_ge(root_in.handle, root_in.at(1))
                act.activation(rstd[:, :], spread[:, :], ACT.Sqrt).then_inc(root_set.handle, 1)
        root_in.phase_over(1)
        root_set.phase_over(1)
        chain.phase_over(5)

    rows_out = staged = work = square = None

    def over_nodes(name, loop, *args):
        nonlocal rows_out, staged, work, square
        with ExitStack() as scope:
            rows_out = [sb(f"{name}_rows{j}", [P, W_GAT], F32, scope) for j in range(2)]
            staged = [sb(f"{name}_staged{j}", [P, KC * P], F32, scope) for j in range(2)]
            work = [sb(f"{name}_work{j}", [P, HID], F32, scope) for j in range(2)]
            square = [sb(f"{name}_square{j}", [P, 4], F32, scope) for j in range(2)]
            loop(*args)

    def blk(a, b):
        return a[:, bass.ds(b, 1), :].rearrange("p a w -> p (a w)")

    def col(a, b):
        return a[:, bass.ds(b, 1)]

    def store_rows(sp, table, width, t, first):
        for j in range(2):
            sp.wait_ge(block_rows.handle, block_rows.at(t * 2 + j + 1))
            sp.dma_start(table[bass.ds((t * 2 + j) * P, P), :], rows_out[j][:, 0:width]).then_inc(stored[j].handle, 16)

    def all_stored(sp):
        for j in range(2):
            sp.wait_ge(stored[j].handle, stored[j].at(16 * NT))

    def load_x():
        with nc.Block() as block:
            @block.gpsimd
            def _(pool):
                pool.memset(nodes[:, NB - 1, :], 0.0).then_inc(root_in.handle, 1)

            @block.sync
            def _(sp):
                sp.wait_ge(root_in.handle, root_in.at(1))
                sp.dma_start(nodes[:, 0:NB - 1, :], x_in[0:FULL, :].rearrange("(b p) d -> p b d", p=P)).then_inc(x_loaded.handle, 16)
                sp.dma_start(nodes[0:LAST, NB - 1, :], x_in[FULL:N, :]).then_inc(x_loaded.handle, 16)
                sp.wait_ge(x_loaded.handle, x_loaded.at(32))
        root_in.phase_over(1)

    def conv_rows_loop(between):
        table = v["rows_conv"][int(between)]
        per = 4 if between else 0
        with nc.Block() as block:
            @block.scalar
            def _(act):
                def body(t, first):
                    if between:
                        for j in range(2):
                            if not first:
                                act.wait_ge(block_product.handle, block_product.at(t * 2 + j - 1))
                                act.sem_inc(waits_passed.handle, 1)
                            act.copy(staged[j][:, 0:P], blk(sums_conv, t * 2 + j)).then_inc(block_staged.handle, 1)
                    for j in range(2):
                        act.wait_ge(block_turned.handle, block_turned.at(t * 2 + j + 1))
                        act.sem_inc(waits_passed.handle, 1)
                        act.copy(blk(sums_conv, t * 2 + j), bank[2 + j][:, 0:P]).then_inc(turned_kept.handle, 1)

                turns(act, NT, body)

            @block.tensor
            def _(pe):
                def body(t, first):
                    if between:
                        for j in range(2):
                            pe.wait_ge(block_staged.handle, block_staged.at(t * 2 + j + 1))
                            if not first:
                                pe.wait_ge(block_rows.handle, block_rows.at(t * 2 + j - 1))
                            pe.matmul(bank[j][:, 0:D], staged[j][:, 0:P], v["w1"][:, :], start=True, stop=True).then_inc(block_product.handle, 1)
                    for j in range(2):
                        pe.wait_ge(block_rows.handle, block_rows.at(t * 2 + j + 1))
                        if not first:
                            pe.wait_ge(turned_kept.handle, turned_kept.at(t * 2 + j - 1))
                        pe.transpose(bank[2 + j][:, 0:P], rows_out[j][:, 0:D], ident[:, :]).then_inc(block_turned.handle, 1)

                turns(pe, NT, body)

            @block.vector
            def _(dve):
                links = Chain(dve, chain, 2 * per)

                def body(t, first):
                    links.turn(t)
                    for j in range(2):
                        b = t * 2 + j
                        rows = rows_out[j][:, 0:D]
                        if between:
                            w = work[j][:, 0:D]
                            dve.wait_ge(block_product.handle, block_product.at(t * 2 + j + 1))
                            links.link(dve.tensor_scalar(w, bank[j][:, 0:D], col(norm["dst"], b), None, ALU.mult))
                            links.link(dve.tensor_tensor(w, w, v["bn_scale"][:, :], ALU.mult))
                            links.link(dve.tensor_tensor(w, w, v["bn_shift"][:, :], ALU.add))
                            links.link(dve.scalar_tensor_tensor(out=w, in0=w, scalar=0.01, in1=w, op0=ALU.mult, op1=ALU.max))
                        else:
                            w = blk(nodes, b)
                        if not first:
                            dve.wait_ge(stored[j].handle, stored[j].at(t * 16))
                            dve.wait_ge(block_turned.handle, block_turned.at(t * 2 + j - 1))
                        dve.tensor_scalar(rows, w, col(norm["src"], b), None, ALU.mult).then_inc(block_rows.handle, 1)

                turns(dve, NT, body)

            @block.sync
            def _(sp):
                turns(sp, NT, lambda t, first: store_rows(sp, table, D, t, first))
                all_stored(sp)
        if between:
            block_staged.phase_over(NB)
            block_product.phase_over(NB)
        block_rows.phase_over(NB)
        block_turned.phase_over(NB)
        turned_kept.phase_over(NB)
        chain.phase_over(NT * 2 * per)
        for j in range(2):
            stored[j].phase_over(16 * NT)

    def conv_out_loop():
        with nc.Block() as block:
            @block.scalar
            def _(act):
                def body(t, first):
                    for j in range(2):
                        if not first:
                            act.wait_ge(block_product.handle, block_product.at(t * 2 + j - 1))
                            act.sem_inc(waits_passed.handle, 1)
                        act.copy(staged[j][:, 0:P], blk(sums_conv, t * 2 + j)).then_inc(block_staged.handle, 1)

                turns(act, NT, body)

            @block.tensor
            def _(pe):
                def body(t, first):
                    for j in range(2):
                        pe.wait_ge(block_staged.handle, block_staged.at(t * 2 + j + 1))
                        if not first:
                            pe.wait_ge(block_rows.handle, block_rows.at(t * 2 + j - 1))
                        pe.matmul(bank[j][:, 0:D], staged[j][:, 0:P], v["w2"][:, :], start=True, stop=True).then_inc(block_product.handle, 1)

                turns(pe, NT, body)

            @block.vector
            def _(dve):
                links = Chain(dve, chain, 2)

                def body(t, first):
                    links.turn(t)
                    for j in range(2):
                        b = t * 2 + j
                        dve.wait_ge(block_product.handle, block_product.at(t * 2 + j + 1))
                        dve.scalar_tensor_tensor(out=work[j][:, 0:D], in0=bank[j][:, 0:D], scalar=col(norm["dst"], b),
                                                 in1=v["b2_row"][:, :], op0=ALU.mult, op1=ALU.add).then_inc(block_rows.handle, 1)
                        dve.wait_ge(block_rows.handle, block_rows.at(t * 2 + j + 1))
                        links.link(dve.tensor_tensor(blk(nodes, b), blk(nodes, b), work[j][:, 0:D], ALU.add))
                        dve.bn_stats(blk(stats, b), blk(nodes, b))

                turns(dve, NT, body)
        block_staged.phase_over(NB)
        block_product.phase_over(NB)
        block_rows.phase_over(NB)
        chain.phase_over(NT * 2)

    def table_loop(kind):
        table, width, weights = {"msg": (v["rows_msg"], D, v["w_msgT"]), "cos": (v["rows_cos"], W_COS, v["w_cos"]),
                                 "gat": (v["rows_gat"], W_GAT, v["w_gat"])}[kind]
        cols = weights.shape[-1]
        per = {"msg": 0, "cos": 4, "gat": 0}[kind]
        with nc.Block() as block:
            @block.tensor
            def _(pe):
                def body(t, first):
                    for j in range(2):
                        pe.wait_ge(block_staged.handle, block_staged.at(t * 2 + j + 1))
                        if not first:
                            pe.wait_ge(turned_kept.handle, turned_kept.at(t * 2 + j - 1))
                        pe.transpose(bank[2 + j][:, 0:P], staged[j][:, P:2 * P], ident[:, :]).then_inc(block_turned.handle, 1)
                    for j in range(2):
                        pe.wait_ge(turned_kept.handle, turned_kept.at(t * 2 + j + 1))
                        if not first:
                            pe.wait_ge(block_rows.handle, block_rows.at(t * 2 + j - 1))
                        pe.matmul(bank[j][:, 0:cols], staged[j][:, 0:P], weights[:, :], start=True, stop=True).then_inc(block_product.handle, 1)

                turns(pe, NT, body)

            @block.scalar
            def _(act):
                def body(t, first):
                    for j in range(2):
                        act.wait_ge(block_turned.handle, block_turned.at(t * 2 + j + 1))
                        if not first:
                            act.wait_ge(block_product.handle, block_product.at(t * 2 + j - 1))
                        act.copy(staged[j][:, 0:P], bank[2 + j][:, 0:P]).then_inc(turned_kept.handle, 1)
                    if kind == "cos":
                        for j in range(2):
                            act.wait_ge(root_in.handle, root_in.at(t * 2 + j + 1))
                            act.activation(square[j][:, 1:2], square[j][:, 0:1], ACT.Sqrt).then_inc(root_set.handle, 1)

                turns(act, NT, body)

            @block.vector
            def _(dve):
                links = Chain(dve, chain, 2 * per)
                if kind != "msg":
                    dve.memset((sums if kind == "gat" else sums[:, 0:NB * W_COS])[:, :], 0.0)
                else:
                    dve.memset(sums[:, 0:NB * D], 0.0)

                def body(t, first):
                    links.turn(t)
                    for j in range(2):
                        b = t * 2 + j
                        if not first:
                            dve.wait_ge(block_turned.handle, block_turned.at(t * 2 + j - 1))
                        dve.tensor_scalar(staged[j][:, P:2 * P], blk(nodes, b), col(mean, b), col(rstd, b), ALU.subtract,
                                          ALU.mult).then_inc(block_staged.handle, 1)
                        dve.tensor_scalar(blk(nodes, b), blk(nodes, b), col(mean, b), col(rstd, b), ALU.subtract, ALU.mult)
                    for j in range(2):
                        b = t * 2 + j
                        rows = rows_out[j]
                        dve.wait_ge(block_product.handle, block_product.at(t * 2 + j + 1))
                        if not first:
                            dve.wait_ge(stored[j].handle, stored[j].at(t * 16))
                        if kind == "msg":
                            dve.tensor_tensor(rows[:, 0:D], bank[j][:, 0:D], v["b_msg_row"][:, :], ALU.add).then_inc(block_rows.handle, 1)
                        elif kind == "gat":
                            dve.tensor_scalar(blk(target, b), bank[j][:, HID:HID + 8], 1.0, None, ALU.mult)
                            dve.tensor_copy(rows[:, 0:W_GAT], bank[j][:, 0:W_GAT]).then_inc(block_rows.handle, 1)
                        else:
                            links.link(dve.tensor_copy(rows[:, 0:D], bank[j][:, 0:D]))
                            links.link(dve.tensor_tensor_reduce(work[j][:, 0:D], rows[:, 0:D], rows[:, 0:D], 1.0, 0.0, ALU.mult,
                                                                ALU.add, square[j][:, 0:1]))
                            dve.tensor_scalar(square[j][:, 0:1], square[j][:, 0:1], 1e-16, None, ALU.max).then_inc(root_in.handle, 1)
                            dve.wait_ge(root_set.handle, root_set.at(t * 2 + j + 1))
                            dve.memset(rows[:, D + 1:D + 2], 1.0)
                            links.link(dve.reciprocal(square[j][:, 2:3], square[j][:, 1:2]))
                            dve.tensor_scalar(blk(unit, b), rows[:, 0:D], square[j][:, 2:3], None, ALU.mult)
                            links.link(dve.tensor_copy(rows[:, D:D + 1], square[j][:, 2:3]))
                            dve.sem_inc(block_rows.handle, 1)

                turns(dve, NT, body)

            @block.sync
            def _(sp):
                turns(sp, NT, lambda t, first: store_rows(sp, table, width, t, first))
                all_stored(sp)
        for s in (block_staged, block_product, block_rows, block_turned, turned_kept):
            s.phase_over(NB)
        if kind == "cos":
            root_in.phase_over(NB)
            root_set.phase_over(NB)
        chain.phase_over(NT * 2 * per)
        for j in range(2):
            stored[j].phase_over(16 * NT)

    def msg_out_loop():
        with nc.Block() as block:
            @block.vector
            def _(dve):
                links = Chain(dve, chain, 2)

                def body(t, first):
                    links.turn(t)
                    for j in range(2):
                        b = t * 2 + j
                        links.link(dve.scalar_tensor_tensor(out=blk(nodes, b), in0=blk(sums_msg, b), scalar=0.0, in1=blk(nodes, b),
                                                            op0=ALU.max, op1=ALU.add))
                        dve.bn_stats(blk(stats, b), blk(nodes, b))

                turns(dve, NT, body)
        chain.phase_over(2 * NT)

    def cos_out_loop():
        with nc.Block() as block:
            @block.vector
            def _(dve):
                links = Chain(dve, chain, 2)
                links.turn(0)
                links.link(dve.tensor_scalar(spread[:, :], sums_cos[:, :, D + 1], EPS_ATT, None, ALU.add))
                links.link(dve.reciprocal(spread[:, :], spread[:, :]))
                chain.phase_over(2)

                def body(t, first):
                    links.turn(t)
                    for j in range(2):
                        b = t * 2 + j
                        links.link(dve.scalar_tensor_tensor(out=blk(nodes, b), in0=sums_cos[:, bass.ds(b, 1), 0:D].rearrange("p a w -> p (a w)"),
                                                            scalar=col(spread, b), in1=blk(nodes, b), op0=ALU.mult, op1=ALU.add))
                        dve.bn_stats(blk(stats, b), blk(nodes, b))

                turns(dve, NT, body)
        chain.phase_over(2 * NT)

    el_max = sb("el_max", [P, HEADS])
    el_all = sb("el_all", [P, HEADS])

    def gat_shift():
        with nc.Block() as block:
            @block.vector
            def _(dve):
                links = Chain(dve, chain, 3)
                links.turn(0)
                for h in range(HEADS):
                    ins = dve.tensor_reduce(el_max[:, h:h + 1], target[:, :, h], AX.X, ALU.max)
                ins.then_inc(root_in.handle, 1)
                dve.wait_ge(root_set.handle, root_set.at(1))
                er = target[:, :, HEADS:2 * HEADS]
                links.link(dve.tensor_tensor(target[:, :, 0:HEADS], er, el_all[:, :].unsqueeze(1).to_broadcast([P, NB, HEADS]), ALU.add))
                shift = target[:, :, 0:HEADS]
                links.link(dve.scalar_tensor_tensor(out=shift, in0=shift, scalar=0.2, in1=shift, op0=ALU.mult, op1=ALU.max))

            @block.gpsimd
            def _(pool):
                pool.wait_ge(root_in.handle, root_in.at(1))
                pool.partition_all_reduce(el_all[:, :], el_max[:, :], P, bass.bass_isa.ReduceOp.max).then_inc(root_set.handle, 1)
        root_in.phase_over(1)
        root_set.phase_over(1)
        chain.phase_over(2)

    def gat_out_loop():
        with ExitStack() as scope:
            hT = sb("hT", [P, KC, 2 * P], F32, scope)
            gate = {k: sb(f"gate_{k}", [P, KC, 2 * P], F32, scope) for k in ("r", "z", "n")}
            state = sb("state", [P, KC, 2 * P], F32, scope)
            share = [sb(f"share{j}", [P, HEADS], F32, scope) for j in range(2)]
            attended = signal("attended")
            attended_turned = signal("attended_turned")
            attended_kept = signal("attended_kept")
            gate_sum = signal("gate_sum")
            nodes_set = signal("nodes_set")
            gates_used = signal("gates_used")
            gate_set = signal("gate_set")
            state_set = signal("state_set")
            result = signal("result")
            with nc.Block() as block:
                @block.vector
                def _(dve):
                    links = Chain(dve, chain, 2 * 3 + 2 * 2)

                    def body(t, first):
                        links.turn(t)
                        for j in range(2):
                            b = t * 2 + j
                            w = work[j]
                            links.link(dve.tensor_scalar(share[j][:, :], sums_gat[:, bass.ds(b, 1), HID:].rearrange("p a w -> p (a w)"),
                                                         1e-30, None, ALU.max))
                            links.link(dve.reciprocal(share[j][:, :], share[j][:, :]))
                            if not first:
                                dve.wait_ge(attended_turned.handle, attended_turned.at(t * 2 + j - 1))
                            links.link(dve.tensor_tensor(w[:, :].rearrange("p (h d) -> p h d", h=HEADS),
                                                         sums_gat[:, bass.ds(b, 1), 0:HID].rearrange("p a (h d) -> p (a h) d", h=HEADS),
                                                         share[j][:, :].unsqueeze(2).to_broadcast([P, HEADS, DH]), ALU.mult))
                            dve.tensor_tensor(w[:, :], w[:, :], v["bias_gat_row"][:, :], ALU.add).then_inc(attended.handle, 1)
                        dve.wait_ge(gate_set.handle, gate_set.at(t * 3 + 1))
                        dve.wait_ge(gate_sum.handle, gate_sum.at(t * 3 + 3))
                        for c in range(KC):
                            ins = dve.scalar_tensor_tensor(out=gate["n"][:, c, :], in0=gate["r"][:, c, :], scalar=v["b_hid_n"][:, c:c + 1],
                                                           in1=bank[6][:, c * 2 * P:(c + 1) * 2 * P], op0=ALU.mult, op1=ALU.add)
                        ins.then_inc(gates_used.handle, 1)
                        dve.wait_ge(gate_set.handle, gate_set.at(t * 3 + 3))
                        if not first:
                            dve.wait_ge(result.handle, result.at(t * 2))
                        dve.tensor_tensor(state[:, :, :], gate["z"][:, :, :], gate["n"][:, :, :], ALU.mult).then_inc(state_set.handle, 1)
                        for j in range(2):
                            b = t * 2 + j
                            dve.wait_ge(result.handle, result.at(t * 2 + j + 1))
                            links.link(dve.tensor_tensor(staged[j][:, 0:D], bank[3 + 4 * j][:, 0:D], v["b_out_row"][:, :], ALU.add))
                            links.link(dve.tensor_tensor(blk(nodes, b), blk(nodes, b), staged[j][:, 0:D], ALU.add))
                            ins = dve.bn_stats(blk(stats, b), blk(nodes, b))
                        ins.then_inc(nodes_set.handle, 1)

                    turns(dve, NT, body)

                @block.tensor
                def _(pe):
                    def body(t, first):
                        for j in range(2):
                            pe.wait_ge(attended.handle, attended.at(t * 2 + j + 1))
                            if not first:
                                pe.wait_ge(attended_kept.handle, attended_kept.at(t * 2 + j - 1))
                            for c in range(KC):
                                ins = pe.transpose(bank[j][:, c * P:(c + 1) * P], work[j][:, c * P:(c + 1) * P], ident[:, :])
                            ins.then_inc(attended_turned.handle, 1)
                        pe.wait_ge(attended_kept.handle, attended_kept.at(t * 2 + 2))
                        if not first:
                            pe.wait_ge(gate_set.handle, gate_set.at(t * 3))
                            pe.wait_ge(gates_used.handle, gates_used.at(t))
                        for g in range(3):
                            for c in range(KC):
                                for k in range(KC):
                                    row = (g * KC + c) * P
                                    ins = pe.matmul(bank[4 + g][:, c * 2 * P:(c + 1) * 2 * P], v["w_ihT"][:, k, row:row + P],
                                                    hT[:, k, :], start=(k == 0), stop=(k == KC - 1))
                            ins.then_inc(gate_sum.handle, 1)
                        pe.wait_ge(state_set.handle, state_set.at(t + 1))
                        if not first:
                            pe.wait_ge(nodes_set.handle, nodes_set.at(t))
                        for j in range(2):
                            for k in range(KC):
                                ins = pe.matmul(bank[3 + 4 * j][:, 0:D], state[:, k, j * P:(j + 1) * P], v["w_outT"][:, k, :],
                                                start=(k == 0), stop=(k == KC - 1))
                            ins.then_inc(result.handle, 1)

                    turns(pe, NT, body)

                @block.scalar
                def _(act):
                    def body(t, first):
                        for j in range(2):
                            act.wait_ge(attended_turned.handle, attended_turned.at(t * 2 + j + 1))
                            if not first:
                                act.wait_ge(gate_sum.handle, gate_sum.at(t * 3))
                            act.copy(hT[:, :, j * P:(j + 1) * P],
                                     bank[j][:, 0:KC * P].rearrange("p (c n) -> p c n", c=KC)).then_inc(attended_kept.handle, 1)
                        if not first:
                            act.wait_ge(gates_used.handle, gates_used.at(t))
                            act.wait_ge(state_set.handle, state_set.at(t))
                        for n, k in enumerate("rz"):
                            act.wait_ge(gate_sum.handle, gate_sum.at(t * 3 + n + 1))
                            for c in range(KC):
                                ins = act.activation(gate[k][:, c, :], bank[4 + n][:, c * 2 * P:(c + 1) * 2 * P], ACT.Sigmoid,
                                                     bias=v["b_gate"][:, n * KC + c:n * KC + c + 1], scale=(1.0, -1.0)[n])
                            ins.then_inc(gate_set.handle, 1)
                        act.wait_ge(gates_used.handle, gates_used.at(t + 1))
                        for c in range(KC):
                            ins = act.activation(gate["n"][:, c, :], gate["n"][:, c, :], ACT.Tanh,
                                                 bias=v["b_gate"][:, 2 * KC + c:2 * KC + c + 1])
                        ins.then_inc(gate_set.handle, 1)

                    turns(act, NT, body)
        chain.phase_over(NT * 10)

    def write_out():
        parts = 7
        size = NB // parts
        with nc.Block() as block:
            @block.vector
            def _(dve):
                links = Chain(dve, chain, parts)
                links.turn(0)
                for q in range(parts):
                    here = nodes[:, q * size:(q + 1) * size, :]
                    links.link(dve.tensor_tensor(here, here, mean[:, q * size:(q + 1) * size].unsqueeze(2).to_broadcast([P, size, D]),
                                                 ALU.subtract))
                    dve.tensor_tensor(here, here, rstd[:, q * size:(q + 1) * size].unsqueeze(2).to_broadcast([P, size, D]),
                                      ALU.mult).then_inc(block_staged.handle, 1)

            @block.sync
            def _(sp):
                for q in range(parts):
                    sp.wait_ge(block_staged.handle, block_staged.at(q + 1))
                    b0, b1 = q * size, min((q + 1) * size, NB - 1)
                    sp.dma_start(out[b0 * P:b1 * P, :].rearrange("(b p) d -> p b d", p=P), nodes[:, b0:b1, :]).then_inc(stored[0].handle, 16)
                sp.dma_start(out[FULL:N, :], nodes[0:LAST, NB - 1, :]).then_inc(stored[0].handle, 16)
                sp.wait_ge(stored[0].handle, stored[0].at(16 * (parts + 1)))
        block_staged.phase_over(parts)
        stored[0].phase_over(16 * (parts + 1))
        chain.phase_over(parts)

    load_x()
    over_nodes("first", conv_rows_loop, False)
    walk("conv1", "dst", v["rows_conv"][0], D, "conv")
    over_nodes("between", conv_rows_loop, True)
    walk("conv2", "dst", v["rows_conv"][1], D, "conv")
    over_nodes("conv_out", conv_out_loop)
    normalise_scales()
    if v.get("stop") == 1:
        return write_out()
    over_nodes("msg_rows", table_loop, "msg")
    walk("msg", "dst", v["rows_msg"], D, "msg")
    msg_out_loop()
    normalise_scales()
    if v.get("stop") == 2:
        return write_out()
    over_nodes("cos_rows", table_loop, "cos")
    walk("cos", "src", v["rows_cos"], W_COS, "cos")
    cos_out_loop()
    normalise_scales()
    if v.get("stop") == 3:
        return write_out()
    over_nodes("gat_rows", table_loop, "gat")
    gat_shift()
    walk("gat", "dst", v["rows_gat"], W_GAT, "gat")
    over_nodes("gat_out", gat_out_loop)
    normalise_scales()
    write_out()


_INS = {"x": "x", "src": "src", "dst": "dst", "edge_weight": "edge_weight", "L0_gnn_W1": "W1", "L0_gnn_b1": "b1",
        "L0_gnn_W2": "W2", "L0_gnn_b2": "b2", "L0_gnn_gamma": "gamma", "L0_gnn_beta": "beta",
        "L0_gnn_run_mean": "run_mean", "L0_gnn_run_var": "run_var", "L1_gnn_W": "W_msg", "L1_gnn_b": "b_msg",
        "L2_gnn_kernel": "W_cos", "L3_gnn_W_fc": "W_fc", "L3_gnn_attn_l": "attn_l", "L3_gnn_attn_r": "attn_r",
        "L3_gnn_bias_gat": "bias_gat", "L3_gnn_W_ih": "W_ih", "L3_gnn_b_ih": "b_ih", "L3_gnn_b_hh": "b_hh",
        "L3_gnn_W_out": "W_out", "L3_gnn_b_out": "b_out"}


def kernel(**inputs):
    import numpy as _np
    import concourse.bacc as _bacc
    from concourse import mybir as _mybir
    from concourse.bass_utils import run_bass_kernel_spmd as _run

    nc = _bacc.Bacc("TRN2", target_bir_lowering=False, num_devices=1)
    arrays, args = {}, {}
    for name, short in _INS.items():
        a = _np.ascontiguousarray(inputs[name])
        arrays[f"in_{name}_dram"] = a
        args[short] = nc.dram_tensor(f"in_{name}_dram", a.shape, _mybir.dt.from_np(a.dtype), kind="ExternalInput").ap()
    args["out"] = nc.dram_tensor("out_0_dram", (N, D), F32, kind="ExternalOutput").ap()
    program(nc, **args)
    r = _run(nc, [arrays], core_ids=[0])
    return r.results[0]["out_0_dram"]
```

```python
from contextlib import ExitStack

import concourse.bass as bass
from concourse import mybir

ALU = mybir.AluOpType
ACT = mybir.ActivationFunctionType
AX = mybir.AxisListType
F32 = mybir.dt.float32
BF16 = mybir.dt.bfloat16
I32 = mybir.dt.int32

P = 128
N = 12500
E = 212500
D = 128
HEADS = 4
HID = 256
DH = HID // HEADS
GATES = 3 * HID
GC = GATES // P
KC = HID // P

NB = -(-N // P)
LAST = N - (NB - 1) * P
NR = NB * P
NK = NB + 1

EC = -(-E // P)
EL = E - (P - 1) * EC
SU = 11
ST = EC // SU
SG = ((0, 6), (6, 5))
PAIR_LAG = 2
NO_EDGE = NB * P
FAR = float(1 << 26)
NO_LANE = 999.0

U = 16
HU = U // 2
KT = -(-((E + NB * (P - 1)) // P) // U) * U
T = KT // U
RW = 4

VH = 2
NT = NB // 2
W_COS = D + 2
W_GAT = HID + HEADS
EPS_LN = 1e-5
EPS_BN = 1e-5
EPS_ATT = 1e-8
WIDE = 60.0
LOW = -1e30
assert ST * SU == EC and NT * 2 == NB


class Signal:

    def __init__(self, handle):
        self.handle = handle
        self.start = 0

    def at(self, n):
        return n + self.start

    def phase_over(self, n):
        self.start += n


class Chain:

    def __init__(self, eng, steps, per_turn):
        self.eng, self.steps, self.per_turn = eng, steps, per_turn

    def turn(self, t):
        self.t, self.n = t, 0

    def link(self, ins):
        self.n += 1
        assert self.n <= self.per_turn
        ins.then_inc(self.steps.handle, 1)
        self.eng.wait_ge(self.steps.handle, self.steps.at(self.t * self.per_turn + self.n))


def turns(eng, count, body):
    body(0, True)
    with eng.Fori(1, count) as t:
        body(t, False)


def program(nc, x, src, dst, edge_weight, W1, b1, W2, b2, gamma, beta, run_mean, run_var, W_msg, b_msg, W_cos,
            W_fc, attn_l, attn_r, bias_gat, W_ih, b_ih, b_hh, W_out, b_out, out):
    ctx = ExitStack()
    with ctx:
        def sb(name, shape, dt=F32, scope=ctx):
            return scope.enter_context(nc.sbuf_tensor(name, shape, dt))

        def signal(name):
            return Signal(ctx.enter_context(nc.semaphore(name)))

        bank = [ctx.enter_context(nc.psum_tensor(f"bank{i}", [P, 512], F32)) for i in range(8)]

        waits_passed = signal("waits_passed")

        rows_conv = [nc.dram_tensor(f"rows_conv{i}", [NR, D], F32).ap() for i in range(2)]
        rows_msg = nc.dram_tensor("rows_msg", [NR, D], F32).ap()
        rows_cos = nc.dram_tensor("rows_cos", [NR, W_COS], F32).ap()
        rows_gat = nc.dram_tensor("rows_gat", [NR, W_GAT], F32).ap()
        records = {k: nc.dram_tensor(f"records_{k}", [P * KT, RW], I32).ap() for k in ("dst", "src")}
        tile_block = {k: nc.dram_tensor(f"tile_block_{k}", [1, KT], I32).ap() for k in ("dst", "src")}

        ident = sb("ident", [P, P])
        iota = sb("iota", [P, P])
        ones = sb("ones", [P, P])
        w1 = sb("w1", [P, D])
        w2 = sb("w2", [P, D])
        w_msgT = sb("w_msgT", [P, D])
        w_cos = sb("w_cos", [P, D])
        w_gat = sb("w_gat", [P, HID + 2 * HEADS])
        w_ihT = sb("w_ihT", [P, KC, GATES])
        w_outT = sb("w_outT", [P, KC, D])
        bn_scale = sb("bn_scale", [P, D])
        bn_shift = sb("bn_shift", [P, D])
        b2_row = sb("b2_row", [P, D])
        b_msg_row = sb("b_msg_row", [P, D])
        bias_gat_row = sb("bias_gat_row", [P, HID])
        b_out_row = sb("b_out_row", [P, D])
        b_gate = sb("b_gate", [P, GC])
        b_hid_n = sb("b_hid_n", [P, KC])
        norm = {k: sb(f"norm_{k}", [P, NB]) for k in ("dst", "src")}

        load_weights(nc, ctx, locals())
        sort_edges(nc, ctx, locals())
        layers(nc, ctx, locals())


def row_of(ap):
    return ap.rearrange("(a d) -> a d", a=1).broadcast_to([P, ap.shape[0]])


def load_weights(nc, ctx, v):
    (bank, ident, iota, ones, w1, w2, w_msgT, w_cos, w_gat, w_ihT, w_outT, bn_scale, bn_shift, b2_row, b_msg_row,
     bias_gat_row, b_out_row, b_gate, b_hid_n) = (v[k] for k in (
         "bank", "ident", "iota", "ones", "w1", "w2", "w_msgT", "w_cos", "w_gat", "w_ihT", "w_outT", "bn_scale",
         "bn_shift", "b2_row", "b_msg_row", "bias_gat_row", "b_out_row", "b_gate", "b_hid_n"))
    signal = v["signal"]
    with ExitStack() as scope:
        def sb(name, shape, dt=F32):
            return v["sb"](name, shape, dt, scope)

        iota_i = sb("iota_i", [P, P], I32)
        msg_in = sb("msg_in", [P, D])
        fc_in = sb("fc_in", [P, KC, D])
        ih_in = sb("ih_in", [P, GC, HID])
        out_in = sb("out_in", [P, HID])
        attn = sb("attn", [P, KC, 2 * HEADS])
        rows = {k: sb(f"row_{k}", [P, D]) for k in ("b1", "gamma", "beta", "mean", "var")}
        b_hh_col = sb("b_hh_col", [P, GC])

        weights_in = signal("weights_in")
        attn_zero = signal("attn_zero")
        attn_in = signal("attn_in")
        consts_set = signal("consts_set")
        iota_set = signal("iota_set")
        turned = signal("turned")
        kept = signal("kept")
        var_eps = signal("var_eps")
        var_root = signal("var_root")
        chain = signal("chain_weights")
        loads = [
            (w1[:, :], v["W1"]), (w2[:, :], v["W2"]), (msg_in[:, :], v["W_msg"]), (w_cos[:, :], v["W_cos"]),
            (fc_in[:, :, :], v["W_fc"].rearrange("(c p) d -> p c d", p=P)),
            (ih_in[:, :, :], v["W_ih"].rearrange("(c p) k -> p c k", p=P)), (out_in[:, :], v["W_out"]),
            (rows["b1"][:, :], row_of(v["b1"])), (rows["gamma"][:, :], row_of(v["gamma"])),
            (rows["beta"][:, :], row_of(v["beta"])), (rows["mean"][:, :], row_of(v["run_mean"])),
            (rows["var"][:, :], row_of(v["run_var"])), (b2_row[:, :], row_of(v["b2"])),
            (b_msg_row[:, :], row_of(v["b_msg"])), (bias_gat_row[:, :], row_of(v["bias_gat"])),
            (b_out_row[:, :], row_of(v["b_out"])),
            (b_gate[:, :], v["b_ih"].rearrange("(c p) -> p c", p=P)),
            (b_hh_col[:, :], v["b_hh"].rearrange("(c p) -> p c", p=P)),
        ]
        turns_of = [(msg_in[:, :], w_msgT[:, :])]
        turns_of += [(fc_in[:, c, :], w_gat[:, c * P:(c + 1) * P]) for c in range(KC)]
        turns_of += [(ih_in[:, g, c * P:(c + 1) * P], w_ihT[:, c, g * P:(g + 1) * P]) for g in range(GC) for c in range(KC)]
        turns_of += [(out_in[:, c * P:(c + 1) * P], w_outT[:, c, :]) for c in range(KC)]

        with nc.Block() as block:
            @block.sync
            def _(sp):
                with nc.allow_non_contiguous_dma(reason="biases, a few hundred words, once"):
                    for to, of in loads:
                        sp.dma_start(to, of).then_inc(weights_in.handle, 16)
                    sp.wait_ge(attn_zero.handle, attn_zero.at(1))
                    for n, a in enumerate((v["attn_l"], v["attn_r"])):
                        for h in range(HEADS):
                            lanes = slice(h % 2 * DH, h % 2 * DH + DH)
                            column = n * HEADS + h
                            sp.dma_start(attn[lanes, h // 2, column:column + 1],
                                         a[h:h + 1, :].rearrange("a d -> d a")).then_inc(attn_in.handle, 16)

            @block.gpsimd
            def _(pool):
                pool.iota(iota_i[:, :], pattern=[[1, P]], base=0, channel_multiplier=0).then_inc(iota_set.handle, 1)
                pool.memset(ident[:, :], 0.0).then_inc(consts_set.handle, 1)
                pool.wait_ge(consts_set.handle, consts_set.at(1))
                pool.affine_select(out=ident[:, :], in_=ident[:, :], compare_op=ALU.not_equal, fill=1.0, base=0,
                                   pattern=[[-1, P]], channel_multiplier=1).then_inc(consts_set.handle, 1)

            @block.tensor
            def _(pe):
                pe.wait_ge(consts_set.handle, consts_set.at(2))
                pe.wait_ge(weights_in.handle, weights_in.at(16 * len(loads)))
                for i, (of, _) in enumerate(turns_of):
                    if i >= 4:
                        pe.wait_ge(kept.handle, kept.at(i - 3))
                    pe.transpose(bank[i % 4][:, 0:P], of, ident[:, :]).then_inc(turned.handle, 1)
                pe.wait_ge(attn_in.handle, attn_in.at(16 * 2 * HEADS))
                for c in range(KC):
                    ins = pe.matmul(bank[4][:, 0:2 * HEADS], fc_in[:, c, :], attn[:, c, :], start=(c == 0),
                                    stop=(c == KC - 1))
                ins.then_inc(turned.handle, 1)

            @block.vector
            def _(dve):
                links = Chain(dve, chain, 8)
                links.turn(0)
                dve.memset(attn[:, :, :], 0.0).then_inc(attn_zero.handle, 1)
                dve.memset(ones[:, :], 1.0)
                dve.wait_ge(iota_set.handle, iota_set.at(1))
                dve.tensor_copy(iota[:, :], iota_i[:, :])
                dve.wait_ge(weights_in.handle, weights_in.at(16 * len(loads)))
                dve.tensor_scalar(rows["var"][:, :], rows["var"][:, :], EPS_BN, None, ALU.add).then_inc(var_eps.handle, 1)
                dve.wait_ge(var_root.handle, var_root.at(1))
                links.link(dve.reciprocal(rows["var"][:, :], rows["var"][:, :]))
                links.link(dve.tensor_tensor(bn_scale[:, :], rows["var"][:, :], rows["gamma"][:, :], ALU.mult))
                links.link(dve.tensor_tensor(rows["b1"][:, :], rows["b1"][:, :], rows["mean"][:, :], ALU.subtract))
                links.link(dve.tensor_tensor(rows["b1"][:, :], rows["b1"][:, :], bn_scale[:, :], ALU.mult))
                links.link(dve.tensor_tensor(bn_shift[:, :], rows["b1"][:, :], rows["beta"][:, :], ALU.add))
                links.link(dve.tensor_copy(b_hid_n[:, :], b_hh_col[:, 2 * KC:3 * KC]))
                links.link(dve.tensor_tensor(b_gate[:, 0:2 * KC], b_gate[:, 0:2 * KC], b_hh_col[:, 0:2 * KC], ALU.add))
                links.link(dve.tensor_scalar(b_gate[:, KC:2 * KC], b_gate[:, KC:2 * KC], -1.0, None, ALU.mult))
                for i, (_, to) in enumerate(turns_of):
                    dve.wait_ge(turned.handle, turned.at(i + 1))
                    dve.tensor_copy(to, bank[i % 4][:, 0:P]).then_inc(kept.handle, 1)
                dve.wait_ge(turned.handle, turned.at(len(turns_of) + 1))
                dve.tensor_copy(w_gat[:, HID:], bank[4][:, 0:2 * HEADS]).then_inc(kept.handle, 1)
                dve.wait_ge(kept.handle, kept.at(len(turns_of) + 1))

            @block.scalar
            def _(act):
                act.wait_ge(var_eps.handle, var_eps.at(1))
                act.activation(rows["var"][:, :], rows["var"][:, :], ACT.Sqrt).then_inc(var_root.handle, 1)


def sort_edges(nc, ctx, v):
    bank, ident, iota, ones, norm, records, tile_block, waits_passed = (
        v[k] for k in ("bank", "ident", "iota", "ones", "norm", "records", "tile_block", "waits_passed"))
    signal = v["signal"]
    keys = ("dst", "src")
    other = {"dst": "src", "src": "dst"}
    with ExitStack() as scope:
        def sb(name, shape, dt=F32):
            return v["sb"](name, shape, dt, scope)

        ends = {k: sb(f"ends_{k}", [P, EC], I32) for k in keys}
        weight = sb("weight", [P, EC])
        hi = {k: sb(f"hi_{k}", [P, EC]) for k in keys}
        lo = {k: sb(f"lo_{k}", [P, EC]) for k in keys}
        bits = sb("bits", [P, EC], I32)
        hot_hi = [sb(f"hot_hi{g}", [P, n, 100], BF16) for g, (_, n) in enumerate(SG)]
        pair_hi = [sb(f"pair_hi{g}", [P, n, 100], BF16) for g, (_, n) in enumerate(SG)]
        pair_lo = [sb(f"pair_lo{g}", [P, n, P], BF16) for g, (_, n) in enumerate(SG)]
        before = sb("before", [P, P])
        before_h = sb("before_h", [P, P], BF16)
        rest_h = sb("rest_h", [P, P], BF16)
        lane_i = sb("lane_i", [P, 1], I32)
        far = sb("far", [P, 1])
        tile_i = sb("tile_i", [P, KT], I32)
        tile_f = sb("tile_f", [P, KT])
        begun = sb("begun", [P, KT])
        block_row = sb("sorted_block_row", [1, KT], I32)
        count = sb("count", [P, P])
        total = sb("total", [P, 1])
        total_i = sb("total_i", [P, 1], I32)
        n_tiles = sb("n_tiles", [P, 1])
        first_tile = sb("first_tile", [P, 1])
        first_place = sb("first_place", [P, 1])
        place_diag = sb("place_diag", [P, NK])
        no_records = sb("no_records", [P, KT, RW], I32)

        zeroed = signal("zeroed")
        edges_in = signal("edges_in")
        index_set = signal("index_set")
        blank_set = signal("blank_set")
        blank_out = signal("blank_out")
        counted = signal("counted")
        hot_set = signal("hot_set")
        hot_used = signal("hot_used")
        pair_set = signal("pair_set")
        pair_used = signal("pair_used")
        chain = signal("chain_sort")
        turned = signal("sort_turned")
        begun_set = signal("begun_set")
        block_sum = signal("block_sum")
        block_kept = signal("block_kept")
        degree_in = signal("degree_in")
        degree_root = signal("degree_root")
        blocks_out = signal("blocks_out")
        consts = signal("sort_consts")

        CH = KT // 4

        def group_of(c):
            return (0, c) if c < SG[1][0] else (1, c - SG[1][0])

        def set_hot_pair(dve, k, t, first, g, c0, n):
            if not first:
                dve.wait_ge(pair_used.handle, pair_used.at(t * 2 + g - 1))
            cols = bass.ds(t * SU + c0, n)
            dve.tensor_tensor(pair_hi[g][:, :, :], hi[k][:, cols].unsqueeze(2).to_broadcast([P, n, 100]),
                              iota[:, 0:100].unsqueeze(1).to_broadcast([P, n, 100]), ALU.is_equal)
            dve.tensor_tensor(pair_lo[g][:, :, :], lo[k][:, cols].unsqueeze(2).to_broadcast([P, n, P]),
                              iota[:, :].unsqueeze(1).to_broadcast([P, n, P]), ALU.is_equal).then_inc(pair_set.handle, 1)

        def count_pairs(pe, b, t, first, g, n):
            pe.wait_ge(pair_set.handle, pair_set.at(t * 2 + g + 1))
            for j in range(n):
                ins = pe.matmul(bank[b][0:NK, 0:P], pair_hi[g][:, j, 0:NK], pair_lo[g][:, j, :],
                                start=first and g == 0 and j == 0, stop=True, skip_group_check=True)
            ins.then_inc(pair_used.handle, 1)

        with nc.Block() as block:
            @block.sync
            def _(sp):
                sp.wait_ge(zeroed.handle, zeroed.at(1))
                for to, of in ((ends["dst"], v["dst"]), (ends["src"], v["src"]), (weight, v["edge_weight"])):
                    sp.dma_start(to[0:P - 1, :], of[0:(P - 1) * EC].rearrange("(p c) -> p c", c=EC)).then_inc(edges_in.handle, 16)
                    sp.dma_start(to[P - 1:P, 0:EL], of[(P - 1) * EC:E].rearrange("(p c) -> p c", p=1)).then_inc(edges_in.handle, 16)
                sp.wait_ge(blank_set.handle, blank_set.at(1))
                for k in keys:
                    sp.dma_start(records[k].rearrange("(p c) w -> p c w", c=KT), no_records[:, :, :]).then_inc(blank_out.handle, 16)
                sp.wait_ge(blank_out.handle, blank_out.at(32))

            @block.gpsimd
            def _(pool):
                pool.memset(before[:, :], 0.0).then_inc(consts.handle, 1)
                pool.wait_ge(consts.handle, consts.at(1))
                pool.affine_select(out=before[:, :], in_=before[:, :], compare_op=ALU.is_ge, fill=1.0, base=0,
                                   pattern=[[-1, P]], channel_multiplier=1).then_inc(index_set.handle, 1)
                pool.iota(lane_i[:, :], pattern=[[0, 1]], base=0, channel_multiplier=1).then_inc(index_set.handle, 1)
                pool.iota(tile_i[:, :], pattern=[[1, KT]], base=0, channel_multiplier=0).then_inc(index_set.handle, 1)

            @block.vector
            def _(dve):
                for k in keys:
                    dve.memset(ends[k][:, :], NO_EDGE)
                dve.memset(weight[:, :], 0.0).then_inc(zeroed.handle, 1)
                links = Chain(dve, chain, 3 + 8)
                links.turn(0)
                links.link(dve.memset(no_records[:, :, :], 0))
                dve.memset(no_records[:, :, 1:2].bitcast(F32), NO_LANE).then_inc(blank_set.handle, 1)
                dve.wait_ge(index_set.handle, index_set.at(3))
                dve.tensor_copy(before_h[:, :], before[:, :])
                dve.tensor_scalar(rest_h[:, :], before[:, :], -1.0, 1.0, ALU.mult, ALU.add)
                dve.tensor_copy(tile_f[:, :], tile_i[:, :])
                links.link(dve.tensor_copy(far[:, :], lane_i[:, :]))
                links.link(dve.tensor_scalar(far[:, :], far[:, :], float(NB), FAR, ALU.is_ge, ALU.mult))
                dve.wait_ge(edges_in.handle, edges_in.at(96))
                for k in keys:
                    links.link(dve.tensor_scalar(bits[:, :], ends[k][:, :], 7, None, ALU.logical_shift_right))
                    links.link(dve.tensor_copy(hi[k][:, :], bits[:, :]))
                    links.link(dve.tensor_scalar(bits[:, :], ends[k][:, :], 127, None, ALU.bitwise_and))
                    links.link(dve.tensor_copy(lo[k][:, :], bits[:, :]))

                def body(t, first):
                    for g, (c0, n) in enumerate(SG):
                        set_hot_pair(dve, "dst", t, first, g, c0, n)

                turns(dve, ST, body)

            @block.tensor
            def _(pe):
                def body(t, first):
                    for g, (_, n) in enumerate(SG):
                        count_pairs(pe, keys.index("dst"), t, first, g, n)

                turns(pe, ST, body)
        chain.phase_over(3 + 8)
        pair_set.phase_over(2 * ST)
        pair_used.phase_over(2 * ST)

        def use_counts(k):
            b = keys.index(k)
            with nc.Block() as block:
                @block.vector
                def _(dve):
                    links = Chain(dve, chain, 9)
                    links.turn(0)
                    links.link(dve.tensor_copy(count[0:NK, :], bank[b][0:NK, 0:P]))
                    links.link(dve.tensor_reduce(total[0:NK, :], count[0:NK, :], AX.X, ALU.add))
                    links.link(dve.tensor_scalar(total[0:NK, :], total[0:NK, :], float(P - 1), None, ALU.add))
                    links.link(dve.tensor_copy(total_i[0:NK, :], total[0:NK, :]))
                    links.link(dve.tensor_scalar(total_i[0:NK, :], total_i[0:NK, :], 7, None, ALU.logical_shift_right))
                    dve.tensor_copy(n_tiles[0:NK, :], total_i[0:NK, :]).then_inc(counted.handle, 1)
                    dve.wait_ge(turned.handle, turned.at(1))
                    dve.tensor_scalar(norm[k][:, :], bank[2][:, 0:NB], 1.0, 1.0, ALU.add, ALU.max).then_inc(degree_in.handle, 1)
                    links.link(dve.tensor_copy(first_tile[0:NK, :], bank[3][0:NK, 0:1]))
                    links.link(dve.tensor_scalar(first_place[0:NK, :], first_tile[0:NK, :], float(P), None, ALU.mult))
                    dve.tensor_scalar(begun[0:NB, :], tile_f[0:NB, :], first_tile[0:NB, :], None, ALU.is_ge).then_inc(begun_set.handle, 1)
                    links.link(dve.tensor_tensor(first_place[0:NK, :], first_place[0:NK, :], far[0:NK, :], ALU.add))
                    links.link(dve.tensor_scalar(place_diag[0:NK, :], ident[0:NK, 0:NK], first_place[0:NK, :], None, ALU.mult))
                    dve.wait_ge(block_sum.handle, block_sum.at(1))
                    for q in range(4):
                        ins = dve.tensor_scalar(block_row[:, q * CH:(q + 1) * CH], bank[4 + q][0:1, 0:CH], -1.0, None, ALU.add)
                    ins.then_inc(block_kept.handle, 1)
                    dve.wait_ge(degree_root.handle, degree_root.at(1))
                    dve.reciprocal(norm[k][:, :], norm[k][:, :])

                @block.tensor
                def _(pe):
                    pe.wait_ge(counted.handle, counted.at(1))
                    pe.transpose(bank[2][:, 0:NB], count[0:NB, :], ident[0:NB, 0:NB])
                    pe.matmul(bank[3][0:NK, 0:1], before[0:NK, 0:NK], n_tiles[0:NK, :], start=True, stop=True).then_inc(turned.handle, 1)
                    pe.wait_ge(begun_set.handle, begun_set.at(1))
                    for q in range(4):
                        ins = pe.matmul(bank[4 + q][0:1, 0:CH], ones[0:NB, 0:1], begun[0:NB, q * CH:(q + 1) * CH], start=True, stop=True)
                    ins.then_inc(block_sum.handle, 1)

                @block.scalar
                def _(act):
                    act.wait_ge(degree_in.handle, degree_in.at(1))
                    act.activation(norm[k][:, :], norm[k][:, :], ACT.Sqrt).then_inc(degree_root.handle, 1)

                @block.sync
                def _(sp):
                    sp.wait_ge(block_kept.handle, block_kept.at(1))
                    sp.dma_start(tile_block[k], block_row[:, :]).then_inc(blocks_out.handle, 16)
                    sp.wait_ge(blocks_out.handle, blocks_out.at(16))
            chain.phase_over(9)
            blocks_out.phase_over(16)
            for s in (counted, turned, degree_in, begun_set, block_sum, block_kept, degree_root):
                s.phase_over(1)

        with ExitStack() as inner:
            place = [v["sb"](f"place{g}", [P, n], F32, inner) for g, (_, n) in enumerate(SG)]
            place_i = [v["sb"](f"place_i{g}", [P, n], I32, inner) for g, (_, n) in enumerate(SG)]
            tile_of = [v["sb"](f"tile_of{g}", [P, n], I32, inner) for g, (_, n) in enumerate(SG)]
            row_to = [v["sb"](f"row_to{g}", [P, n], I32, inner) for g, (_, n) in enumerate(SG)]
            record = [v["sb"](f"record{g}", [P, n, RW], I32, inner) for g, (_, n) in enumerate(SG)]
            ranked = v["sb"]("ranked", [P, NK], F32, inner)
            record_clear = signal("record_clear")
            prefix_set = signal("prefix_set")
            place_read = signal("place_read")
            rows_set = signal("rows_set")
            record_set = signal("record_set")
            scattered = [signal(f"scattered{g}") for g in range(2)]
            prefix = bank[0][:, 0:NK]

            for k in keys:
                use_counts(k)
                with nc.Block() as block:
                    @block.tensor
                    def _(pe):
                        pe.matmul(prefix, ones[0:NK, :], place_diag[0:NK, :], start=True, stop=True, skip_group_check=True)

                        def count_column(t, c, first):
                            g, j = group_of(c % SU)
                            pe.wait_ge(pair_set.handle, pair_set.at(t * SU + c + 1))
                            pe.matmul(bank[1][0:NK, 0:P], pair_hi[g][:, j, 0:NK], pair_lo[g][:, j, :], start=first and c == 0,
                                      stop=True, skip_group_check=True)

                        def body(t, first):
                            for g, (c0, n) in enumerate(SG):
                                pe.wait_ge(hot_set.handle, hot_set.at(t * 2 + g + 1))
                                for j in range(n):
                                    pe.matmul(prefix, before_h[:, :], hot_hi[g][:, j, 0:NK], start=False, stop=True,
                                              skip_group_check=True).then_inc(prefix_set.handle, 1)
                                    if k == "dst" and not (first and c0 + j < PAIR_LAG):
                                        count_column(t, c0 + j - PAIR_LAG, first)
                                    pe.wait_ge(place_read.handle, place_read.at(t * SU + c0 + j + 1))
                                    ins = pe.matmul(prefix, rest_h[:, :], hot_hi[g][:, j, 0:NK], start=False, stop=True,
                                                    skip_group_check=True)
                                ins.then_inc(hot_used.handle, 1)

                        turns(pe, ST, body)
                        if k == "dst":
                            for c in range(PAIR_LAG):
                                count_column(ST, c - PAIR_LAG, False)

                    @block.vector
                    def _(dve):
                        links = Chain(dve, chain, 4)

                        def body(t, first):
                            links.turn(t)
                            for g, (c0, n) in enumerate(SG):
                                if not first:
                                    dve.wait_ge(hot_used.handle, hot_used.at(t * 2 + g - 1))
                                dve.tensor_tensor(hot_hi[g][:, :, :],
                                                  hi[k][:, bass.ds(t * SU + c0, n)].unsqueeze(2).to_broadcast([P, n, 100]),
                                                  iota[:, 0:100].unsqueeze(1).to_broadcast([P, n, 100]),
                                                  ALU.is_equal).then_inc(hot_set.handle, 1)
                            for g, (c0, n) in enumerate(SG):
                                for j in range(n):
                                    dve.wait_ge(prefix_set.handle, prefix_set.at(t * SU + c0 + j + 1))
                                    dve.tensor_tensor_reduce(ranked[:, :], prefix, hot_hi[g][:, j, 0:NK], 1.0, 0.0, ALU.mult,
                                                             ALU.add, place[g][:, j:j + 1]).then_inc(place_read.handle, 1)
                                    if k == "dst":
                                        src_col = bass.ds(t * SU + c0 + j, 1)
                                        dve.tensor_tensor(pair_hi[g][:, j:j + 1, :], hi["src"][:, src_col].unsqueeze(2).to_broadcast([P, 1, 100]),
                                                          iota[:, 0:100].unsqueeze(1), ALU.is_equal)
                                        dve.tensor_tensor(pair_lo[g][:, j:j + 1, :], lo["src"][:, src_col].unsqueeze(2).to_broadcast([P, 1, P]),
                                                          iota[:, :].unsqueeze(1), ALU.is_equal).then_inc(pair_set.handle, 1)
                                dve.wait_ge(place_read.handle, place_read.at(t * SU + c0 + n))
                                links.link(dve.tensor_copy(place_i[g][:, :], place[g][:, :]))
                                dve.tensor_scalar(tile_of[g][:, :], place_i[g][:, :], 7, None, ALU.logical_shift_right)
                                links.link(dve.tensor_scalar(place_i[g][:, :], place_i[g][:, :], 127, None, ALU.bitwise_and))
                                if not first:
                                    dve.wait_ge(scattered[g].handle, scattered[g].at(t * (16 * n)))
                                dve.scalar_tensor_tensor(out=row_to[g][:, :], in0=place_i[g][:, :], scalar=float(KT),
                                                         in1=tile_of[g][:, :], op0=ALU.mult, op1=ALU.add).then_inc(rows_set.handle, 1)

                        turns(dve, ST, body)

                    @block.scalar
                    def _(act):
                        act.wait_ge(record_clear.handle, record_clear.at(2))

                        def body(t, first):
                            for g, (c0, n) in enumerate(SG):
                                if not first:
                                    act.wait_ge(scattered[g].handle, scattered[g].at(t * (16 * n)))
                                cols = bass.ds(t * SU + c0, n)
                                act.copy(record[g][:, :, 0:1], ends[other[k]][:, cols].unsqueeze(2))
                                act.copy(record[g][:, :, 1:2].bitcast(F32), lo[k][:, cols].unsqueeze(2))
                                act.copy(record[g][:, :, 2:3].bitcast(F32), weight[:, cols].unsqueeze(2)).then_inc(record_set.handle, 1)

                        turns(act, ST, body)

                    @block.gpsimd
                    def _(pool):
                        if k == keys[0]:
                            for g in range(2):
                                pool.memset(record[g][:, :, :], 0).then_inc(record_clear.handle, 1)

                        def body(t, first):
                            for g, (_, n) in enumerate(SG):
                                pool.wait_ge(rows_set.handle, rows_set.at(t * 2 + g + 1))
                                pool.wait_ge(record_set.handle, record_set.at(t * 2 + g + 1))
                                pool.sem_inc(waits_passed.handle, 1)
                                for j in range(n):
                                    pool.indirect_dma_start(
                                        out=records[k], out_offset=bass.IndirectOffsetOnAxis(ap=row_to[g][:, j:j + 1], axis=0),
                                        in_=record[g][:, j, :], in_offset=None, bounds_check=P * KT - 1,
                                        oob_is_err=False).then_inc(scattered[g].handle, 16)

                        turns(pool, ST, body)
                        for g, (_, n) in enumerate(SG):
                            pool.wait_ge(scattered[g].handle, scattered[g].at(16 * n * ST))
                if k == "dst":
                    pair_set.phase_over(EC)
                hot_set.phase_over(2 * ST)
                hot_used.phase_over(2 * ST)
                prefix_set.phase_over(EC)
                place_read.phase_over(EC)
                rows_set.phase_over(2 * ST)
                record_set.phase_over(2 * ST)
                chain.phase_over(4 * ST)
                for g, (_, n) in enumerate(SG):
                    scattered[g].phase_over(16 * n * ST)


def layers(nc, ctx, v):
    bank, ident, iota, norm, records, tile_block, waits_passed = (
        v[k] for k in ("bank", "ident", "iota", "norm", "records", "tile_block", "waits_passed"))
    sb, signal = v["sb"], v["signal"]
    x_in, out = v["x"], v["out"]
    FULL = (NB - 1) * P

    nodes = sb("nodes", [P, NB, D])
    sums = sb("sums", [P, NB * W_GAT])
    sums_conv = sums[:, 0:NB * D].rearrange("p (b w) -> p b w", w=D)
    sums_msg = sums_conv
    sums_cos = sums[:, 0:NB * W_COS].rearrange("p (b w) -> p b w", w=W_COS)
    sums_gat = sums[:, :].rearrange("p (b w) -> p b w", w=W_GAT)
    unit = sums[:, NB * W_COS:NB * (W_COS + D)].rearrange("p (b w) -> p b w", w=D)
    target = sb("target", [P, NB, 2 * HEADS])
    stats = sb("stats", [P, NB, 6])
    mean = sb("mean", [P, NB])
    rstd = sb("rstd", [P, NB])
    spread = sb("spread", [P, NB])
    block_row = sb("block_row", [1, KT], I32)

    record_in = [signal(f"record_in{h}") for h in range(2)]
    gathered = [signal(f"gathered{s}") for s in range(U)]
    hot_set = signal("walk_hot_set")
    product = signal("product")
    added = signal("added")
    hot_turned = signal("hot_turned")
    hot_kept = signal("hot_kept")
    target_set = signal("target_set")
    logit_set = signal("logit_set")
    exp_set = signal("exp_set")
    weighted = signal("weighted")
    weighted_act = signal("weighted_act")
    blocks_in = signal("blocks_in")
    chain = signal("chain_layers")
    block_staged = signal("block_staged")
    block_product = signal("block_product")
    block_rows = signal("block_rows")
    block_turned = signal("block_turned")
    turned_kept = signal("turned_kept")
    stored = [signal(f"stored{j}") for j in range(2)]
    root_in = signal("root_in")
    root_set = signal("root_set")
    x_loaded = signal("x_loaded")

    def walk(name, key, rows, width, kind):
        looks_up = kind in ("cos", "gat")
        banks = range(4, 8) if looks_up else range(8)
        with ExitStack() as scope:
            record = [sb(f"{name}_record{h}", [P, HU, RW], I32, scope) for h in range(2)]
            got = sb(f"{name}_got", [P, U, width], F32, scope)
            hot = sb(f"{name}_hot", [P, U, P], F32, scope)
            if looks_up:
                hotT = sb(f"{name}_hotT", [P, 8, P], F32, scope)
            if kind == "cos":
                hot_w = sb(f"{name}_hot_w", [P, 4, P], F32, scope)
                scratch = sb(f"{name}_scratch", [P, 4, D], F32, scope)
                cos = sb(f"{name}_cos", [P, U], F32, scope)
                exps = sb(f"{name}_exps", [P, U], F32, scope)
            if kind == "gat":
                logit = sb(f"{name}_logit", [P, 2, 4, HEADS], F32, scope)
                leaky = sb(f"{name}_leaky", [P, 2, 4, HEADS], F32, scope)
            acc = {"conv": sums_conv, "msg": sums_msg, "cos": sums_cos, "gat": sums_gat}[kind]
            list_v = records[key].rearrange("(p c) w -> p c w", c=KT)

            def word(s, n):
                return record[s // HU][:, s % HU, n:n + 1].bitcast(F32)

            def staged_turns(eng, stages):
                def body(t, first):
                    for i in range(U):
                        for stage, lag in stages:
                            if not (first and i < lag):
                                stage(t, i - lag, first)

                turns(eng, T, body)
                for i in range(max(lag for _, lag in stages)):
                    for stage, lag in stages:
                        if i < lag:
                            stage(T, i - lag, False)

            def block_of(eng, regs, t, c):
                if c % HU == 0:
                    eng.load(regs, block_row[0:1, bass.ds(t * U + c, HU)])
                return eng.snap(regs[c % HU], min_val=0, max_val=NB - 1)

            with nc.Block() as block:
                @block.sync
                def _(sp):
                    sp.dma_start(block_row[:, :], tile_block[key]).then_inc(blocks_in.handle, 16)

                    def body(t, first):
                        for h in range(2):
                            if not first:
                                sp.wait_ge(hot_set.handle, hot_set.at(t * U + (h + 1) * HU - U))
                                sp.sem_inc(waits_passed.handle, 1)
                                for s in range(h * HU, (h + 1) * HU):
                                    sp.wait_ge(gathered[s].handle, gathered[s].at(t * 16))
                                sp.sem_inc(waits_passed.handle, 1)
                            sp.dma_start(record[h][:, :, :], list_v[:, bass.ds(t * U + h * HU, HU), :]).then_inc(record_in[h].handle, 16)

                    turns(sp, T, body)

                @block.gpsimd
                def _(pool):
                    def body(t, first):
                        for s in range(U):
                            if s % HU == 0:
                                pool.wait_ge(record_in[s // HU].handle, record_in[s // HU].at(t * 16 + 16))
                            if s % 4 == 0 and not first:
                                pool.wait_ge(product.handle, product.at(t * U + s + 4 - U))
                                pool.sem_inc(waits_passed.handle, 1)
                            pool.indirect_dma_start(
                                out=got[:, s, :], out_offset=None, in_=rows,
                                in_offset=bass.IndirectOffsetOnAxis(ap=record[s // HU][:, s % HU, 0:1], axis=0),
                                bounds_check=N - 1, oob_is_err=False).then_inc(gathered[s].handle, 16)

                    turns(pool, T, body)

                @block.tensor
                def _(pe):
                    if looks_up:
                        regs = [pe.alloc_register(f"{name}_pe_block{j}") for j in range(HU)]
                        pe.wait_ge(blocks_in.handle, blocks_in.at(16))

                    def turn_hot(t, c, first):
                        s = c % U
                        pe.wait_ge(hot_set.handle, hot_set.at(t * U + c + 1))
                        if kind == "cos" and not (first and s < 2):
                            pe.wait_ge(hot_kept.handle, hot_kept.at(t * U + c - 1))
                        pe.transpose(bank[s % 2][:, 0:P], hot[:, s, :], ident[:, :]).then_inc(hot_turned.handle, 1)

                    def look_up(t, c, first):
                        s = c % U
                        b = block_of(pe, regs, t, c)
                        pe.wait_ge(hot_kept.handle, hot_kept.at(t * U + c + 1))
                        if kind == "cos":
                            if not (first and s < 2):
                                pe.wait_ge(logit_set.handle, logit_set.at(t * U + c - 1))
                            pe.matmul(bank[2 + s % 2][:, 0:D], hotT[:, s % 8, :], unit[:, bass.ds(b, 1), :],
                                      start=True, stop=True).then_inc(target_set.handle, 1)
                        else:
                            q = s // 4
                            if s % 4 == 0 and not (first and q < 2):
                                pe.wait_ge(logit_set.handle, logit_set.at(t * 4 + c // 4 - 1))
                            pe.matmul(bank[2 + q % 2][:, s % 4 * 8:s % 4 * 8 + 8], hotT[:, s % 8, :],
                                      target[:, bass.ds(b, 1), :], start=True, stop=True).then_inc(target_set.handle, 1)

                    def multiply(t, c, first):
                        s = c % U
                        if kind in ("conv", "msg"):
                            pe.wait_ge(hot_set.handle, hot_set.at(t * U + c + 1))
                            pe.wait_ge(gathered[s].handle, gathered[s].at(t * 16 + (c // U + 1) * 16))
                        else:
                            pe.wait_ge(weighted.handle, weighted.at(t * U + c + 1))
                        if kind == "gat":
                            pe.wait_ge(weighted_act.handle, weighted_act.at(t * U + c + 1))
                        left, right = {"conv": (got[:, s, :], hot[:, s, :]), "msg": (hot[:, s, :], got[:, s, :]),
                                       "cos": (hot_w[:, s % 4, :] if kind == "cos" else None, got[:, s, :]),
                                       "gat": (hot[:, s, :], got[:, s, :])}[kind]
                        pe.matmul(bank[banks[s % len(banks)]][:, 0:right.shape[-1]], left, right, start=True,
                                  stop=True).then_inc(product.handle, 1)

                    staged_turns(pe, {"conv": [(multiply, 0)], "msg": [(multiply, 0)],
                                      "cos": [(turn_hot, 0), (look_up, 3), (multiply, 8)],
                                      "gat": [(look_up, 2), (turn_hot, 0), (multiply, 9)]}[kind])

                @block.vector
                def _(dve):
                    regs = [dve.alloc_register(f"{name}_dve_block{j}") for j in range(HU)]
                    dve.wait_ge(blocks_in.handle, blocks_in.at(16))

                    def set_hot(t, c, first):
                        s = c % U
                        if s % HU == 0:
                            dve.wait_ge(record_in[s // HU].handle, record_in[s // HU].at(t * 16 + (c // U + 1) * 16))
                        if kind == "msg":
                            ins = dve.tensor_scalar(hot[:, s, :], iota[:, :], word(s, 1), word(s, 2), ALU.is_equal, ALU.mult)
                        else:
                            ins = dve.tensor_scalar(hot[:, s, :], iota[:, :], word(s, 1), None, ALU.is_equal)
                        ins.then_inc(hot_set.handle, 1)

                    def score(t, c, first):
                        s = c % U
                        dve.wait_ge(target_set.handle, target_set.at(t * U + c + 1))
                        dve.wait_ge(gathered[s].handle, gathered[s].at(t * 16 + (c // U + 1) * 16))
                        dve.tensor_tensor_reduce(scratch[:, s % 4, :], bank[2 + s % 2][:, 0:D], got[:, s, 0:D], 1.0, 0.0,
                                                 ALU.mult, ALU.add, cos[:, s:s + 1]).then_inc(logit_set.handle, 1)

                    def weigh_hot(t, c, first):
                        s = c % U
                        dve.wait_ge(exp_set.handle, exp_set.at(t * U + c + 1))
                        dve.tensor_scalar(hot_w[:, s % 4, :], hot[:, s, :], exps[:, s:s + 1], None,
                                          ALU.mult).then_inc(weighted.handle, 1)

                    def logits(t, c, first):
                        s = c % U
                        """leaky(el + er) - shift, for four tiles at once."""
                        if s % 4 != 3:
                            return
                        q = s // 4
                        dve.wait_ge(target_set.handle, target_set.at(t * U + c + 1))
                        for i in range(4):
                            dve.wait_ge(gathered[4 * q + i].handle, gathered[4 * q + i].at(t * 16 + (c // U + 1) * 16))
                        here = bank[2 + q % 2][:, 0:32].rearrange("p (i c) -> p i c", c=8)
                        a, b = logit[:, q % 2, :, :], leaky[:, q % 2, :, :]
                        dve.tensor_tensor(a, here[:, :, HEADS:], got[:, 4 * q:4 * q + 4, HID:], ALU.add).then_inc(chain.handle, 1)
                        dve.wait_ge(chain.handle, chain.at(t * 8 + c // 4 * 2 + 1))
                        dve.scalar_tensor_tensor(out=b, in0=a, scalar=0.2, in1=a, op0=ALU.mult, op1=ALU.max).then_inc(chain.handle, 1)
                        dve.wait_ge(chain.handle, chain.at(t * 8 + c // 4 * 2 + 2))
                        dve.tensor_tensor(a, b, here[:, :, 0:HEADS], ALU.subtract).then_inc(logit_set.handle, 1)

                    def weigh_rows(t, c, first):
                        s = c % U
                        dve.wait_ge(exp_set.handle, exp_set.at(t * 4 + c // 4 + 1))
                        feat = got[:, s, 0:VH * DH].rearrange("p (h d) -> p h d", h=VH)
                        dve.tensor_tensor(feat, feat, got[:, s, HID:HID + VH].unsqueeze(2).to_broadcast([P, VH, DH]),
                                          ALU.mult).then_inc(weighted.handle, 1)

                    def add(t, c, first):
                        s = c % U
                        b = block_of(dve, regs, t, c)
                        place = acc[:, bass.ds(b, 1), :]
                        dve.wait_ge(product.handle, product.at(t * U + c + 1))
                        if not (first and s == 0):
                            dve.wait_ge(added.handle, added.at(t * U + c))
                        dve.tensor_tensor(place, place, bank[banks[s % len(banks)]][:, 0:place.shape[-1]].unsqueeze(1),
                                          ALU.add).then_inc(added.handle, 1)

                    staged_turns(dve, {"conv": [(set_hot, 0), (add, 3)], "msg": [(set_hot, 0), (add, 3)],
                                       "cos": [(set_hot, 0), (score, 5), (weigh_hot, 7), (add, 9)],
                                       "gat": [(set_hot, 0), (logits, 4), (weigh_rows, 8), (add, 10)]}[kind])

                if looks_up:
                    @block.scalar
                    def _(act):
                        def keep_hot(t, c, first):
                            s = c % U
                            act.wait_ge(hot_turned.handle, hot_turned.at(t * U + c + 1))
                            act.copy(hotT[:, s % 8, :], bank[s % 2][:, 0:P]).then_inc(hot_kept.handle, 1)

                        def exp_cos(t, c, first):
                            s = c % U
                            act.wait_ge(logit_set.handle, logit_set.at(t * U + c + 1))
                            act.activation(exps[:, s:s + 1], cos[:, s:s + 1], ACT.Exp,
                                           scale=got[:, s, D:D + 1]).then_inc(exp_set.handle, 1)

                        def exp_gat(t, c, first):
                            s = c % U
                            if s % 4 == 3:
                                q = s // 4
                                act.wait_ge(logit_set.handle, logit_set.at(t * 4 + c // 4 + 1))
                                act.activation(got[:, 4 * q:4 * q + 4, HID:], logit[:, q % 2, :, :],
                                               ACT.Exp).then_inc(exp_set.handle, 1)

                        def weigh_heads(t, c, first):
                            s = c % U
                            """The heads that VectorE leaves."""
                            act.wait_ge(exp_set.handle, exp_set.at(t * 4 + c // 4 + 1))
                            for h in range(VH, HEADS):
                                feat = got[:, s, h * DH:(h + 1) * DH]
                                ins = act.activation(feat, feat, ACT.Copy, scale=got[:, s, HID + h:HID + h + 1])
                            ins.then_inc(weighted_act.handle, 1)

                        staged_turns(act, {"cos": [(exp_cos, 6), (keep_hot, 0)],
                                           "gat": [(keep_hot, 0), (exp_gat, 4), (weigh_heads, 8)]}[kind])
        for s in record_in:
            s.phase_over(16 * T)
        for s in gathered:
            s.phase_over(16 * T)
        blocks_in.phase_over(16)
        hot_set.phase_over(KT)
        product.phase_over(KT)
        added.phase_over(KT)
        if looks_up:
            hot_turned.phase_over(KT)
            hot_kept.phase_over(KT)
            target_set.phase_over(KT)
            weighted.phase_over(KT)
            for s in (logit_set, exp_set):
                s.phase_over(KT if kind == "cos" else KT // 4)
        if kind == "gat":
            chain.phase_over(KT // 2)

    def normalise_scales():
        with nc.Block() as block:
            @block.vector
            def _(dve):
                links = Chain(dve, chain, 6)
                links.turn(0)
                dve.tensor_tensor(mean[:, :], stats[:, :, 1], stats[:, :, 4], ALU.add)
                dve.tensor_tensor(rstd[:, :], stats[:, :, 1], stats[:, :, 4], ALU.subtract)
                links.link(dve.tensor_tensor(spread[:, :], stats[:, :, 2], stats[:, :, 5], ALU.add))
                links.link(dve.tensor_scalar(mean[:, :], mean[:, :], 0.5, None, ALU.mult))
                links.link(dve.scalar_tensor_tensor(out=rstd[:, :], in0=rstd[:, :], scalar=0.25, in1=rstd[:, :], op0=ALU.mult, op1=ALU.mult))
                links.link(dve.scalar_tensor_tensor(out=spread[:, :], in0=spread[:, :], scalar=1.0 / D, in1=rstd[:, :], op0=ALU.mult, op1=ALU.add))
                dve.tensor_scalar(spread[:, :], spread[:, :], EPS_LN, None, ALU.add).then_inc(root_in.handle, 1)
                dve.wait_ge(root_set.handle, root_set.at(1))
                links.link(dve.reciprocal(rstd[:, :], rstd[:, :]))

            @block.scalar
            def _(act):
                act.wait_ge(root_in.handle, root_in.at(1))
                act.activation(rstd[:, :], spread[:, :], ACT.Sqrt).then_inc(root_set.handle, 1)
        root_in.phase_over(1)
        root_set.phase_over(1)
        chain.phase_over(5)

    rows_out = staged = work = square = None

    def over_nodes(name, loop, *args):
        nonlocal rows_out, staged, work, square
        with ExitStack() as scope:
            rows_out = [sb(f"{name}_rows{j}", [P, W_GAT], F32, scope) for j in range(2)]
            staged = [sb(f"{name}_staged{j}", [P, KC * P], F32, scope) for j in range(2)]
            work = [sb(f"{name}_work{j}", [P, HID], F32, scope) for j in range(2)]
            square = [sb(f"{name}_square{j}", [P, 4], F32, scope) for j in range(2)]
            loop(*args)

    def blk(a, b):
        return a[:, bass.ds(b, 1), :].rearrange("p a w -> p (a w)")

    def col(a, b):
        return a[:, bass.ds(b, 1)]

    def store_rows(sp, table, width, t, first):
        for j in range(2):
            sp.wait_ge(block_rows.handle, block_rows.at(t * 2 + j + 1))
            sp.dma_start(table[bass.ds((t * 2 + j) * P, P), :], rows_out[j][:, 0:width]).then_inc(stored[j].handle, 16)

    def all_stored(sp):
        for j in range(2):
            sp.wait_ge(stored[j].handle, stored[j].at(16 * NT))

    def load_x():
        with nc.Block() as block:
            @block.gpsimd
            def _(pool):
                pool.memset(nodes[:, NB - 1, :], 0.0).then_inc(root_in.handle, 1)

            @block.sync
            def _(sp):
                sp.wait_ge(root_in.handle, root_in.at(1))
                sp.dma_start(nodes[:, 0:NB - 1, :], x_in[0:FULL, :].rearrange("(b p) d -> p b d", p=P)).then_inc(x_loaded.handle, 16)
                sp.dma_start(nodes[0:LAST, NB - 1, :], x_in[FULL:N, :]).then_inc(x_loaded.handle, 16)
                sp.wait_ge(x_loaded.handle, x_loaded.at(32))
        root_in.phase_over(1)

    def conv_rows_loop(between):
        table = v["rows_conv"][int(between)]
        per = 4 if between else 0
        with nc.Block() as block:
            @block.scalar
            def _(act):
                def body(t, first):
                    if between:
                        for j in range(2):
                            if not first:
                                act.wait_ge(block_product.handle, block_product.at(t * 2 + j - 1))
                                act.sem_inc(waits_passed.handle, 1)
                            act.copy(staged[j][:, 0:P], blk(sums_conv, t * 2 + j)).then_inc(block_staged.handle, 1)
                    for j in range(2):
                        act.wait_ge(block_turned.handle, block_turned.at(t * 2 + j + 1))
                        act.sem_inc(waits_passed.handle, 1)
                        act.copy(blk(sums_conv, t * 2 + j), bank[2 + j][:, 0:P]).then_inc(turned_kept.handle, 1)

                turns(act, NT, body)

            @block.tensor
            def _(pe):
                def body(t, first):
                    if between:
                        for j in range(2):
                            pe.wait_ge(block_staged.handle, block_staged.at(t * 2 + j + 1))
                            if not first:
                                pe.wait_ge(block_rows.handle, block_rows.at(t * 2 + j - 1))
                            pe.matmul(bank[j][:, 0:D], staged[j][:, 0:P], v["w1"][:, :], start=True, stop=True).then_inc(block_product.handle, 1)
                    for j in range(2):
                        pe.wait_ge(block_rows.handle, block_rows.at(t * 2 + j + 1))
                        if not first:
                            pe.wait_ge(turned_kept.handle, turned_kept.at(t * 2 + j - 1))
                        pe.transpose(bank[2 + j][:, 0:P], rows_out[j][:, 0:D], ident[:, :]).then_inc(block_turned.handle, 1)

                turns(pe, NT, body)

            @block.vector
            def _(dve):
                links = Chain(dve, chain, 2 * per)

                def body(t, first):
                    links.turn(t)
                    for j in range(2):
                        b = t * 2 + j
                        rows = rows_out[j][:, 0:D]
                        if between:
                            w = work[j][:, 0:D]
                            dve.wait_ge(block_product.handle, block_product.at(t * 2 + j + 1))
                            links.link(dve.tensor_scalar(w, bank[j][:, 0:D], col(norm["dst"], b), None, ALU.mult))
                            links.link(dve.tensor_tensor(w, w, v["bn_scale"][:, :], ALU.mult))
                            links.link(dve.tensor_tensor(w, w, v["bn_shift"][:, :], ALU.add))
                            links.link(dve.scalar_tensor_tensor(out=w, in0=w, scalar=0.01, in1=w, op0=ALU.mult, op1=ALU.max))
                        else:
                            w = blk(nodes, b)
                        if not first:
                            dve.wait_ge(stored[j].handle, stored[j].at(t * 16))
                            dve.wait_ge(block_turned.handle, block_turned.at(t * 2 + j - 1))
                        dve.tensor_scalar(rows, w, col(norm["src"], b), None, ALU.mult).then_inc(block_rows.handle, 1)

                turns(dve, NT, body)

            @block.sync
            def _(sp):
                turns(sp, NT, lambda t, first: store_rows(sp, table, D, t, first))
                all_stored(sp)
        if between:
            block_staged.phase_over(NB)
            block_product.phase_over(NB)
        block_rows.phase_over(NB)
        block_turned.phase_over(NB)
        turned_kept.phase_over(NB)
        chain.phase_over(NT * 2 * per)
        for j in range(2):
            stored[j].phase_over(16 * NT)

    def conv_out_loop():
        with nc.Block() as block:
            @block.scalar
            def _(act):
                def body(t, first):
                    for j in range(2):
                        if not first:
                            act.wait_ge(block_product.handle, block_product.at(t * 2 + j - 1))
                            act.sem_inc(waits_passed.handle, 1)
                        act.copy(staged[j][:, 0:P], blk(sums_conv, t * 2 + j)).then_inc(block_staged.handle, 1)

                turns(act, NT, body)

            @block.tensor
            def _(pe):
                def body(t, first):
                    for j in range(2):
                        pe.wait_ge(block_staged.handle, block_staged.at(t * 2 + j + 1))
                        if not first:
                            pe.wait_ge(block_rows.handle, block_rows.at(t * 2 + j - 1))
                        pe.matmul(bank[j][:, 0:D], staged[j][:, 0:P], v["w2"][:, :], start=True, stop=True).then_inc(block_product.handle, 1)

                turns(pe, NT, body)

            @block.vector
            def _(dve):
                links = Chain(dve, chain, 2)

                def body(t, first):
                    links.turn(t)
                    for j in range(2):
                        b = t * 2 + j
                        dve.wait_ge(block_product.handle, block_product.at(t * 2 + j + 1))
                        dve.scalar_tensor_tensor(out=work[j][:, 0:D], in0=bank[j][:, 0:D], scalar=col(norm["dst"], b),
                                                 in1=v["b2_row"][:, :], op0=ALU.mult, op1=ALU.add).then_inc(block_rows.handle, 1)
                        dve.wait_ge(block_rows.handle, block_rows.at(t * 2 + j + 1))
                        links.link(dve.tensor_tensor(blk(nodes, b), blk(nodes, b), work[j][:, 0:D], ALU.add))
                        dve.bn_stats(blk(stats, b), blk(nodes, b))

                turns(dve, NT, body)
        block_staged.phase_over(NB)
        block_product.phase_over(NB)
        block_rows.phase_over(NB)
        chain.phase_over(NT * 2)

    def table_loop(kind):
        table, width, weights = {"msg": (v["rows_msg"], D, v["w_msgT"]), "cos": (v["rows_cos"], W_COS, v["w_cos"]),
                                 "gat": (v["rows_gat"], W_GAT, v["w_gat"])}[kind]
        cols = weights.shape[-1]
        per = {"msg": 0, "cos": 4, "gat": 0}[kind]
        with nc.Block() as block:
            @block.tensor
            def _(pe):
                def body(t, first):
                    for j in range(2):
                        pe.wait_ge(block_staged.handle, block_staged.at(t * 2 + j + 1))
                        if not first:
                            pe.wait_ge(turned_kept.handle, turned_kept.at(t * 2 + j - 1))
                        pe.transpose(bank[2 + j][:, 0:P], staged[j][:, P:2 * P], ident[:, :]).then_inc(block_turned.handle, 1)
                    for j in range(2):
                        pe.wait_ge(turned_kept.handle, turned_kept.at(t * 2 + j + 1))
                        if not first:
                            pe.wait_ge(block_rows.handle, block_rows.at(t * 2 + j - 1))
                        pe.matmul(bank[j][:, 0:cols], staged[j][:, 0:P], weights[:, :], start=True, stop=True).then_inc(block_product.handle, 1)

                turns(pe, NT, body)

            @block.scalar
            def _(act):
                def body(t, first):
                    for j in range(2):
                        act.wait_ge(block_turned.handle, block_turned.at(t * 2 + j + 1))
                        if not first:
                            act.wait_ge(block_product.handle, block_product.at(t * 2 + j - 1))
                        act.copy(staged[j][:, 0:P], bank[2 + j][:, 0:P]).then_inc(turned_kept.handle, 1)
                    if kind == "cos":
                        for j in range(2):
                            act.wait_ge(root_in.handle, root_in.at(t * 2 + j + 1))
                            act.activation(square[j][:, 1:2], square[j][:, 0:1], ACT.Sqrt).then_inc(root_set.handle, 1)

                turns(act, NT, body)

            @block.vector
            def _(dve):
                links = Chain(dve, chain, 2 * per)
                if kind != "msg":
                    dve.memset((sums if kind == "gat" else sums[:, 0:NB * W_COS])[:, :], 0.0)
                else:
                    dve.memset(sums[:, 0:NB * D], 0.0)

                def body(t, first):
                    links.turn(t)
                    for j in range(2):
                        b = t * 2 + j
                        if not first:
                            dve.wait_ge(block_turned.handle, block_turned.at(t * 2 + j - 1))
                        dve.tensor_scalar(staged[j][:, P:2 * P], blk(nodes, b), col(mean, b), col(rstd, b), ALU.subtract,
                                          ALU.mult).then_inc(block_staged.handle, 1)
                        dve.tensor_scalar(blk(nodes, b), blk(nodes, b), col(mean, b), col(rstd, b), ALU.subtract, ALU.mult)
                    for j in range(2):
                        b = t * 2 + j
                        rows = rows_out[j]
                        dve.wait_ge(block_product.handle, block_product.at(t * 2 + j + 1))
                        if not first:
                            dve.wait_ge(stored[j].handle, stored[j].at(t * 16))
                        if kind == "msg":
                            dve.tensor_tensor(rows[:, 0:D], bank[j][:, 0:D], v["b_msg_row"][:, :], ALU.add).then_inc(block_rows.handle, 1)
                        elif kind == "gat":
                            dve.tensor_scalar(blk(target, b), bank[j][:, HID:HID + 8], 1.0, None, ALU.mult)
                            dve.tensor_copy(rows[:, 0:W_GAT], bank[j][:, 0:W_GAT]).then_inc(block_rows.handle, 1)
                        else:
                            links.link(dve.tensor_copy(rows[:, 0:D], bank[j][:, 0:D]))
                            links.link(dve.tensor_tensor_reduce(work[j][:, 0:D], rows[:, 0:D], rows[:, 0:D], 1.0, 0.0, ALU.mult,
                                                                ALU.add, square[j][:, 0:1]))
                            dve.tensor_scalar(square[j][:, 0:1], square[j][:, 0:1], 1e-16, None, ALU.max).then_inc(root_in.handle, 1)
                            dve.wait_ge(root_set.handle, root_set.at(t * 2 + j + 1))
                            dve.memset(rows[:, D + 1:D + 2], 1.0)
                            links.link(dve.reciprocal(square[j][:, 2:3], square[j][:, 1:2]))
                            dve.tensor_scalar(blk(unit, b), rows[:, 0:D], square[j][:, 2:3], None, ALU.mult)
                            links.link(dve.tensor_copy(rows[:, D:D + 1], square[j][:, 2:3]))
                            dve.sem_inc(block_rows.handle, 1)

                turns(dve, NT, body)

            @block.sync
            def _(sp):
                turns(sp, NT, lambda t, first: store_rows(sp, table, width, t, first))
                all_stored(sp)
        for s in (block_staged, block_product, block_rows, block_turned, turned_kept):
            s.phase_over(NB)
        if kind == "cos":
            root_in.phase_over(NB)
            root_set.phase_over(NB)
        chain.phase_over(NT * 2 * per)
        for j in range(2):
            stored[j].phase_over(16 * NT)

    def msg_out_loop():
        with nc.Block() as block:
            @block.vector
            def _(dve):
                links = Chain(dve, chain, 2)

                def body(t, first):
                    links.turn(t)
                    for j in range(2):
                        b = t * 2 + j
                        links.link(dve.scalar_tensor_tensor(out=blk(nodes, b), in0=blk(sums_msg, b), scalar=0.0, in1=blk(nodes, b),
                                                            op0=ALU.max, op1=ALU.add))
                        dve.bn_stats(blk(stats, b), blk(nodes, b))

                turns(dve, NT, body)
        chain.phase_over(2 * NT)

    def cos_out_loop():
        with nc.Block() as block:
            @block.vector
            def _(dve):
                links = Chain(dve, chain, 2)
                links.turn(0)
                links.link(dve.tensor_scalar(spread[:, :], sums_cos[:, :, D + 1], EPS_ATT, None, ALU.add))
                links.link(dve.reciprocal(spread[:, :], spread[:, :]))
                chain.phase_over(2)

                def body(t, first):
                    links.turn(t)
                    for j in range(2):
                        b = t * 2 + j
                        links.link(dve.scalar_tensor_tensor(out=blk(nodes, b), in0=sums_cos[:, bass.ds(b, 1), 0:D].rearrange("p a w -> p (a w)"),
                                                            scalar=col(spread, b), in1=blk(nodes, b), op0=ALU.mult, op1=ALU.add))
                        dve.bn_stats(blk(stats, b), blk(nodes, b))

                turns(dve, NT, body)
        chain.phase_over(2 * NT)

    el_ends = sb("el_ends", [P, 2 * HEADS])
    el_ends_all = sb("el_ends_all", [P, 2 * HEADS])
    el_range = sb("el_range", [P, HEADS])
    wide_i = sb("wide_i", [P, 1], I32)

    def gat_shift():
        with nc.Block() as block:
            @block.vector
            def _(dve):
                links = Chain(dve, chain, 8)
                links.turn(0)
                for h in range(HEADS):
                    dve.tensor_reduce(el_ends[:, h:h + 1], target[:, :, h], AX.X, ALU.max)
                    ins = dve.tensor_reduce(el_ends[:, HEADS + h:HEADS + h + 1], target[:, :, h], AX.X, ALU.min)
                links.link(ins)
                links.link(dve.tensor_scalar(el_ends[:, HEADS:], el_ends[:, HEADS:], -1.0, None, ALU.mult))
                dve.sem_inc(root_in.handle, 1)
                dve.wait_ge(root_set.handle, root_set.at(1))
                links.link(dve.tensor_copy(target[:, :, 0:HEADS], el_ends_all[:, 0:HEADS].unsqueeze(1).to_broadcast([P, NB, HEADS])))
                links.link(dve.tensor_tensor(el_range[:, :], el_ends_all[:, 0:HEADS], el_ends_all[:, HEADS:], ALU.add))
                links.link(dve.tensor_reduce(spread[:, 0:1], el_range[:, :], AX.X, ALU.max))
                links.link(dve.tensor_scalar(spread[:, 0:1], spread[:, 0:1], WIDE, None, ALU.is_lt))
                links.link(dve.tensor_copy(wide_i[:, :], spread[:, 0:1]))

            @block.gpsimd
            def _(pool):
                pool.wait_ge(root_in.handle, root_in.at(1))
                pool.partition_all_reduce(el_ends_all[:, :], el_ends[:, :], P, bass.bass_isa.ReduceOp.max).then_inc(root_set.handle, 1)
        root_in.phase_over(1)
        root_set.phase_over(1)
        chain.phase_over(7)
        max_of_edges()
        with nc.Block() as block:
            @block.vector
            def _(dve):
                links = Chain(dve, chain, 2)
                links.turn(0)
                shift = target[:, :, 0:HEADS]
                links.link(dve.tensor_tensor(shift, shift, target[:, :, HEADS:2 * HEADS], ALU.add))
                links.link(dve.scalar_tensor_tensor(out=shift, in0=shift, scalar=0.2, in1=shift, op0=ALU.mult, op1=ALU.max))
        chain.phase_over(2)

    def max_of_edges():
        list_v = records["dst"].rearrange("(p c) w -> p c w", c=KT)
        with ExitStack() as scope:
            record = sb("max_record", [P, 1, RW], I32, scope)
            got = sb("max_got", [P, W_GAT], F32, scope)
            hot = sb("max_hot", [P, P], F32, scope)
            outside = sb("max_outside", [P, P], F32, scope)
            spread_el = sb("max_spread_el", [P, HEADS, P], F32, scope)
            tile_max = sb("tile_max", [P, HEADS], F32, scope)
            max_blocks_in = signal("max_blocks_in")
            max_record_in = signal("max_record_in")
            max_gathered = signal("max_gathered")
            max_turned = signal("max_turned")
            max_steps = signal("max_steps")

            def narrow(eng, name):
                reg = eng.alloc_register(f"{name}_narrow")
                eng.load(reg, wide_i[0:1, 0:1])
                return eng.snap(reg, min_val=0, max_val=1)

            with nc.Block() as block:
                @block.sync
                def _(sp):
                    with sp.If(narrow(sp, "sp") < 1):
                        sp.dma_start(block_row[:, :], tile_block["dst"]).then_inc(max_blocks_in.handle, 16)

                        def body(t, first):
                            if not first:
                                sp.wait_ge(max_steps.handle, 5 * t + 1)
                                sp.sem_inc(waits_passed.handle, 1)
                            sp.dma_start(record[:, :, :], list_v[:, bass.ds(t, 1), :]).then_inc(max_record_in.handle, 16)

                        turns(sp, KT, body)

                @block.gpsimd
                def _(pool):
                    with pool.If(narrow(pool, "pool") < 1):
                        def body(t, first):
                            pool.wait_ge(max_record_in.handle, 16 * t + 16)
                            pool.sem_inc(waits_passed.handle, 1)
                            pool.indirect_dma_start(
                                out=got[:, :], out_offset=None, in_=v["rows_gat"],
                                in_offset=bass.IndirectOffsetOnAxis(ap=record[:, 0, 0:1], axis=0),
                                bounds_check=N - 1, oob_is_err=False).then_inc(max_gathered.handle, 16)

                        turns(pool, KT, body)

                @block.tensor
                def _(pe):
                    with pe.If(narrow(pe, "pe") < 1):
                        def body(t, first):
                            pe.wait_ge(max_steps.handle, 5 * t + 4)
                            for h in range(HEADS):
                                ins = pe.transpose(bank[0][:, h * P:(h + 1) * P], spread_el[:, h, :], ident[:, :])
                            ins.then_inc(max_turned.handle, 1)

                        turns(pe, KT, body)

                @block.vector
                def _(dve):
                    with dve.If(narrow(dve, "dve") < 1):
                        block_reg = dve.alloc_register("max_block")
                        dve.memset(target[:, :, 0:HEADS], LOW).then_inc(max_steps.handle, 1)
                        dve.wait_ge(max_blocks_in.handle, 16)

                        def body(t, first):
                            dve.load(block_reg, block_row[0:1, bass.ds(t, 1)])
                            b = dve.snap(block_reg, min_val=0, max_val=NB - 1)
                            dve.wait_ge(max_gathered.handle, 16 * t + 16)
                            dve.tensor_scalar(hot[:, :], iota[:, :], record[:, 0, 1:2].bitcast(F32), None,
                                              ALU.is_equal).then_inc(max_steps.handle, 1)
                            dve.wait_ge(max_steps.handle, 5 * t + 2)
                            dve.tensor_scalar(outside[:, :], hot[:, :], -LOW, LOW, ALU.mult, ALU.add).then_inc(max_steps.handle, 1)
                            dve.wait_ge(max_steps.handle, 5 * t + 3)
                            for h in range(HEADS):
                                ins = dve.scalar_tensor_tensor(out=spread_el[:, h, :], in0=hot[:, :], scalar=got[:, HID + h:HID + h + 1],
                                                               in1=outside[:, :], op0=ALU.mult, op1=ALU.add)
                            ins.then_inc(max_steps.handle, 1)
                            dve.wait_ge(max_turned.handle, t + 1)
                            dve.tensor_reduce(tile_max[:, :], bank[0][:, :].rearrange("p (h e) -> p h e", h=HEADS), AX.X,
                                              ALU.max).then_inc(max_steps.handle, 1)
                            dve.wait_ge(max_steps.handle, 5 * t + 5)
                            place = target[:, bass.ds(b, 1), 0:HEADS]
                            dve.tensor_tensor(place, place, tile_max[:, :].unsqueeze(1), ALU.max).then_inc(max_steps.handle, 1)
                            dve.wait_ge(max_steps.handle, 5 * t + 6)

                        turns(dve, KT, body)

    def gat_out_loop():
        with ExitStack() as scope:
            hT = sb("hT", [P, KC, 2 * P], F32, scope)
            gate = {k: sb(f"gate_{k}", [P, KC, 2 * P], F32, scope) for k in ("r", "z", "n")}
            state = sb("state", [P, KC, 2 * P], F32, scope)
            share = [sb(f"share{j}", [P, HEADS], F32, scope) for j in range(2)]
            attended = signal("attended")
            attended_turned = signal("attended_turned")
            attended_kept = signal("attended_kept")
            gate_sum = signal("gate_sum")
            rz_set = signal("rz_set")
            n_in = signal("n_in")
            n_set = signal("n_set")
            state_set = signal("state_set")
            result = signal("result")
            nodes_set = signal("nodes_set")
            attend_steps = signal("attend_steps")
            add_steps = signal("add_steps")

            def lagged_turns(eng, stages):
                most = max(lag for _, lag in stages)
                for i in range(most + 1):
                    for stage, lag in stages:
                        if i >= lag:
                            stage(i - lag, i == lag)
                with eng.Fori(most + 1, NT) as t:
                    for stage, lag in stages:
                        stage(t - lag, False)
                for i in range(NT, NT + most):
                    for stage, lag in stages:
                        if i - lag < NT:
                            stage(i - lag, False)

            with nc.Block() as block:
                @block.vector
                def _(dve):
                    attend_links = Chain(dve, attend_steps, 2 * 3)
                    add_links = Chain(dve, add_steps, 2 * 2)

                    def attend(t, first):
                        attend_links.turn(t)
                        for j in range(2):
                            b = t * 2 + j
                            w = work[j]
                            attend_links.link(dve.tensor_scalar(share[j][:, :], sums_gat[:, bass.ds(b, 1), HID:].rearrange("p a w -> p (a w)"),
                                                                1e-30, None, ALU.max))
                            attend_links.link(dve.reciprocal(share[j][:, :], share[j][:, :]))
                            if not first:
                                dve.wait_ge(attended_turned.handle, attended_turned.at(t * 2 + j - 1))
                            attend_links.link(dve.tensor_tensor(w[:, :].rearrange("p (h d) -> p h d", h=HEADS),
                                                                sums_gat[:, bass.ds(b, 1), 0:HID].rearrange("p a (h d) -> p (a h) d", h=HEADS),
                                                                share[j][:, :].unsqueeze(2).to_broadcast([P, HEADS, DH]), ALU.mult))
                            dve.tensor_tensor(w[:, :], w[:, :], v["bias_gat_row"][:, :], ALU.add).then_inc(attended.handle, 1)

                    def new_gate(t, first):
                        dve.wait_ge(rz_set.handle, rz_set.at(t * 2 + 1))
                        dve.wait_ge(gate_sum.handle, gate_sum.at(t * 3 + 3))
                        if not first:
                            dve.wait_ge(state_set.handle, state_set.at(t))
                        for c in range(KC):
                            ins = dve.scalar_tensor_tensor(out=gate["n"][:, c, :], in0=gate["r"][:, c, :], scalar=v["b_hid_n"][:, c:c + 1],
                                                           in1=bank[6][:, c * 2 * P:(c + 1) * 2 * P], op0=ALU.mult, op1=ALU.add)
                        ins.then_inc(n_in.handle, 1)

                    def new_state(t, first):
                        dve.wait_ge(rz_set.handle, rz_set.at(t * 2 + 2))
                        dve.wait_ge(n_set.handle, n_set.at(t + 1))
                        if not first:
                            dve.wait_ge(result.handle, result.at(t * 2))
                        dve.tensor_tensor(state[:, :, :], gate["z"][:, :, :], gate["n"][:, :, :], ALU.mult).then_inc(state_set.handle, 1)

                    def add_result(t, first):
                        add_links.turn(t)
                        for j in range(2):
                            b = t * 2 + j
                            dve.wait_ge(result.handle, result.at(t * 2 + j + 1))
                            add_links.link(dve.tensor_tensor(staged[j][:, 0:D], bank[3 + 4 * j][:, 0:D], v["b_out_row"][:, :], ALU.add))
                            add_links.link(dve.tensor_tensor(blk(nodes, b), blk(nodes, b), staged[j][:, 0:D], ALU.add))
                            ins = dve.bn_stats(blk(stats, b), blk(nodes, b))
                        ins.then_inc(nodes_set.handle, 1)

                    lagged_turns(dve, [(attend, 0), (add_result, 3), (new_state, 2), (new_gate, 1)])

                @block.tensor
                def _(pe):
                    def turn_attended(t, first):
                        for j in range(2):
                            pe.wait_ge(attended.handle, attended.at(t * 2 + j + 1))
                            if not first:
                                pe.wait_ge(attended_kept.handle, attended_kept.at(t * 2 + j - 1))
                            for c in range(KC):
                                ins = pe.transpose(bank[j][:, c * P:(c + 1) * P], work[j][:, c * P:(c + 1) * P], ident[:, :])
                            ins.then_inc(attended_turned.handle, 1)

                    def gates(t, first):
                        pe.wait_ge(attended_kept.handle, attended_kept.at(t * 2 + 2))
                        if not first:
                            pe.wait_ge(rz_set.handle, rz_set.at(t * 2))
                        for g in range(3):
                            if g == 2 and not first:
                                pe.wait_ge(n_in.handle, n_in.at(t))
                            for c in range(KC):
                                for k in range(KC):
                                    row = (g * KC + c) * P
                                    ins = pe.matmul(bank[4 + g][:, c * 2 * P:(c + 1) * 2 * P], v["w_ihT"][:, k, row:row + P],
                                                    hT[:, k, :], start=(k == 0), stop=(k == KC - 1))
                            ins.then_inc(gate_sum.handle, 1)

                    def project(t, first):
                        pe.wait_ge(state_set.handle, state_set.at(t + 1))
                        if not first:
                            pe.wait_ge(nodes_set.handle, nodes_set.at(t))
                        for j in range(2):
                            for k in range(KC):
                                ins = pe.matmul(bank[3 + 4 * j][:, 0:D], state[:, k, j * P:(j + 1) * P], v["w_outT"][:, k, :],
                                                start=(k == 0), stop=(k == KC - 1))
                            ins.then_inc(result.handle, 1)

                    lagged_turns(pe, [(project, 3), (gates, 1), (turn_attended, 0)])

                @block.scalar
                def _(act):
                    def keep_attended(t, first):
                        for j in range(2):
                            act.wait_ge(attended_turned.handle, attended_turned.at(t * 2 + j + 1))
                            if not first:
                                act.wait_ge(gate_sum.handle, gate_sum.at(t * 3))
                            act.copy(hT[:, :, j * P:(j + 1) * P],
                                     bank[j][:, 0:KC * P].rearrange("p (c n) -> p c n", c=KC)).then_inc(attended_kept.handle, 1)

                    def sigmoids(t, first):
                        if not first:
                            act.wait_ge(n_in.handle, n_in.at(t))
                            act.wait_ge(state_set.handle, state_set.at(t))
                        for n, k in enumerate("rz"):
                            act.wait_ge(gate_sum.handle, gate_sum.at(t * 3 + n + 1))
                            for c in range(KC):
                                ins = act.activation(gate[k][:, c, :], bank[4 + n][:, c * 2 * P:(c + 1) * 2 * P], ACT.Sigmoid,
                                                     bias=v["b_gate"][:, n * KC + c:n * KC + c + 1], scale=(1.0, -1.0)[n])
                            ins.then_inc(rz_set.handle, 1)

                    def tanh(t, first):
                        act.wait_ge(n_in.handle, n_in.at(t + 1))
                        for c in range(KC):
                            ins = act.activation(gate["n"][:, c, :], gate["n"][:, c, :], ACT.Tanh,
                                                 bias=v["b_gate"][:, 2 * KC + c:2 * KC + c + 1])
                        ins.then_inc(n_set.handle, 1)

                    lagged_turns(act, [(keep_attended, 1), (tanh, 2), (sigmoids, 1)])

    def write_out():
        parts = 7
        size = NB // parts
        with nc.Block() as block:
            @block.vector
            def _(dve):
                links = Chain(dve, chain, parts)
                links.turn(0)
                for q in range(parts):
                    here = nodes[:, q * size:(q + 1) * size, :]
                    links.link(dve.tensor_tensor(here, here, mean[:, q * size:(q + 1) * size].unsqueeze(2).to_broadcast([P, size, D]),
                                                 ALU.subtract))
                    dve.tensor_tensor(here, here, rstd[:, q * size:(q + 1) * size].unsqueeze(2).to_broadcast([P, size, D]),
                                      ALU.mult).then_inc(block_staged.handle, 1)

            @block.sync
            def _(sp):
                for q in range(parts):
                    sp.wait_ge(block_staged.handle, block_staged.at(q + 1))
                    b0, b1 = q * size, min((q + 1) * size, NB - 1)
                    sp.dma_start(out[b0 * P:b1 * P, :].rearrange("(b p) d -> p b d", p=P), nodes[:, b0:b1, :]).then_inc(stored[0].handle, 16)
                sp.dma_start(out[FULL:N, :], nodes[0:LAST, NB - 1, :]).then_inc(stored[0].handle, 16)
                sp.wait_ge(stored[0].handle, stored[0].at(16 * (parts + 1)))
        block_staged.phase_over(parts)
        stored[0].phase_over(16 * (parts + 1))
        chain.phase_over(parts)

    load_x()
    over_nodes("first", conv_rows_loop, False)
    walk("conv1", "dst", v["rows_conv"][0], D, "conv")
    over_nodes("between", conv_rows_loop, True)
    walk("conv2", "dst", v["rows_conv"][1], D, "conv")
    over_nodes("conv_out", conv_out_loop)
    normalise_scales()
    if v.get("stop") == 1:
        return write_out()
    over_nodes("msg_rows", table_loop, "msg")
    walk("msg", "dst", v["rows_msg"], D, "msg")
    msg_out_loop()
    normalise_scales()
    if v.get("stop") == 2:
        return write_out()
    over_nodes("cos_rows", table_loop, "cos")
    walk("cos", "src", v["rows_cos"], W_COS, "cos")
    cos_out_loop()
    normalise_scales()
    if v.get("stop") == 3:
        return write_out()
    over_nodes("gat_rows", table_loop, "gat")
    gat_shift()
    walk("gat", "dst", v["rows_gat"], W_GAT, "gat")
    over_nodes("gat_out", gat_out_loop)
    normalise_scales()
    write_out()


_INS = {"x": "x", "src": "src", "dst": "dst", "edge_weight": "edge_weight", "L0_gnn_W1": "W1", "L0_gnn_b1": "b1",
        "L0_gnn_W2": "W2", "L0_gnn_b2": "b2", "L0_gnn_gamma": "gamma", "L0_gnn_beta": "beta",
        "L0_gnn_run_mean": "run_mean", "L0_gnn_run_var": "run_var", "L1_gnn_W": "W_msg", "L1_gnn_b": "b_msg",
        "L2_gnn_kernel": "W_cos", "L3_gnn_W_fc": "W_fc", "L3_gnn_attn_l": "attn_l", "L3_gnn_attn_r": "attn_r",
        "L3_gnn_bias_gat": "bias_gat", "L3_gnn_W_ih": "W_ih", "L3_gnn_b_ih": "b_ih", "L3_gnn_b_hh": "b_hh",
        "L3_gnn_W_out": "W_out", "L3_gnn_b_out": "b_out"}


def kernel(**inputs):
    import numpy as _np
    import concourse.bacc as _bacc
    from concourse import mybir as _mybir
    from concourse.bass_utils import run_bass_kernel_spmd as _run

    nc = _bacc.Bacc("TRN2", target_bir_lowering=False, num_devices=1)
    arrays, args = {}, {}
    for name, short in _INS.items():
        a = _np.ascontiguousarray(inputs[name])
        arrays[f"in_{name}_dram"] = a
        args[short] = nc.dram_tensor(f"in_{name}_dram", a.shape, _mybir.dt.from_np(a.dtype), kind="ExternalInput").ap()
    args["out"] = nc.dram_tensor("out_0_dram", (N, D), F32, kind="ExternalOutput").ap()
    program(nc, **args)
    r = _run(nc, [arrays], core_ids=[0])
    return r.results[0]["out_0_dram"]
```

```python
from contextlib import ExitStack

import concourse.bass as bass
from concourse import mybir

ALU = mybir.AluOpType
ACT = mybir.ActivationFunctionType
AX = mybir.AxisListType
F32 = mybir.dt.float32
BF16 = mybir.dt.bfloat16
I32 = mybir.dt.int32

P = 128
N = 12500
E = 212500
D = 128
HEADS = 4
HID = 256
DH = HID // HEADS
GATES = 3 * HID
GC = GATES // P
KC = HID // P

NB = -(-N // P)
LAST = N - (NB - 1) * P
NR = NB * P
NK = NB + 1

EC = -(-E // P)
EL = E - (P - 1) * EC
SU = 11
ST = EC // SU
SG = ((0, 6), (6, 5))
HC = SG[0][1]
PAIR_LAG = 2
NO_EDGE = NB * P
FAR = float(1 << 26)
NO_LANE = 999.0

U = 16
HU = U // 2
KT = -(-((E + NB * (P - 1)) // P) // U) * U
T = KT // U
TC = -(-KT // P)
KP = TC * P
ER = E // P
ELSE_LANE = 1000.0
RW = 4

VH = 2
NT = NB // 2
W_COS = D + 2
W_GAT = HID + HEADS
EPS_LN = 1e-5
EPS_BN = 1e-5
EPS_ATT = 1e-8
WIDE = 60.0
LOW = -1e30
assert ST * SU == EC and NT * 2 == NB


class Signal:

    def __init__(self, handle):
        self.handle = handle
        self.start = 0

    def at(self, n):
        return n + self.start

    def phase_over(self, n):
        self.start += n


class Chain:

    def __init__(self, eng, steps, per_turn):
        self.eng, self.steps, self.per_turn = eng, steps, per_turn

    def turn(self, t):
        self.t, self.n = t, 0

    def note(self, ins):
        self.n += 1
        ins.then_inc(self.steps.handle, 1)

    def link(self, ins):
        self.note(ins)
        self.wait()

    def wait(self):
        assert self.n <= self.per_turn
        self.eng.wait_ge(self.steps.handle, self.steps.at(self.t * self.per_turn + self.n))


def turns(eng, count, body):
    body(0, True)
    with eng.Fori(1, count) as t:
        body(t, False)


def lagged_turns(eng, stages):
    most = max(lag for _, lag in stages)
    for i in range(most + 1):
        for stage, lag in stages:
            if i >= lag:
                stage(i - lag, i == lag)
    with eng.Fori(most + 1, NT) as t:
        for stage, lag in stages:
            stage(t - lag, False)
    for i in range(NT, NT + most):
        for stage, lag in stages:
            if i - lag < NT:
                stage(i - lag, False)


def program(nc, x, src, dst, edge_weight, W1, b1, W2, b2, gamma, beta, run_mean, run_var, W_msg, b_msg, W_cos,
            W_fc, attn_l, attn_r, bias_gat, W_ih, b_ih, b_hh, W_out, b_out, out):
    ctx = ExitStack()
    with ctx:
        def sb(name, shape, dt=F32, scope=ctx):
            return scope.enter_context(nc.sbuf_tensor(name, shape, dt))

        def signal(name):
            return Signal(ctx.enter_context(nc.semaphore(name)))

        bank = [ctx.enter_context(nc.psum_tensor(f"bank{i}", [P, 512], F32)) for i in range(8)]

        waits_passed = signal("waits_passed")

        rows_conv = [nc.dram_tensor(f"rows_conv{i}", [NR, D], F32).ap() for i in range(2)]
        rows_msg = nc.dram_tensor("rows_msg", [NR, D], F32).ap()
        rows_cos = nc.dram_tensor("rows_cos", [NR, W_COS], F32).ap()
        rows_gat = nc.dram_tensor("rows_gat", [NR, W_GAT], F32).ap()
        records = {k: nc.dram_tensor(f"records_{k}", [P * KT, RW], I32).ap() for k in ("dst", "src")}
        tile_block = {k: nc.dram_tensor(f"tile_block_{k}", [1, KT], I32).ap() for k in ("dst", "src")}

        ident = sb("ident", [P, P])
        iota = sb("iota", [P, P])
        ones = sb("ones", [P, P])
        w1 = sb("w1", [P, D])
        w2 = sb("w2", [P, D])
        w_msgT = sb("w_msgT", [P, D])
        w_cos = sb("w_cos", [P, D])
        w_gat = sb("w_gat", [P, HID + 2 * HEADS])
        w_ihT = sb("w_ihT", [P, KC, GATES])
        w_outT = sb("w_outT", [P, KC, D])
        bn_scale = sb("bn_scale", [P, D])
        bn_shift = sb("bn_shift", [P, D])
        b2_row = sb("b2_row", [P, D])
        b_msg_row = sb("b_msg_row", [P, D])
        bias_gat_row = sb("bias_gat_row", [P, HID])
        b_out_row = sb("b_out_row", [P, D])
        b_gate = sb("b_gate", [P, GC])
        b_hid_n = sb("b_hid_n", [P, KC])
        norm = {k: sb(f"norm_{k}", [P, NB]) for k in ("dst", "src")}

        load_weights(nc, ctx, locals())
        sort_edges(nc, ctx, locals())
        layers(nc, ctx, locals())


def row_of(ap):
    return ap.rearrange("(a d) -> a d", a=1).broadcast_to([P, ap.shape[0]])


def load_weights(nc, ctx, v):
    (bank, ident, iota, ones, w1, w2, w_msgT, w_cos, w_gat, w_ihT, w_outT, bn_scale, bn_shift, b2_row, b_msg_row,
     bias_gat_row, b_out_row, b_gate, b_hid_n) = (v[k] for k in (
         "bank", "ident", "iota", "ones", "w1", "w2", "w_msgT", "w_cos", "w_gat", "w_ihT", "w_outT", "bn_scale",
         "bn_shift", "b2_row", "b_msg_row", "bias_gat_row", "b_out_row", "b_gate", "b_hid_n"))
    signal = v["signal"]
    with ExitStack() as scope:
        def sb(name, shape, dt=F32):
            return v["sb"](name, shape, dt, scope)

        iota_i = sb("iota_i", [P, P], I32)
        msg_in = sb("msg_in", [P, D])
        fc_in = sb("fc_in", [P, KC, D])
        ih_in = sb("ih_in", [P, GC, HID])
        out_in = sb("out_in", [P, HID])
        attn = sb("attn", [P, KC, 2 * HEADS])
        rows = {k: sb(f"row_{k}", [P, D]) for k in ("b1", "gamma", "beta", "mean", "var")}
        b_hh_col = sb("b_hh_col", [P, GC])

        weights_in = signal("weights_in")
        attn_zero = signal("attn_zero")
        attn_in = signal("attn_in")
        consts_set = signal("consts_set")
        iota_set = signal("iota_set")
        turned = signal("turned")
        kept = signal("kept")
        var_eps = signal("var_eps")
        var_root = signal("var_root")
        chain = signal("chain_weights")
        loads = [
            (w1[:, :], v["W1"]), (w2[:, :], v["W2"]), (msg_in[:, :], v["W_msg"]), (w_cos[:, :], v["W_cos"]),
            (fc_in[:, :, :], v["W_fc"].rearrange("(c p) d -> p c d", p=P)),
            (ih_in[:, :, :], v["W_ih"].rearrange("(c p) k -> p c k", p=P)), (out_in[:, :], v["W_out"]),
            (rows["b1"][:, :], row_of(v["b1"])), (rows["gamma"][:, :], row_of(v["gamma"])),
            (rows["beta"][:, :], row_of(v["beta"])), (rows["mean"][:, :], row_of(v["run_mean"])),
            (rows["var"][:, :], row_of(v["run_var"])), (b2_row[:, :], row_of(v["b2"])),
            (b_msg_row[:, :], row_of(v["b_msg"])), (bias_gat_row[:, :], row_of(v["bias_gat"])),
            (b_out_row[:, :], row_of(v["b_out"])),
            (b_gate[:, :], v["b_ih"].rearrange("(c p) -> p c", p=P)),
            (b_hh_col[:, :], v["b_hh"].rearrange("(c p) -> p c", p=P)),
        ]
        turns_of = [(msg_in[:, :], w_msgT[:, :])]
        turns_of += [(fc_in[:, c, :], w_gat[:, c * P:(c + 1) * P]) for c in range(KC)]
        turns_of += [(ih_in[:, g, c * P:(c + 1) * P], w_ihT[:, c, g * P:(g + 1) * P]) for g in range(GC) for c in range(KC)]
        turns_of += [(out_in[:, c * P:(c + 1) * P], w_outT[:, c, :]) for c in range(KC)]

        with nc.Block() as block:
            @block.sync
            def _(sp):
                with nc.allow_non_contiguous_dma(reason="biases, a few hundred words, once"):
                    for to, of in loads:
                        sp.dma_start(to, of).then_inc(weights_in.handle, 16)
                    sp.wait_ge(attn_zero.handle, attn_zero.at(1))
                    for n, a in enumerate((v["attn_l"], v["attn_r"])):
                        for h in range(HEADS):
                            lanes = slice(h % 2 * DH, h % 2 * DH + DH)
                            column = n * HEADS + h
                            sp.dma_start(attn[lanes, h // 2, column:column + 1],
                                         a[h:h + 1, :].rearrange("a d -> d a")).then_inc(attn_in.handle, 16)

            @block.gpsimd
            def _(pool):
                pool.iota(iota_i[:, :], pattern=[[1, P]], base=0, channel_multiplier=0).then_inc(iota_set.handle, 1)
                pool.memset(ident[:, :], 0.0).then_inc(consts_set.handle, 1)
                pool.wait_ge(consts_set.handle, consts_set.at(1))
                pool.affine_select(out=ident[:, :], in_=ident[:, :], compare_op=ALU.not_equal, fill=1.0, base=0,
                                   pattern=[[-1, P]], channel_multiplier=1).then_inc(consts_set.handle, 1)

            @block.tensor
            def _(pe):
                pe.wait_ge(consts_set.handle, consts_set.at(2))
                pe.wait_ge(weights_in.handle, weights_in.at(16 * len(loads)))
                for i, (of, _) in enumerate(turns_of):
                    if i >= 4:
                        pe.wait_ge(kept.handle, kept.at(i - 3))
                    pe.transpose(bank[i % 4][:, 0:P], of, ident[:, :]).then_inc(turned.handle, 1)
                pe.wait_ge(attn_in.handle, attn_in.at(16 * 2 * HEADS))
                for c in range(KC):
                    ins = pe.matmul(bank[4][:, 0:2 * HEADS], fc_in[:, c, :], attn[:, c, :], start=(c == 0),
                                    stop=(c == KC - 1))
                ins.then_inc(turned.handle, 1)

            @block.vector
            def _(dve):
                links = Chain(dve, chain, 8)
                links.turn(0)
                dve.memset(attn[:, :, :], 0.0).then_inc(attn_zero.handle, 1)
                dve.memset(ones[:, :], 1.0)
                dve.wait_ge(iota_set.handle, iota_set.at(1))
                dve.tensor_copy(iota[:, :], iota_i[:, :])
                dve.wait_ge(weights_in.handle, weights_in.at(16 * len(loads)))
                dve.tensor_scalar(rows["var"][:, :], rows["var"][:, :], EPS_BN, None, ALU.add).then_inc(var_eps.handle, 1)
                dve.wait_ge(var_root.handle, var_root.at(1))
                links.link(dve.reciprocal(rows["var"][:, :], rows["var"][:, :]))
                links.link(dve.tensor_tensor(bn_scale[:, :], rows["var"][:, :], rows["gamma"][:, :], ALU.mult))
                links.link(dve.tensor_tensor(rows["b1"][:, :], rows["b1"][:, :], rows["mean"][:, :], ALU.subtract))
                links.link(dve.tensor_tensor(rows["b1"][:, :], rows["b1"][:, :], bn_scale[:, :], ALU.mult))
                links.link(dve.tensor_tensor(bn_shift[:, :], rows["b1"][:, :], rows["beta"][:, :], ALU.add))
                links.link(dve.tensor_copy(b_hid_n[:, :], b_hh_col[:, 2 * KC:3 * KC]))
                links.link(dve.tensor_tensor(b_gate[:, 0:2 * KC], b_gate[:, 0:2 * KC], b_hh_col[:, 0:2 * KC], ALU.add))
                links.link(dve.tensor_scalar(b_gate[:, KC:2 * KC], b_gate[:, KC:2 * KC], -1.0, None, ALU.mult))
                for i, (_, to) in enumerate(turns_of):
                    dve.wait_ge(turned.handle, turned.at(i + 1))
                    dve.tensor_copy(to, bank[i % 4][:, 0:P]).then_inc(kept.handle, 1)
                dve.wait_ge(turned.handle, turned.at(len(turns_of) + 1))
                dve.tensor_copy(w_gat[:, HID:], bank[4][:, 0:2 * HEADS]).then_inc(kept.handle, 1)
                dve.wait_ge(kept.handle, kept.at(len(turns_of) + 1))

            @block.scalar
            def _(act):
                act.wait_ge(var_eps.handle, var_eps.at(1))
                act.activation(rows["var"][:, :], rows["var"][:, :], ACT.Sqrt).then_inc(var_root.handle, 1)


def sort_edges(nc, ctx, v):
    bank, ident, iota, ones, norm, records, tile_block, waits_passed = (
        v[k] for k in ("bank", "ident", "iota", "ones", "norm", "records", "tile_block", "waits_passed"))
    signal = v["signal"]
    keys = ("src", "dst")
    other = {"dst": "src", "src": "dst"}
    with ExitStack() as scope:
        def sb(name, shape, dt=F32):
            return v["sb"](name, shape, dt, scope)

        ends = {k: sb(f"ends_{k}", [P, EC], I32) for k in keys}
        weight = sb("weight", [P, EC])
        hi = {k: sb(f"hi_{k}", [P, EC]) for k in keys}
        lo = {k: sb(f"lo_{k}", [P, EC]) for k in keys}
        bits = sb("bits", [P, EC], I32)
        hot_hi = [sb(f"hot_hi{g}", [P, n, 100], BF16) for g, (_, n) in enumerate(SG)]
        pair_hi = [sb(f"pair_hi{g}", [P, n, 100], BF16) for g, (_, n) in enumerate(SG)]
        pair_lo = [sb(f"pair_lo{g}", [P, n, P], BF16) for g, (_, n) in enumerate(SG)]
        before = sb("before", [P, P])
        before_h = sb("before_h", [P, P], BF16)
        rest_h = sb("rest_h", [P, P], BF16)
        lane_i = sb("lane_i", [P, 1], I32)
        far = sb("far", [P, 1])
        tile_i = sb("tile_i", [P, KP], I32)
        tile_f = sb("tile_f", [P, KP])
        begun = sb("begun", [P, KP])
        block_row = sb("sorted_block_row", [1, KT], I32)
        count = sb("count", [P, P])
        total = sb("total", [P, 1])
        total_i = sb("total_i", [P, 1], I32)
        n_tiles = sb("n_tiles", [P, 1])
        first_tile = sb("first_tile", [P, 1])
        first_place = sb("first_place", [P, 1])
        place_diag = sb("place_diag", [P, NK])
        no_records = sb("no_records", [P, KT, RW], I32)

        next_end = sb("next_end", [P, 1], I32)
        next_hi = sb("next_hi", [P, 1])
        falls = sb("falls", [P, 2])
        falls_all = sb("falls_all", [P, 2])
        any_fall = sb("any_fall", [P, 1])
        unsorted_i = sb("unsorted_i", [P, 1], I32)

        zeroed = signal("zeroed")
        edges_in = signal("edges_in")
        index_set = signal("index_set")
        blank_set = signal("blank_set")
        blank_out = signal("blank_out")
        counted = signal("counted")
        falls_set = signal("falls_set")
        falls_met = signal("falls_met")
        pair_set = signal("pair_set")
        pair_used = signal("pair_used")
        chain = signal("chain_sort")
        turned = signal("sort_turned")
        begun_set = signal("begun_set")
        block_sum = signal("block_sum")
        block_kept = signal("block_kept")
        degree_in = signal("degree_in")
        degree_root = signal("degree_root")
        blocks_out = signal("blocks_out")
        consts = signal("sort_consts")

        CH = KT // 4

        def group_of(c):
            return (0, c) if c < SG[1][0] else (1, c - SG[1][0])

        hist_scope = ExitStack()
        hist_hi = v["sb"]("hist_hi", [P, ST, 2 * HC], BF16, hist_scope)
        hist_lo = v["sb"]("hist_lo", [P, ST, 2 * HC], BF16, hist_scope)
        iota_cols = v["sb"]("iota_cols", [P, P, HC], BF16, hist_scope)
        hist_hot_hi = [v["sb"](f"hist_hot_hi{g}", [P, 100, HC], BF16, hist_scope) for g in range(2)]
        hist_hot_lo = [v["sb"](f"hist_hot_lo{g}", [P, P, HC], BF16, hist_scope) for g in range(2)]

        with nc.Block() as block:
            @block.sync
            def _(sp):
                sp.wait_ge(zeroed.handle, zeroed.at(1))
                for to, of in ((ends["dst"], v["dst"]), (ends["src"], v["src"]), (weight, v["edge_weight"])):
                    sp.dma_start(to[0:P - 1, :], of[0:(P - 1) * EC].rearrange("(p c) -> p c", c=EC)).then_inc(edges_in.handle, 16)
                    sp.dma_start(to[P - 1:P, 0:EL], of[(P - 1) * EC:E].rearrange("(p c) -> p c", p=1)).then_inc(edges_in.handle, 16)
                with nc.allow_non_contiguous_dma(reason="128 words, once"):
                    sp.dma_start(next_end[0:P - 2, :], v["dst"][0:(P - 1) * EC].rearrange("(p c) -> p c", c=EC)[1:P - 1, 0:1]).then_inc(edges_in.handle, 16)
                sp.dma_start(next_end[P - 2:P - 1, :], v["dst"][(P - 1) * EC:(P - 1) * EC + 1].rearrange("(p c) -> p c", p=1)).then_inc(edges_in.handle, 16)
                sp.wait_ge(blank_set.handle, blank_set.at(1))
                for k in keys:
                    sp.dma_start(records[k].rearrange("(p c) w -> p c w", c=KT), no_records[:, :, :]).then_inc(blank_out.handle, 16)
                sp.wait_ge(blank_out.handle, blank_out.at(32))

            @block.gpsimd
            def _(pool):
                pool.memset(before[:, :], 0.0).then_inc(consts.handle, 1)
                pool.wait_ge(consts.handle, consts.at(1))
                pool.affine_select(out=before[:, :], in_=before[:, :], compare_op=ALU.is_ge, fill=1.0, base=0,
                                   pattern=[[-1, P]], channel_multiplier=1).then_inc(index_set.handle, 1)
                pool.iota(lane_i[:, :], pattern=[[0, 1]], base=0, channel_multiplier=1).then_inc(index_set.handle, 1)
                pool.iota(tile_i[:, :], pattern=[[1, KP]], base=0, channel_multiplier=0).then_inc(index_set.handle, 1)
                pool.wait_ge(falls_set.handle, falls_set.at(1))
                pool.partition_all_reduce(falls_all[:, :], falls[:, :], P, bass.bass_isa.ReduceOp.max).then_inc(falls_met.handle, 1)

            @block.vector
            def _(dve):
                for k in keys:
                    dve.memset(ends[k][:, :], NO_EDGE)
                dve.memset(next_end[:, :], NO_EDGE)
                dve.memset(weight[:, :], 0.0).then_inc(zeroed.handle, 1)
                links = Chain(dve, chain, 3 + 8 + 6)
                links.turn(0)
                links.link(dve.memset(no_records[:, :, :], 0))
                dve.memset(no_records[:, :, 1:2].bitcast(F32), NO_LANE).then_inc(blank_set.handle, 1)
                dve.wait_ge(index_set.handle, index_set.at(3))
                dve.tensor_copy(before_h[:, :], before[:, :])
                dve.tensor_scalar(rest_h[:, :], before[:, :], -1.0, 1.0, ALU.mult, ALU.add)
                dve.tensor_copy(tile_f[:, :], tile_i[:, :])
                links.link(dve.tensor_copy(far[:, :], lane_i[:, :]))
                links.link(dve.tensor_scalar(far[:, :], far[:, :], float(NB), FAR, ALU.is_ge, ALU.mult))
                dve.wait_ge(edges_in.handle, edges_in.at(128))
                for k in keys:
                    links.link(dve.tensor_scalar(bits[:, :], ends[k][:, :], 7, None, ALU.logical_shift_right))
                    links.link(dve.tensor_copy(hi[k][:, :], bits[:, :]))
                    links.link(dve.tensor_scalar(bits[:, :], ends[k][:, :], 127, None, ALU.bitwise_and))
                    links.link(dve.tensor_copy(lo[k][:, :], bits[:, :]))

                for padded, key in ((hist_hi, hi["src"]), (hist_lo, lo["src"])):
                    dve.memset(padded[:, :, SU:], -1.0)
                    dve.tensor_copy(padded[:, :, 0:SU], key[:, :].rearrange("p (t c) -> p t c", c=SU))
                dve.tensor_copy(iota_cols[:, :, :], iota[:, :].unsqueeze(2).to_broadcast([P, P, HC]))
                links.link(dve.tensor_scalar(next_end[:, :], next_end[:, :], 7, None, ALU.logical_shift_right))
                links.link(dve.tensor_copy(next_hi[:, :], next_end[:, :]))
                links.link(dve.tensor_tensor(begun[:, 0:EC - 1], hi["dst"][:, 0:EC - 1], hi["dst"][:, 1:EC], ALU.is_gt))
                dve.tensor_reduce(falls[:, 0:1], begun[:, 0:EC - 1], AX.X, ALU.max)
                links.link(dve.tensor_tensor(falls[:, 1:2], hi["dst"][:, EC - 1:EC], next_hi[:, :], ALU.is_gt))
                dve.sem_inc(falls_set.handle, 1)

                def body(t, first):
                    for g in range(2):
                        if not first:
                            dve.wait_ge(pair_used.handle, pair_used.at(t * 2 + g - 1))
                        for hot, key, size in ((hist_hot_hi, hist_hi, 100), (hist_hot_lo, hist_lo, P)):
                            ins = dve.tensor_tensor(hot[g][:, :, :], key[:, bass.ds(t, 1), g * HC:(g + 1) * HC].to_broadcast([P, size, HC]),
                                                    iota_cols[:, 0:size, :], ALU.is_equal)
                        ins.then_inc(pair_set.handle, 1)

                turns(dve, ST, body)
                dve.wait_ge(falls_met.handle, falls_met.at(1))
                links.link(dve.tensor_tensor(any_fall[:, :], falls_all[:, 0:1], falls_all[:, 1:2], ALU.max))
                links.link(dve.tensor_copy(unsorted_i[:, :], any_fall[:, :]))

            @block.tensor
            def _(pe):
                def body(t, first):
                    for g, (_, n) in enumerate(SG):
                        pe.wait_ge(pair_set.handle, pair_set.at(t * 2 + g + 1))
                        for j in range(n):
                            ins = pe.matmul(bank[keys.index("src")][0:NK, 0:P], hist_hot_hi[g][:, 0:NK, j], hist_hot_lo[g][:, :, j],
                                            start=first and g == 0 and j == 0, stop=True, skip_group_check=True)
                        ins.then_inc(pair_used.handle, 1)

                turns(pe, ST, body)
        hist_scope.close()
        chain.phase_over(3 + 8 + 6)
        pair_set.phase_over(2 * ST)
        pair_used.phase_over(2 * ST)

        def use_counts(k):
            b = keys.index(k)
            with nc.Block() as block:
                @block.vector
                def _(dve):
                    links = Chain(dve, chain, 9)
                    links.turn(0)
                    links.link(dve.tensor_copy(count[0:NK, :], bank[b][0:NK, 0:P]))
                    links.link(dve.tensor_reduce(total[0:NK, :], count[0:NK, :], AX.X, ALU.add))
                    links.link(dve.tensor_scalar(total[0:NK, :], total[0:NK, :], float(P - 1), None, ALU.add))
                    links.link(dve.tensor_copy(total_i[0:NK, :], total[0:NK, :]))
                    links.link(dve.tensor_scalar(total_i[0:NK, :], total_i[0:NK, :], 7, None, ALU.logical_shift_right))
                    dve.tensor_copy(n_tiles[0:NK, :], total_i[0:NK, :]).then_inc(counted.handle, 1)
                    dve.wait_ge(turned.handle, turned.at(1))
                    dve.tensor_scalar(norm[k][:, :], bank[2][:, 0:NB], 1.0, 1.0, ALU.add, ALU.max).then_inc(degree_in.handle, 1)
                    links.link(dve.tensor_copy(first_tile[0:NK, :], bank[3][0:NK, 0:1]))
                    links.link(dve.tensor_scalar(first_place[0:NK, :], first_tile[0:NK, :], float(P), None, ALU.mult))
                    dve.tensor_scalar(begun[0:NB, :], tile_f[0:NB, :], first_tile[0:NB, :], None, ALU.is_ge).then_inc(begun_set.handle, 1)
                    links.link(dve.tensor_tensor(first_place[0:NK, :], first_place[0:NK, :], far[0:NK, :], ALU.add))
                    links.link(dve.tensor_scalar(place_diag[0:NK, :], ident[0:NK, 0:NK], first_place[0:NK, :], None, ALU.mult))
                    dve.wait_ge(block_sum.handle, block_sum.at(1))
                    for q in range(4):
                        ins = dve.tensor_scalar(block_row[:, q * CH:(q + 1) * CH], bank[4 + q][0:1, 0:CH], -1.0, None, ALU.add)
                    ins.then_inc(block_kept.handle, 1)
                    dve.wait_ge(degree_root.handle, degree_root.at(1))
                    dve.reciprocal(norm[k][:, :], norm[k][:, :])

                @block.tensor
                def _(pe):
                    pe.wait_ge(counted.handle, counted.at(1))
                    pe.transpose(bank[2][:, 0:NB], count[0:NB, :], ident[0:NB, 0:NB])
                    pe.matmul(bank[3][0:NK, 0:1], before[0:NK, 0:NK], n_tiles[0:NK, :], start=True, stop=True).then_inc(turned.handle, 1)
                    pe.wait_ge(begun_set.handle, begun_set.at(1))
                    for q in range(4):
                        ins = pe.matmul(bank[4 + q][0:1, 0:CH], ones[0:NB, 0:1], begun[0:NB, q * CH:(q + 1) * CH], start=True, stop=True)
                    ins.then_inc(block_sum.handle, 1)

                @block.scalar
                def _(act):
                    act.wait_ge(degree_in.handle, degree_in.at(1))
                    act.activation(norm[k][:, :], norm[k][:, :], ACT.Sqrt).then_inc(degree_root.handle, 1)

                @block.sync
                def _(sp):
                    sp.wait_ge(block_kept.handle, block_kept.at(1))
                    sp.dma_start(tile_block[k], block_row[:, :]).then_inc(blocks_out.handle, 16)
                    sp.wait_ge(blocks_out.handle, blocks_out.at(16))
            chain.phase_over(9)
            blocks_out.phase_over(16)
            for s in (counted, turned, degree_in, begun_set, block_sum, block_kept, degree_root):
                s.phase_over(1)

        def unsorted(eng, name):
            reg = eng.alloc_register(f"{name}_unsorted")
            eng.load(reg, unsorted_i[0:1, 0:1])
            return eng.snap(reg, min_val=0, max_val=1)

        edge_rows = nc.dram_tensor("edge_rows", [KP, 3, P], I32).ap()

        def records_in_order():
            with ExitStack() as inner:
                def sb(name, shape, dt=F32):
                    return v["sb"](name, shape, dt, inner)

                pad_rows = sb("pad_rows", [P, 3, P], I32)
                edges_of = sb("edges_of", [P, 1])
                begin = sb("block_begin", [P, 1])
                begin_i = sb("block_begin_i", [P, 1], I32)
                end = sb("block_end", [P, 1])
                end_i = sb("block_end_i", [P, 1], I32)
                tiles_of = sb("tiles_of", [P, 1])
                lead = sb("lead", [P, 1])
                rise = sb("rise", [P, NB])
                tile_terms = sb("tile_terms", [P, 2])
                tile_data = sb("tile_data", [P, TC, 2])
                tile_no_i = sb("tile_no_i", [P, TC], I32)
                tile_no = sb("tile_no", [P, TC])
                row_of_tile = sb("row_of_tile", [P, TC], I32)
                block_of_tile = sb("block_of_tile", [P, TC])
                got = sb("edge_rows_got", [P, TC, 3, P], I32)
                tile_words = [sb(f"tile_words{w}", [P, TC, P]) for w in range(3)]
                rows_hi = sb("rows_hi", [P, TC, P])
                rows_bits = sb("rows_bits", [P, TC, P], I32)
                steps = signal("in_order_steps")
                pads_set = signal("pads_set")
                pads_out = signal("pads_out")
                rows_out = signal("edge_rows_out")
                numbers_set = signal("numbers_set")
                prepared = signal("in_order_prepared")
                multiplied = signal("in_order_multiplied")
                blocks_kept = signal("in_order_blocks_kept")
                blocks_stored = signal("in_order_blocks_stored")
                rows_known = signal("rows_known")
                rows_got = signal("edge_rows_in")
                words_set = signal("words_set")
                words_turned = signal("words_turned")
                words_kept = signal("words_kept")
                records_out = signal("in_order_records_out")

                with nc.Block() as block:
                    @block.sync
                    def _(sp):
                        with sp.If(unsorted(sp, "sp") < 1):
                            sp.wait_ge(pads_set.handle, 1)
                            sp.dma_start(edge_rows[KP - P:KP, :, :], pad_rows[:, :, :]).then_inc(pads_out.handle, 16)
                            sp.dma_start(edge_rows[ER:KP - P, :, :], pad_rows[0:KP - P - ER, :, :]).then_inc(pads_out.handle, 16)
                            sp.wait_ge(pads_out.handle, 32)
                            for w, of in enumerate((v["src"], v["dst"], v["edge_weight"].bitcast(I32))):
                                sp.dma_start(edge_rows[0:ER, w, :], of[0:ER * P].rearrange("(r l) -> r l", l=P)).then_inc(rows_out.handle, 16)
                                sp.dma_start(edge_rows[ER:ER + 1, w, 0:E - ER * P], of[ER * P:E].rearrange("(r l) -> r l", r=1)).then_inc(rows_out.handle, 16)
                            sp.wait_ge(blocks_kept.handle, 1)
                            sp.dma_start(tile_block["dst"], block_row[:, :]).then_inc(blocks_stored.handle, 16)
                            sp.wait_ge(words_kept.handle, 3 * TC)
                            sp.dma_start(records["dst"].rearrange("(p c) w -> p c w", c=KT), no_records[:, :, :]).then_inc(records_out.handle, 16)
                            sp.wait_ge(blocks_stored.handle, 16)
                            sp.wait_ge(records_out.handle, 16)

                    @block.gpsimd
                    def _(pool):
                        with pool.If(unsorted(pool, "pool") < 1):
                            pool.iota(tile_no_i[:, :], pattern=[[P, TC]], base=0, channel_multiplier=1).then_inc(numbers_set.handle, 1)
                            pool.wait_ge(rows_out.handle, 6 * 16)
                            pool.wait_ge(rows_known.handle, 1)
                            for q in range(TC):
                                pool.indirect_dma_start(
                                    out=got[:, q, :, :].rearrange("p w l -> p (w l)"), out_offset=None,
                                    in_=edge_rows.rearrange("r w l -> r (w l)"),
                                    in_offset=bass.IndirectOffsetOnAxis(ap=row_of_tile[:, q:q + 1], axis=0),
                                    bounds_check=KP - 1, oob_is_err=False).then_inc(rows_got.handle, 16)

                    @block.tensor
                    def _(pe):
                        with pe.If(unsorted(pe, "pe") < 1):
                            pe.wait_ge(prepared.handle, 1)
                            pe.matmul(bank[2][0:NB, 0:1], before[0:NB, 0:NB], edges_of[0:NB, :], start=True, stop=True).then_inc(multiplied.handle, 1)
                            pe.wait_ge(prepared.handle, 2)
                            pe.matmul(bank[3][0:NB, 0:1], before[0:NB, 0:NB], tiles_of[0:NB, :], start=True, stop=True).then_inc(multiplied.handle, 1)
                            pe.wait_ge(prepared.handle, 3)
                            pe.matmul(bank[2][0:NB, 0:1], rise[0:NB, :], lead[0:NB, :], start=True, stop=True).then_inc(multiplied.handle, 1)
                            pe.wait_ge(prepared.handle, 4)
                            for q in range(TC):
                                pe.matmul(bank[3][:, 2 * q:2 * q + 2], begun[0:NB, q * P:(q + 1) * P], tile_terms[0:NB, :], start=True, stop=True)
                            for q in range(4):
                                ins = pe.matmul(bank[4 + q][0:1, 0:CH], ones[0:NB, 0:1], begun[0:NB, q * CH:(q + 1) * CH], start=True, stop=True)
                            ins.then_inc(multiplied.handle, 1)
                            pe.wait_ge(blocks_kept.handle, 1)
                            pe.wait_ge(words_set.handle, 1)
                            for q in range(TC):
                                for w in range(3):
                                    n = 3 * q + w
                                    if n >= 4:
                                        pe.wait_ge(words_kept.handle, n - 3)
                                    pe.transpose(bank[4 + n % 4][:, 0:P], tile_words[w][:, q, :], ident[:, :]).then_inc(words_turned.handle, 1)

                    @block.vector
                    def _(dve):
                        with dve.If(unsorted(dve, "dve") < 1):
                            links = Chain(dve, steps, 30)
                            links.turn(0)
                            links.link(dve.memset(pad_rows[:, :, :], 0))
                            dve.memset(pad_rows[:, 1, :], NO_EDGE).then_inc(pads_set.handle, 1)
                            links.link(dve.memset(rise[:, :], 0.0))
                            links.link(dve.tensor_copy(rise[:, 1:NB], ident[:, 0:NB - 1]))
                            links.link(dve.tensor_tensor(rise[:, :], ident[:, 0:NB], rise[:, :], ALU.subtract))
                            links.link(dve.tensor_reduce(edges_of[0:NB, :], count[0:NB, :], AX.X, ALU.add))
                            dve.sem_inc(prepared.handle, 1)
                            dve.wait_ge(multiplied.handle, 1)
                            links.link(dve.tensor_copy(begin[0:NB, :], bank[2][0:NB, 0:1]))
                            links.link(dve.tensor_tensor(end[0:NB, :], begin[0:NB, :], edges_of[0:NB, :], ALU.add))
                            links.link(dve.tensor_scalar(end[0:NB, :], end[0:NB, :], float(P - 1), None, ALU.add))
                            links.link(dve.tensor_copy(begin_i[0:NB, :], begin[0:NB, :]))
                            links.link(dve.tensor_copy(end_i[0:NB, :], end[0:NB, :]))
                            links.link(dve.tensor_scalar(begin_i[0:NB, :], begin_i[0:NB, :], 7, None, ALU.logical_shift_right))
                            links.link(dve.tensor_scalar(end_i[0:NB, :], end_i[0:NB, :], 7, None, ALU.logical_shift_right))
                            links.link(dve.tensor_copy(begin[0:NB, :], begin_i[0:NB, :]))
                            links.link(dve.tensor_copy(end[0:NB, :], end_i[0:NB, :]))
                            links.link(dve.tensor_tensor(tiles_of[0:NB, :], end[0:NB, :], begin[0:NB, :], ALU.subtract))
                            links.link(dve.tensor_scalar(edges_of[0:NB, :], edges_of[0:NB, :], 1.0, None, ALU.is_ge))
                            links.link(dve.tensor_tensor(tiles_of[0:NB, :], tiles_of[0:NB, :], edges_of[0:NB, :], ALU.mult))
                            dve.sem_inc(prepared.handle, 1)
                            dve.wait_ge(multiplied.handle, 2)
                            links.link(dve.tensor_copy(first_tile[0:NB, :], bank[3][0:NB, 0:1]))
                            links.link(dve.tensor_tensor(lead[0:NB, :], begin[0:NB, :], first_tile[0:NB, :], ALU.subtract))
                            dve.sem_inc(prepared.handle, 1)
                            dve.tensor_scalar(begun[0:NB, :], tile_f[0:NB, :], first_tile[0:NB, :], None, ALU.is_ge)
                            dve.memset(tile_terms[:, 0:1], 1.0)
                            dve.wait_ge(multiplied.handle, 3)
                            links.link(dve.tensor_copy(tile_terms[0:NB, 1:2], bank[2][0:NB, 0:1]))
                            dve.sem_inc(prepared.handle, 1)
                            dve.wait_ge(multiplied.handle, 4)
                            links.link(dve.tensor_copy(tile_data[:, :, :].rearrange("p q d -> p (q d)"), bank[3][:, 0:2 * TC]))
                            for q in range(4):
                                ins = dve.tensor_scalar(block_row[:, q * CH:(q + 1) * CH], bank[4 + q][0:1, 0:CH], -1.0, None, ALU.add)
                            ins.then_inc(blocks_kept.handle, 1)
                            dve.wait_ge(numbers_set.handle, 1)
                            links.link(dve.tensor_copy(tile_no[:, :], tile_no_i[:, :]))
                            links.link(dve.tensor_tensor(tile_no[:, :], tile_no[:, :], tile_data[:, :, 1], ALU.add))
                            dve.tensor_copy(row_of_tile[:, :], tile_no[:, :]).then_inc(rows_known.handle, 1)
                            dve.tensor_scalar(block_of_tile[:, :], tile_data[:, :, 0], -1.0, None, ALU.add)
                            dve.wait_ge(rows_got.handle, 16 * TC)
                            dve.tensor_copy(tile_words[0][:, :, :], got[:, :, 0, :])
                            dve.tensor_copy(tile_words[2][:, :, :], got[:, :, 2, :].bitcast(F32))
                            links.link(dve.tensor_scalar(rows_bits[:, :, :], got[:, :, 1, :], 7, None, ALU.logical_shift_right))
                            links.link(dve.tensor_copy(rows_hi[:, :, :], rows_bits[:, :, :]))
                            links.link(dve.tensor_tensor(rows_hi[:, :, :], rows_hi[:, :, :], block_of_tile[:, :].unsqueeze(2).to_broadcast([P, TC, P]),
                                                         ALU.not_equal))
                            links.link(dve.tensor_scalar(rows_bits[:, :, :], got[:, :, 1, :], 127, None, ALU.bitwise_and))
                            links.link(dve.tensor_copy(tile_words[1][:, :, :], rows_bits[:, :, :]))
                            dve.scalar_tensor_tensor(out=tile_words[1][:, :, :], in0=rows_hi[:, :, :], scalar=ELSE_LANE,
                                                     in1=tile_words[1][:, :, :], op0=ALU.mult, op1=ALU.add).then_inc(words_set.handle, 1)
                            for q in range(TC):
                                k0, k1 = q * P, min(q * P + P, KT)
                                for w in range(3):
                                    n = 3 * q + w
                                    dve.wait_ge(words_turned.handle, n + 1)
                                    to = no_records[:, k0:k1, w]
                                    dve.tensor_copy(to if w == 0 else to.bitcast(F32), bank[4 + n % 4][:, 0:k1 - k0]).then_inc(words_kept.handle, 1)

        with ExitStack() as inner:
            place = [v["sb"](f"place{g}", [P, n], F32, inner) for g, (_, n) in enumerate(SG)]
            place_i = [v["sb"](f"place_i{g}", [P, n], I32, inner) for g, (_, n) in enumerate(SG)]
            tile_of = [v["sb"](f"tile_of{g}", [P, n], I32, inner) for g, (_, n) in enumerate(SG)]
            row_to = [v["sb"](f"row_to{g}", [P, n], I32, inner) for g, (_, n) in enumerate(SG)]
            record = [v["sb"](f"record{g}", [P, n, RW], I32, inner) for g, (_, n) in enumerate(SG)]
            ranked = v["sb"]("ranked", [P, NK], F32, inner)
            prefix = bank[0][:, 0:NK]

            def over_engine(eng, k, work):
                if k == "src":
                    work()
                else:
                    with eng.If(unsorted(eng, "general") > 0):
                        work()

            def sort_by(k):
                hot_set = signal(f"hot_set_{k}")
                hot_used = signal(f"hot_used_{k}")
                record_clear = signal(f"record_clear_{k}")
                prefix_set = signal(f"prefix_set_{k}")
                place_read = signal(f"place_read_{k}")
                rows_set = signal(f"rows_set_{k}")
                record_set = signal(f"record_set_{k}")
                scattered = [signal(f"scattered_{k}{g}") for g in range(2)]
                column_set = signal(f"column_set_{k}")
                steps = signal(f"sort_steps_{k}")
                with nc.Block() as block:
                    @block.tensor
                    def _(pe):
                        def work():
                            pe.matmul(prefix, ones[0:NK, :], place_diag[0:NK, :], start=True, stop=True, skip_group_check=True)

                            def count_column(t, c, first):
                                g, j = group_of(c % SU)
                                pe.wait_ge(column_set.handle, column_set.at(t * SU + c + 1))
                                pe.matmul(bank[1][0:NK, 0:P], pair_hi[g][:, j, 0:NK], pair_lo[g][:, j, :], start=first and c == 0,
                                          stop=True, skip_group_check=True)

                            def body(t, first):
                                for g, (c0, n) in enumerate(SG):
                                    pe.wait_ge(hot_set.handle, hot_set.at(t * 2 + g + 1))
                                    for j in range(n):
                                        pe.matmul(prefix, before_h[:, :], hot_hi[g][:, j, 0:NK], start=False, stop=True,
                                                  skip_group_check=True).then_inc(prefix_set.handle, 1)
                                        if k == "src" and not (first and c0 + j < PAIR_LAG):
                                            count_column(t, c0 + j - PAIR_LAG, first)
                                        pe.wait_ge(place_read.handle, place_read.at(t * SU + c0 + j + 1))
                                        ins = pe.matmul(prefix, rest_h[:, :], hot_hi[g][:, j, 0:NK], start=False, stop=True,
                                                        skip_group_check=True)
                                    ins.then_inc(hot_used.handle, 1)

                            turns(pe, ST, body)
                            if k == "src":
                                for c in range(PAIR_LAG):
                                    count_column(ST, c - PAIR_LAG, False)

                        over_engine(pe, k, work)

                    @block.vector
                    def _(dve):
                        def work():
                            links = Chain(dve, steps, 4)

                            def body(t, first):
                                links.turn(t)
                                for g, (c0, n) in enumerate(SG):
                                    if not first:
                                        dve.wait_ge(hot_used.handle, hot_used.at(t * 2 + g - 1))
                                    dve.tensor_tensor(hot_hi[g][:, :, :],
                                                      hi[k][:, bass.ds(t * SU + c0, n)].unsqueeze(2).to_broadcast([P, n, 100]),
                                                      iota[:, 0:100].unsqueeze(1).to_broadcast([P, n, 100]),
                                                      ALU.is_equal).then_inc(hot_set.handle, 1)
                                for g, (c0, n) in enumerate(SG):
                                    for j in range(n):
                                        dve.wait_ge(prefix_set.handle, prefix_set.at(t * SU + c0 + j + 1))
                                        dve.tensor_tensor_reduce(ranked[:, :], prefix, hot_hi[g][:, j, 0:NK], 1.0, 0.0, ALU.mult,
                                                                 ALU.add, place[g][:, j:j + 1]).then_inc(place_read.handle, 1)
                                        if k == "src":
                                            dst_col = bass.ds(t * SU + c0 + j, 1)
                                            dve.tensor_tensor(pair_hi[g][:, j:j + 1, :], hi["dst"][:, dst_col].unsqueeze(2).to_broadcast([P, 1, 100]),
                                                              iota[:, 0:100].unsqueeze(1), ALU.is_equal)
                                            dve.tensor_tensor(pair_lo[g][:, j:j + 1, :], lo["dst"][:, dst_col].unsqueeze(2).to_broadcast([P, 1, P]),
                                                              iota[:, :].unsqueeze(1), ALU.is_equal).then_inc(column_set.handle, 1)
                                    dve.wait_ge(place_read.handle, place_read.at(t * SU + c0 + n))
                                    links.link(dve.tensor_copy(place_i[g][:, :], place[g][:, :]))
                                    dve.tensor_scalar(tile_of[g][:, :], place_i[g][:, :], 7, None, ALU.logical_shift_right)
                                    links.link(dve.tensor_scalar(place_i[g][:, :], place_i[g][:, :], 127, None, ALU.bitwise_and))
                                    if not first:
                                        dve.wait_ge(scattered[g].handle, scattered[g].at(t * (16 * n)))
                                    dve.scalar_tensor_tensor(out=row_to[g][:, :], in0=place_i[g][:, :], scalar=float(KT),
                                                             in1=tile_of[g][:, :], op0=ALU.mult, op1=ALU.add).then_inc(rows_set.handle, 1)

                            turns(dve, ST, body)

                        over_engine(dve, k, work)

                    @block.scalar
                    def _(act):
                        def work():
                            act.wait_ge(record_clear.handle, record_clear.at(2))

                            def body(t, first):
                                for g, (c0, n) in enumerate(SG):
                                    if not first:
                                        act.wait_ge(scattered[g].handle, scattered[g].at(t * (16 * n)))
                                    cols = bass.ds(t * SU + c0, n)
                                    act.copy(record[g][:, :, 0:1], ends[other[k]][:, cols].unsqueeze(2))
                                    act.copy(record[g][:, :, 1:2].bitcast(F32), lo[k][:, cols].unsqueeze(2))
                                    act.copy(record[g][:, :, 2:3].bitcast(F32), weight[:, cols].unsqueeze(2)).then_inc(record_set.handle, 1)

                            turns(act, ST, body)

                        over_engine(act, k, work)

                    @block.gpsimd
                    def _(pool):
                        def work():
                            for g in range(2):
                                pool.memset(record[g][:, :, :], 0).then_inc(record_clear.handle, 1)

                            def body(t, first):
                                for g, (_, n) in enumerate(SG):
                                    pool.wait_ge(rows_set.handle, rows_set.at(t * 2 + g + 1))
                                    pool.wait_ge(record_set.handle, record_set.at(t * 2 + g + 1))
                                    pool.sem_inc(waits_passed.handle, 1)
                                    for j in range(n):
                                        pool.indirect_dma_start(
                                            out=records[k], out_offset=bass.IndirectOffsetOnAxis(ap=row_to[g][:, j:j + 1], axis=0),
                                            in_=record[g][:, j, :], in_offset=None, bounds_check=P * KT - 1,
                                            oob_is_err=False).then_inc(scattered[g].handle, 16)

                            turns(pool, ST, body)
                            for g, (_, n) in enumerate(SG):
                                pool.wait_ge(scattered[g].handle, scattered[g].at(16 * n * ST))

                        over_engine(pool, k, work)

            use_counts("src")
            sort_by("src")
            use_counts("dst")
            sort_by("dst")
            records_in_order()


def layers(nc, ctx, v):
    bank, ident, iota, norm, records, tile_block, waits_passed = (
        v[k] for k in ("bank", "ident", "iota", "norm", "records", "tile_block", "waits_passed"))
    sb, signal = v["sb"], v["signal"]
    x_in, out = v["x"], v["out"]
    FULL = (NB - 1) * P

    nodes = sb("nodes", [P, NB, D])
    sums = sb("sums", [P, NB * W_GAT])
    sums_conv = sums[:, 0:NB * D].rearrange("p (b w) -> p b w", w=D)
    sums_msg = sums_conv
    sums_cos = sums[:, 0:NB * W_COS].rearrange("p (b w) -> p b w", w=W_COS)
    sums_gat = sums[:, :].rearrange("p (b w) -> p b w", w=W_GAT)
    unit = sums[:, NB * W_COS:NB * (W_COS + D)].rearrange("p (b w) -> p b w", w=D)
    target = sb("target", [P, NB, 2 * HEADS])
    stats = sb("stats", [P, NB, 6])
    mean = sb("mean", [P, NB])
    rstd = sb("rstd", [P, NB])
    spread = sb("spread", [P, NB])
    block_row = sb("block_row", [1, KT], I32)

    record_in = [signal(f"record_in{h}") for h in range(2)]
    gathered = [signal(f"gathered{s}") for s in range(U)]
    hot_set = signal("walk_hot_set")
    product = signal("product")
    added = signal("added")
    hot_turned = signal("hot_turned")
    hot_kept = signal("hot_kept")
    target_set = signal("target_set")
    logit_set = signal("logit_set")
    exp_set = signal("exp_set")
    weighted = signal("weighted")
    weighted_act = signal("weighted_act")
    blocks_in = signal("blocks_in")
    chain = signal("chain_layers")
    block_staged = signal("block_staged")
    block_product = signal("block_product")
    block_rows = signal("block_rows")
    block_turned = signal("block_turned")
    turned_kept = signal("turned_kept")
    stored = [signal(f"stored{j}") for j in range(2)]
    root_in = signal("root_in")
    root_set = signal("root_set")
    x_loaded = signal("x_loaded")
    unit_set = signal("unit_set")
    sums_clear = signal("sums_clear")

    def walk(name, key, rows, width, kind):
        looks_up = kind in ("cos", "gat")
        banks = range(4, 8) if looks_up else range(8)
        with ExitStack() as scope:
            record = [sb(f"{name}_record{h}", [P, HU, RW], I32, scope) for h in range(2)]
            got = sb(f"{name}_got", [P, U, width], F32, scope)
            hot = sb(f"{name}_hot", [P, U, P], F32, scope)
            if looks_up:
                hotT = sb(f"{name}_hotT", [P, 8, P], F32, scope)
            if kind == "cos":
                hot_w = sb(f"{name}_hot_w", [P, 4, P], F32, scope)
                scratch = sb(f"{name}_scratch", [P, 4, D], F32, scope)
                cos = sb(f"{name}_cos", [P, U], F32, scope)
                exps = sb(f"{name}_exps", [P, U], F32, scope)
            if kind == "gat":
                logit = sb(f"{name}_logit", [P, 2, 4, HEADS], F32, scope)
                leaky = sb(f"{name}_leaky", [P, 2, 4, HEADS], F32, scope)
            acc = {"conv": sums_conv, "msg": sums_msg, "cos": sums_cos, "gat": sums_gat}[kind]
            list_v = records[key].rearrange("(p c) w -> p c w", c=KT)

            def word(s, n):
                return record[s // HU][:, s % HU, n:n + 1].bitcast(F32)

            def staged_turns(eng, stages):
                def body(t, first):
                    for i in range(U):
                        for stage, lag in stages:
                            if not (first and i < lag):
                                stage(t, i - lag, first)

                turns(eng, T, body)
                for i in range(max(lag for _, lag in stages)):
                    for stage, lag in stages:
                        if i < lag:
                            stage(T, i - lag, False)

            def block_of(eng, regs, t, c):
                if c % HU == 0:
                    eng.load(regs, block_row[0:1, bass.ds(t * U + c, HU)])
                return eng.snap(regs[c % HU], min_val=0, max_val=NB - 1)

            with nc.Block() as block:
                @block.sync
                def _(sp):
                    sp.dma_start(block_row[:, :], tile_block[key]).then_inc(blocks_in.handle, 16)

                    def body(t, first):
                        for h in range(2):
                            if not first:
                                sp.wait_ge(hot_set.handle, hot_set.at(t * U + (h + 1) * HU - U))
                                sp.sem_inc(waits_passed.handle, 1)
                                for s in range(h * HU, (h + 1) * HU):
                                    sp.wait_ge(gathered[s].handle, gathered[s].at(t * 16))
                                sp.sem_inc(waits_passed.handle, 1)
                            sp.dma_start(record[h][:, :, :], list_v[:, bass.ds(t * U + h * HU, HU), :]).then_inc(record_in[h].handle, 16)

                    turns(sp, T, body)

                @block.gpsimd
                def _(pool):
                    def body(t, first):
                        for s in range(U):
                            if s % HU == 0:
                                pool.wait_ge(record_in[s // HU].handle, record_in[s // HU].at(t * 16 + 16))
                            if s % 4 == 0 and not first:
                                pool.wait_ge(product.handle, product.at(t * U + s + 4 - U))
                                pool.sem_inc(waits_passed.handle, 1)
                            pool.indirect_dma_start(
                                out=got[:, s, :], out_offset=None, in_=rows,
                                in_offset=bass.IndirectOffsetOnAxis(ap=record[s // HU][:, s % HU, 0:1], axis=0),
                                bounds_check=N - 1, oob_is_err=False).then_inc(gathered[s].handle, 16)

                    turns(pool, T, body)

                @block.tensor
                def _(pe):
                    if looks_up:
                        regs = [pe.alloc_register(f"{name}_pe_block{j}") for j in range(HU)]
                        pe.wait_ge(blocks_in.handle, blocks_in.at(16))

                    def turn_hot(t, c, first):
                        s = c % U
                        pe.wait_ge(hot_set.handle, hot_set.at(t * U + c + 1))
                        if kind == "cos" and not (first and s < 2):
                            pe.wait_ge(hot_kept.handle, hot_kept.at(t * U + c - 1))
                        pe.transpose(bank[s % 2][:, 0:P], hot[:, s, :], ident[:, :]).then_inc(hot_turned.handle, 1)

                    def look_up(t, c, first):
                        s = c % U
                        b = block_of(pe, regs, t, c)
                        pe.wait_ge(hot_kept.handle, hot_kept.at(t * U + c + 1))
                        if kind == "cos":
                            if not (first and s < 2):
                                pe.wait_ge(logit_set.handle, logit_set.at(t * U + c - 1))
                            pe.matmul(bank[2 + s % 2][:, 0:D], hotT[:, s % 8, :], unit[:, bass.ds(b, 1), :],
                                      start=True, stop=True).then_inc(target_set.handle, 1)
                        else:
                            q = s // 4
                            if s % 4 == 0 and not (first and q < 2):
                                pe.wait_ge(logit_set.handle, logit_set.at(t * 4 + c // 4 - 1))
                            pe.matmul(bank[2 + q % 2][:, s % 4 * 8:s % 4 * 8 + 8], hotT[:, s % 8, :],
                                      target[:, bass.ds(b, 1), :], start=True, stop=True).then_inc(target_set.handle, 1)

                    def multiply(t, c, first):
                        s = c % U
                        if kind in ("conv", "msg"):
                            pe.wait_ge(hot_set.handle, hot_set.at(t * U + c + 1))
                            pe.wait_ge(gathered[s].handle, gathered[s].at(t * 16 + (c // U + 1) * 16))
                        else:
                            pe.wait_ge(weighted.handle, weighted.at(t * U + c + 1))
                        if kind == "gat":
                            pe.wait_ge(weighted_act.handle, weighted_act.at(t * U + c + 1))
                        left, right = {"conv": (got[:, s, :], hot[:, s, :]), "msg": (hot[:, s, :], got[:, s, :]),
                                       "cos": (hot_w[:, s % 4, :] if kind == "cos" else None, got[:, s, :]),
                                       "gat": (hot[:, s, :], got[:, s, :])}[kind]
                        pe.matmul(bank[banks[s % len(banks)]][:, 0:right.shape[-1]], left, right, start=True,
                                  stop=True).then_inc(product.handle, 1)

                    staged_turns(pe, {"conv": [(multiply, 0)], "msg": [(multiply, 0)],
                                      "cos": [(turn_hot, 0), (look_up, 3), (multiply, 8)],
                                      "gat": [(look_up, 2), (turn_hot, 0), (multiply, 9)]}[kind])

                @block.vector
                def _(dve):
                    regs = [dve.alloc_register(f"{name}_dve_block{j}") for j in range(HU)]
                    dve.wait_ge(blocks_in.handle, blocks_in.at(16))

                    def set_hot(t, c, first):
                        s = c % U
                        if s % HU == 0:
                            dve.wait_ge(record_in[s // HU].handle, record_in[s // HU].at(t * 16 + (c // U + 1) * 16))
                        if kind == "msg":
                            ins = dve.tensor_scalar(hot[:, s, :], iota[:, :], word(s, 1), word(s, 2), ALU.is_equal, ALU.mult)
                        else:
                            ins = dve.tensor_scalar(hot[:, s, :], iota[:, :], word(s, 1), None, ALU.is_equal)
                        ins.then_inc(hot_set.handle, 1)

                    def score(t, c, first):
                        s = c % U
                        dve.wait_ge(target_set.handle, target_set.at(t * U + c + 1))
                        dve.wait_ge(gathered[s].handle, gathered[s].at(t * 16 + (c // U + 1) * 16))
                        dve.tensor_tensor_reduce(scratch[:, s % 4, :], bank[2 + s % 2][:, 0:D], got[:, s, 0:D], 1.0, 0.0,
                                                 ALU.mult, ALU.add, cos[:, s:s + 1]).then_inc(logit_set.handle, 1)

                    def weigh_hot(t, c, first):
                        s = c % U
                        dve.wait_ge(exp_set.handle, exp_set.at(t * U + c + 1))
                        dve.tensor_scalar(hot_w[:, s % 4, :], hot[:, s, :], exps[:, s:s + 1], None,
                                          ALU.mult).then_inc(weighted.handle, 1)

                    def logits(t, c, first):
                        s = c % U
                        """leaky(el + er) - shift, for four tiles at once."""
                        if s % 4 != 3:
                            return
                        q = s // 4
                        dve.wait_ge(target_set.handle, target_set.at(t * U + c + 1))
                        for i in range(4):
                            dve.wait_ge(gathered[4 * q + i].handle, gathered[4 * q + i].at(t * 16 + (c // U + 1) * 16))
                        here = bank[2 + q % 2][:, 0:32].rearrange("p (i c) -> p i c", c=8)
                        a, b = logit[:, q % 2, :, :], leaky[:, q % 2, :, :]
                        dve.tensor_tensor(a, here[:, :, HEADS:], got[:, 4 * q:4 * q + 4, HID:], ALU.add).then_inc(chain.handle, 1)
                        dve.wait_ge(chain.handle, chain.at(t * 8 + c // 4 * 2 + 1))
                        dve.scalar_tensor_tensor(out=b, in0=a, scalar=0.2, in1=a, op0=ALU.mult, op1=ALU.max).then_inc(chain.handle, 1)
                        dve.wait_ge(chain.handle, chain.at(t * 8 + c // 4 * 2 + 2))
                        dve.tensor_tensor(a, b, here[:, :, 0:HEADS], ALU.subtract).then_inc(logit_set.handle, 1)

                    def weigh_rows(t, c, first):
                        s = c % U
                        dve.wait_ge(exp_set.handle, exp_set.at(t * 4 + c // 4 + 1))
                        feat = got[:, s, 0:VH * DH].rearrange("p (h d) -> p h d", h=VH)
                        dve.tensor_tensor(feat, feat, got[:, s, HID:HID + VH].unsqueeze(2).to_broadcast([P, VH, DH]),
                                          ALU.mult).then_inc(weighted.handle, 1)

                    def add(t, c, first):
                        s = c % U
                        b = block_of(dve, regs, t, c)
                        place = acc[:, bass.ds(b, 1), :]
                        dve.wait_ge(product.handle, product.at(t * U + c + 1))
                        if not (first and s == 0):
                            dve.wait_ge(added.handle, added.at(t * U + c))
                        dve.tensor_tensor(place, place, bank[banks[s % len(banks)]][:, 0:place.shape[-1]].unsqueeze(1),
                                          ALU.add).then_inc(added.handle, 1)

                    staged_turns(dve, {"conv": [(set_hot, 0), (add, 3)], "msg": [(set_hot, 0), (add, 3)],
                                       "cos": [(set_hot, 0), (score, 5), (weigh_hot, 7), (add, 9)],
                                       "gat": [(set_hot, 0), (logits, 4), (weigh_rows, 8), (add, 10)]}[kind])

                if looks_up:
                    @block.scalar
                    def _(act):
                        def keep_hot(t, c, first):
                            s = c % U
                            act.wait_ge(hot_turned.handle, hot_turned.at(t * U + c + 1))
                            act.copy(hotT[:, s % 8, :], bank[s % 2][:, 0:P]).then_inc(hot_kept.handle, 1)

                        def exp_cos(t, c, first):
                            s = c % U
                            act.wait_ge(logit_set.handle, logit_set.at(t * U + c + 1))
                            act.activation(exps[:, s:s + 1], cos[:, s:s + 1], ACT.Exp,
                                           scale=got[:, s, D:D + 1]).then_inc(exp_set.handle, 1)

                        def exp_gat(t, c, first):
                            s = c % U
                            if s % 4 == 3:
                                q = s // 4
                                act.wait_ge(logit_set.handle, logit_set.at(t * 4 + c // 4 + 1))
                                act.activation(got[:, 4 * q:4 * q + 4, HID:], logit[:, q % 2, :, :],
                                               ACT.Exp).then_inc(exp_set.handle, 1)

                        def weigh_heads(t, c, first):
                            s = c % U
                            """The heads that VectorE leaves."""
                            act.wait_ge(exp_set.handle, exp_set.at(t * 4 + c // 4 + 1))
                            for h in range(VH, HEADS):
                                feat = got[:, s, h * DH:(h + 1) * DH]
                                ins = act.activation(feat, feat, ACT.Copy, scale=got[:, s, HID + h:HID + h + 1])
                            ins.then_inc(weighted_act.handle, 1)

                        staged_turns(act, {"cos": [(exp_cos, 6), (keep_hot, 0)],
                                           "gat": [(keep_hot, 0), (exp_gat, 4), (weigh_heads, 8)]}[kind])
        for s in record_in:
            s.phase_over(16 * T)
        for s in gathered:
            s.phase_over(16 * T)
        blocks_in.phase_over(16)
        hot_set.phase_over(KT)
        product.phase_over(KT)
        added.phase_over(KT)
        if looks_up:
            hot_turned.phase_over(KT)
            hot_kept.phase_over(KT)
            target_set.phase_over(KT)
            weighted.phase_over(KT)
            for s in (logit_set, exp_set):
                s.phase_over(KT if kind == "cos" else KT // 4)
        if kind == "gat":
            chain.phase_over(KT // 2)

    def normalise_scales():
        with nc.Block() as block:
            @block.vector
            def _(dve):
                links = Chain(dve, chain, 6)
                links.turn(0)
                dve.tensor_tensor(mean[:, :], stats[:, :, 1], stats[:, :, 4], ALU.add)
                dve.tensor_tensor(rstd[:, :], stats[:, :, 1], stats[:, :, 4], ALU.subtract)
                links.link(dve.tensor_tensor(spread[:, :], stats[:, :, 2], stats[:, :, 5], ALU.add))
                links.link(dve.tensor_scalar(mean[:, :], mean[:, :], 0.5, None, ALU.mult))
                links.link(dve.scalar_tensor_tensor(out=rstd[:, :], in0=rstd[:, :], scalar=0.25, in1=rstd[:, :], op0=ALU.mult, op1=ALU.mult))
                links.link(dve.scalar_tensor_tensor(out=spread[:, :], in0=spread[:, :], scalar=1.0 / D, in1=rstd[:, :], op0=ALU.mult, op1=ALU.add))
                dve.tensor_scalar(spread[:, :], spread[:, :], EPS_LN, None, ALU.add).then_inc(root_in.handle, 1)
                dve.wait_ge(root_set.handle, root_set.at(1))
                links.link(dve.reciprocal(rstd[:, :], rstd[:, :]))

            @block.scalar
            def _(act):
                act.wait_ge(root_in.handle, root_in.at(1))
                act.activation(rstd[:, :], spread[:, :], ACT.Sqrt).then_inc(root_set.handle, 1)
        root_in.phase_over(1)
        root_set.phase_over(1)
        chain.phase_over(5)

    rows_out = staged = work = square = None

    def over_nodes(name, loop, *args):
        nonlocal rows_out, staged, work, square
        with ExitStack() as scope:
            rows_out = [sb(f"{name}_rows{j}", [P, W_GAT], F32, scope) for j in range(2)]
            staged = [sb(f"{name}_staged{j}", [P, KC * P], F32, scope) for j in range(2)]
            work = [sb(f"{name}_work{j}", [P, HID], F32, scope) for j in range(2)]
            square = [sb(f"{name}_square{j}", [P, 4], F32, scope) for j in range(2)]
            loop(*args)

    def blk(a, b):
        return a[:, bass.ds(b, 1), :].rearrange("p a w -> p (a w)")

    def col(a, b):
        return a[:, bass.ds(b, 1)]

    def store_rows(sp, table, width, t, first):
        for j in range(2):
            sp.wait_ge(block_rows.handle, block_rows.at(t * 2 + j + 1))
            sp.dma_start(table[bass.ds((t * 2 + j) * P, P), :], rows_out[j][:, 0:width]).then_inc(stored[j].handle, 16)

    def all_stored(sp):
        for j in range(2):
            sp.wait_ge(stored[j].handle, stored[j].at(16 * NT))

    def load_x():
        with nc.Block() as block:
            @block.gpsimd
            def _(pool):
                pool.memset(nodes[:, NB - 1, :], 0.0).then_inc(root_in.handle, 1)

            @block.sync
            def _(sp):
                sp.wait_ge(root_in.handle, root_in.at(1))
                sp.dma_start(nodes[:, 0:NB - 1, :], x_in[0:FULL, :].rearrange("(b p) d -> p b d", p=P)).then_inc(x_loaded.handle, 16)
                sp.dma_start(nodes[0:LAST, NB - 1, :], x_in[FULL:N, :]).then_inc(x_loaded.handle, 16)
                sp.wait_ge(x_loaded.handle, x_loaded.at(32))
        root_in.phase_over(1)

    def first_rows():
        SEG = 7
        count = NB // (2 * SEG)
        table = v["rows_conv"][0]
        with ExitStack() as scope:
            part = [sb(f"first_part{g}", [P, SEG, D], F32, scope) for g in range(2)]
            with nc.Block() as block:
                @block.vector
                def _(dve):
                    def body(t, first):
                        for g in range(2):
                            here = bass.ds((t * 2 + g) * SEG, SEG)
                            if not first:
                                dve.wait_ge(stored[g].handle, stored[g].at(t * 16))
                                dve.wait_ge(block_turned.handle, block_turned.at(t * SEG - (1 - g) * (SEG // 2)))
                            dve.tensor_tensor(part[g][:, :, :], nodes[:, here, :], norm["src"][:, here].unsqueeze(2).to_broadcast([P, SEG, D]),
                                              ALU.mult).then_inc(block_rows.handle, 1)

                    turns(dve, count, body)

                @block.sync
                def _(sp):
                    def body(t, first):
                        for g in range(2):
                            sp.wait_ge(block_rows.handle, block_rows.at(t * 2 + g + 1))
                            sp.dma_start(table[bass.ds((t * 2 + g) * SEG * P, SEG * P), :].rearrange("(b p) d -> p b d", p=P),
                                         part[g][:, :, :]).then_inc(stored[g].handle, 16)

                    turns(sp, count, body)
                    for g in range(2):
                        sp.wait_ge(stored[g].handle, stored[g].at(16 * count))

                @block.tensor
                def _(pe):
                    def body(t, first):
                        for i in range(2 * SEG):
                            g, pair = i // SEG, i // 2
                            if i % SEG == 0:
                                pe.wait_ge(block_rows.handle, block_rows.at(t * 2 + g + 1))
                            if i % 2 == 0 and not first:
                                pe.wait_ge(turned_kept.handle, turned_kept.at(t * SEG + pair + 1 - SEG))
                            ins = pe.transpose(bank[pair][:, i % 2 * P:(i % 2 + 1) * P], part[g][:, i % SEG, :], ident[:, :])
                            if i % 2 == 1:
                                ins.then_inc(block_turned.handle, 1)

                    turns(pe, count, body)

                @block.scalar
                def _(act):
                    def body(t, first):
                        for pair in range(SEG):
                            act.wait_ge(block_turned.handle, block_turned.at(t * SEG + pair + 1))
                            act.sem_inc(waits_passed.handle, 1)
                            act.copy(sums_conv[:, bass.ds((t * SEG + pair) * 2, 2), :],
                                     bank[pair][:, 0:2 * P].rearrange("p (b d) -> p b d", b=2)).then_inc(turned_kept.handle, 1)

                    turns(act, count, body)
        block_rows.phase_over(2 * count)
        block_turned.phase_over(SEG * count)
        turned_kept.phase_over(SEG * count)
        for g in range(2):
            stored[g].phase_over(16 * count)

    def conv_rows_loop():
        table = v["rows_conv"][1]
        per = 3
        with nc.Block() as block:
            @block.scalar
            def _(act):
                def stage_sums(t, first):
                    for j in range(2):
                        if not first:
                            act.wait_ge(block_product.handle, block_product.at(t * 2 + j - 1))
                            act.sem_inc(waits_passed.handle, 1)
                        act.copy(staged[j][:, 0:P], blk(sums_conv, t * 2 + j)).then_inc(block_staged.handle, 1)

                def keep_turned(t, first):
                    for j in range(2):
                        act.wait_ge(block_turned.handle, block_turned.at(t * 2 + j + 1))
                        act.sem_inc(waits_passed.handle, 1)
                        act.copy(blk(sums_conv, t * 2 + j), bank[2 + j][:, 0:P]).then_inc(turned_kept.handle, 1)

                lagged_turns(act, [(stage_sums, 0), (keep_turned, 1)])

            @block.tensor
            def _(pe):
                def multiply(t, first):
                    for j in range(2):
                        pe.wait_ge(block_staged.handle, block_staged.at(t * 2 + j + 1))
                        if not first:
                            pe.wait_ge(block_rows.handle, block_rows.at(t * 2 + j - 1))
                        pe.matmul(bank[j][:, 0:D], staged[j][:, 0:P], v["w1"][:, :], start=True, stop=True).then_inc(block_product.handle, 1)

                def turn_rows(t, first):
                    for j in range(2):
                        pe.wait_ge(block_rows.handle, block_rows.at(t * 2 + j + 1))
                        if not first:
                            pe.wait_ge(turned_kept.handle, turned_kept.at(t * 2 + j - 1))
                        pe.transpose(bank[2 + j][:, 0:P], rows_out[j][:, 0:D], ident[:, :]).then_inc(block_turned.handle, 1)

                lagged_turns(pe, [(multiply, 0), (turn_rows, 1)])

            @block.vector
            def _(dve):
                links = Chain(dve, chain, 2 * per)

                def body(t, first):
                    links.turn(t)
                    w = [work[j][:, 0:D] for j in range(2)]
                    for j in range(2):
                        dve.wait_ge(block_product.handle, block_product.at(t * 2 + j + 1))
                        links.note(dve.scalar_tensor_tensor(out=w[j], in0=bank[j][:, 0:D], scalar=col(norm["dst"], t * 2 + j),
                                                            in1=v["bn_scale"][:, :], op0=ALU.mult, op1=ALU.mult))
                    links.wait()
                    for j in range(2):
                        links.note(dve.tensor_tensor(w[j], w[j], v["bn_shift"][:, :], ALU.add))
                    links.wait()
                    for j in range(2):
                        links.note(dve.scalar_tensor_tensor(out=w[j], in0=w[j], scalar=0.01, in1=w[j], op0=ALU.mult, op1=ALU.max))
                    links.wait()
                    for j in range(2):
                        b = t * 2 + j
                        if not first:
                            dve.wait_ge(stored[j].handle, stored[j].at(t * 16))
                            dve.wait_ge(block_turned.handle, block_turned.at(t * 2 + j - 1))
                        dve.tensor_scalar(rows_out[j][:, 0:D], w[j], col(norm["src"], b), None,
                                          ALU.mult).then_inc(block_rows.handle, 1)

                turns(dve, NT, body)

            @block.sync
            def _(sp):
                turns(sp, NT, lambda t, first: store_rows(sp, table, D, t, first))
                all_stored(sp)
        block_staged.phase_over(NB)
        block_product.phase_over(NB)
        block_rows.phase_over(NB)
        block_turned.phase_over(NB)
        turned_kept.phase_over(NB)
        chain.phase_over(NT * 2 * per)
        for j in range(2):
            stored[j].phase_over(16 * NT)

    def conv_out_loop():
        with nc.Block() as block:
            @block.scalar
            def _(act):
                def body(t, first):
                    for j in range(2):
                        if not first:
                            act.wait_ge(block_product.handle, block_product.at(t * 2 + j - 1))
                            act.sem_inc(waits_passed.handle, 1)
                        act.copy(staged[j][:, 0:P], blk(sums_conv, t * 2 + j)).then_inc(block_staged.handle, 1)

                turns(act, NT, body)

            @block.tensor
            def _(pe):
                def body(t, first):
                    for j in range(2):
                        pe.wait_ge(block_staged.handle, block_staged.at(t * 2 + j + 1))
                        if not first:
                            pe.wait_ge(block_rows.handle, block_rows.at(t * 2 + j - 1))
                        pe.matmul(bank[j][:, 0:D], staged[j][:, 0:P], v["w2"][:, :], start=True, stop=True).then_inc(block_product.handle, 1)

                turns(pe, NT, body)

            @block.vector
            def _(dve):
                links = Chain(dve, chain, 2)

                def body(t, first):
                    links.turn(t)
                    for j in range(2):
                        dve.wait_ge(block_product.handle, block_product.at(t * 2 + j + 1))
                        dve.scalar_tensor_tensor(out=work[j][:, 0:D], in0=bank[j][:, 0:D], scalar=col(norm["dst"], t * 2 + j),
                                                 in1=v["b2_row"][:, :], op0=ALU.mult, op1=ALU.add).then_inc(block_rows.handle, 1)
                    dve.wait_ge(block_rows.handle, block_rows.at(t * 2 + 2))
                    for j in range(2):
                        here = blk(nodes, t * 2 + j)
                        links.note(dve.tensor_tensor(here, here, work[j][:, 0:D], ALU.add))
                    links.wait()
                    for j in range(2):
                        dve.bn_stats(blk(stats, t * 2 + j), blk(nodes, t * 2 + j))

                turns(dve, NT, body)
        block_staged.phase_over(NB)
        block_product.phase_over(NB)
        block_rows.phase_over(NB)
        chain.phase_over(NT * 2)

    def table_loop(kind):
        table, width, weights = {"msg": (v["rows_msg"], D, v["w_msgT"]), "cos": (v["rows_cos"], W_COS, v["w_cos"]),
                                 "gat": (v["rows_gat"], W_GAT, v["w_gat"])}[kind]
        cols = weights.shape[-1]
        per = {"msg": 0, "cos": 4, "gat": 0}[kind]
        with nc.Block() as block:
            @block.gpsimd
            def _(pool):
                pool.memset(sums[:, 0:NB * {"msg": D, "cos": W_COS, "gat": W_GAT}[kind]], 0.0).then_inc(sums_clear.handle, 1)
                pool.wait_ge(sums_clear.handle, sums_clear.at(1))

            @block.tensor
            def _(pe):
                def turn_nodes(t, first):
                    for j in range(2):
                        pe.wait_ge(block_staged.handle, block_staged.at(t * 2 + j + 1))
                        if not first:
                            pe.wait_ge(turned_kept.handle, turned_kept.at(t * 2 + j - 1))
                        pe.transpose(bank[2 + j][:, 0:P], staged[j][:, P:2 * P], ident[:, :]).then_inc(block_turned.handle, 1)

                def multiply(t, first):
                    for j in range(2):
                        pe.wait_ge(turned_kept.handle, turned_kept.at(t * 2 + j + 1))
                        if not first:
                            pe.wait_ge(block_rows.handle, block_rows.at(t * 2 + j - 1))
                        pe.matmul(bank[j][:, 0:cols], staged[j][:, 0:P], weights[:, :], start=True, stop=True).then_inc(block_product.handle, 1)

                lagged_turns(pe, [(turn_nodes, 0), (multiply, 1)])

            @block.scalar
            def _(act):
                def keep_turned(t, first):
                    for j in range(2):
                        act.wait_ge(block_turned.handle, block_turned.at(t * 2 + j + 1))
                        if not first:
                            act.wait_ge(block_product.handle, block_product.at(t * 2 + j - 1))
                        act.copy(staged[j][:, 0:P], bank[2 + j][:, 0:P]).then_inc(turned_kept.handle, 1)

                def roots(t, first):
                    for j in range(2):
                        act.wait_ge(root_in.handle, root_in.at(t * 2 + j + 1))
                        act.activation(square[j][:, 1:2], square[j][:, 0:1], ACT.Sqrt).then_inc(root_set.handle, 1)

                lagged_turns(act, [(keep_turned, 0)] + ([(roots, 1)] if kind == "cos" else []))

            @block.vector
            def _(dve):
                links = Chain(dve, chain, 2 * per)
                def normalise(t, first):
                    for j in range(2):
                        b = t * 2 + j
                        if not first:
                            dve.wait_ge(block_turned.handle, block_turned.at(t * 2 + j - 1))
                        dve.tensor_scalar(staged[j][:, P:2 * P], blk(nodes, b), col(mean, b), col(rstd, b), ALU.subtract,
                                          ALU.mult).then_inc(block_staged.handle, 1)
                    for j in range(2):
                        b = t * 2 + j
                        dve.tensor_scalar(blk(nodes, b), blk(nodes, b), col(mean, b), col(rstd, b), ALU.subtract, ALU.mult)

                def set_rows(t, first):
                    links.turn(t)
                    for j in range(2):
                        rows = rows_out[j]
                        dve.wait_ge(block_product.handle, block_product.at(t * 2 + j + 1))
                        if not first:
                            dve.wait_ge(stored[j].handle, stored[j].at(t * 16))
                        if kind == "cos" and not first:
                            dve.wait_ge(unit_set.handle, unit_set.at(t * 2 + j - 1))
                        if kind == "msg":
                            dve.tensor_tensor(rows[:, 0:D], bank[j][:, 0:D], v["b_msg_row"][:, :], ALU.add).then_inc(block_rows.handle, 1)
                        elif kind == "gat":
                            dve.tensor_scalar(blk(target, t * 2 + j), bank[j][:, HID:HID + 8], 1.0, None, ALU.mult)
                            dve.tensor_copy(rows[:, 0:W_GAT], bank[j][:, 0:W_GAT]).then_inc(block_rows.handle, 1)
                        else:
                            links.note(dve.tensor_copy(rows[:, 0:D], bank[j][:, 0:D]))
                    if kind == "cos":
                        links.wait()
                        for j in range(2):
                            rows = rows_out[j]
                            links.note(dve.tensor_tensor_reduce(work[j][:, 0:D], rows[:, 0:D], rows[:, 0:D], 1.0, 0.0, ALU.mult,
                                                                ALU.add, square[j][:, 0:1]))
                        links.wait()
                        for j in range(2):
                            dve.tensor_scalar(square[j][:, 0:1], square[j][:, 0:1], 1e-16, None, ALU.max).then_inc(root_in.handle, 1)
                        for j in range(2):
                            dve.wait_ge(root_set.handle, root_set.at(t * 2 + j + 1))
                            links.note(dve.reciprocal(square[j][:, 2:3], square[j][:, 1:2]))
                        links.wait()
                        for j in range(2):
                            dve.memset(rows_out[j][:, D + 1:D + 2], 1.0)
                            links.note(dve.tensor_copy(rows_out[j][:, D:D + 1], square[j][:, 2:3]))
                        links.wait()
                        for j in range(2):
                            dve.sem_inc(block_rows.handle, 1)
                        for j in range(2):
                            dve.tensor_scalar(blk(unit, t * 2 + j), rows_out[j][:, 0:D], square[j][:, 2:3], None, ALU.mult).then_inc(unit_set.handle, 1)

                lagged_turns(dve, [(normalise, 0), (set_rows, 1)])

            @block.sync
            def _(sp):
                turns(sp, NT, lambda t, first: store_rows(sp, table, width, t, first))
                all_stored(sp)
        for s in (block_staged, block_product, block_rows, block_turned, turned_kept):
            s.phase_over(NB)
        sums_clear.phase_over(1)
        if kind == "cos":
            unit_set.phase_over(NB)
            root_in.phase_over(NB)
            root_set.phase_over(NB)
        chain.phase_over(NT * 2 * per)
        for j in range(2):
            stored[j].phase_over(16 * NT)

    def node_stats(dve):
        with dve.Fori(0, NT) as t:
            for j in range(2):
                dve.bn_stats(blk(stats, t * 2 + j), blk(nodes, t * 2 + j))

    def msg_out():
        with nc.Block() as block:
            @block.vector
            def _(dve):
                links = Chain(dve, chain, 1)
                links.turn(0)
                links.link(dve.scalar_tensor_tensor(out=nodes[:, :, :], in0=sums_msg[:, :, :], scalar=0.0, in1=nodes[:, :, :],
                                                    op0=ALU.max, op1=ALU.add))
                node_stats(dve)
        chain.phase_over(1)

    def cos_out():
        with nc.Block() as block:
            @block.vector
            def _(dve):
                links = Chain(dve, chain, 4)
                links.turn(0)
                links.link(dve.tensor_scalar(spread[:, :], sums_cos[:, :, D + 1], EPS_ATT, None, ALU.add))
                links.link(dve.reciprocal(spread[:, :], spread[:, :]))
                shared = sums_cos[:, :, 0:D]
                links.link(dve.tensor_tensor(shared, shared, spread[:, :].unsqueeze(2).to_broadcast([P, NB, D]), ALU.mult))
                links.link(dve.tensor_tensor(nodes[:, :, :], nodes[:, :, :], shared, ALU.add))
                node_stats(dve)
        chain.phase_over(4)

    el_ends = sb("el_ends", [P, 2 * HEADS])
    el_ends_all = sb("el_ends_all", [P, 2 * HEADS])
    el_range = sb("el_range", [P, HEADS])
    wide_i = sb("wide_i", [P, 1], I32)

    def gat_shift():
        with nc.Block() as block:
            @block.vector
            def _(dve):
                links = Chain(dve, chain, 8)
                links.turn(0)
                for h in range(HEADS):
                    dve.tensor_reduce(el_ends[:, h:h + 1], target[:, :, h], AX.X, ALU.max)
                    ins = dve.tensor_reduce(el_ends[:, HEADS + h:HEADS + h + 1], target[:, :, h], AX.X, ALU.min)
                links.link(ins)
                links.link(dve.tensor_scalar(el_ends[:, HEADS:], el_ends[:, HEADS:], -1.0, None, ALU.mult))
                dve.sem_inc(root_in.handle, 1)
                dve.wait_ge(root_set.handle, root_set.at(1))
                links.link(dve.tensor_copy(target[:, :, 0:HEADS], el_ends_all[:, 0:HEADS].unsqueeze(1).to_broadcast([P, NB, HEADS])))
                links.link(dve.tensor_tensor(el_range[:, :], el_ends_all[:, 0:HEADS], el_ends_all[:, HEADS:], ALU.add))
                links.link(dve.tensor_reduce(spread[:, 0:1], el_range[:, :], AX.X, ALU.max))
                links.link(dve.tensor_scalar(spread[:, 0:1], spread[:, 0:1], WIDE, None, ALU.is_lt))
                links.link(dve.tensor_copy(wide_i[:, :], spread[:, 0:1]))

            @block.gpsimd
            def _(pool):
                pool.wait_ge(root_in.handle, root_in.at(1))
                pool.partition_all_reduce(el_ends_all[:, :], el_ends[:, :], P, bass.bass_isa.ReduceOp.max).then_inc(root_set.handle, 1)
        root_in.phase_over(1)
        root_set.phase_over(1)
        chain.phase_over(7)
        max_of_edges()
        with nc.Block() as block:
            @block.vector
            def _(dve):
                links = Chain(dve, chain, 2)
                links.turn(0)
                shift = target[:, :, 0:HEADS]
                links.link(dve.tensor_tensor(shift, shift, target[:, :, HEADS:2 * HEADS], ALU.add))
                links.link(dve.scalar_tensor_tensor(out=shift, in0=shift, scalar=0.2, in1=shift, op0=ALU.mult, op1=ALU.max))
        chain.phase_over(2)

    def max_of_edges():
        list_v = records["dst"].rearrange("(p c) w -> p c w", c=KT)
        with ExitStack() as scope:
            record = sb("max_record", [P, 1, RW], I32, scope)
            got = sb("max_got", [P, W_GAT], F32, scope)
            hot = sb("max_hot", [P, P], F32, scope)
            outside = sb("max_outside", [P, P], F32, scope)
            spread_el = sb("max_spread_el", [P, HEADS, P], F32, scope)
            tile_max = sb("tile_max", [P, HEADS], F32, scope)
            max_blocks_in = signal("max_blocks_in")
            max_record_in = signal("max_record_in")
            max_gathered = signal("max_gathered")
            max_turned = signal("max_turned")
            max_steps = signal("max_steps")

            def narrow(eng, name):
                reg = eng.alloc_register(f"{name}_narrow")
                eng.load(reg, wide_i[0:1, 0:1])
                return eng.snap(reg, min_val=0, max_val=1)

            with nc.Block() as block:
                @block.sync
                def _(sp):
                    with sp.If(narrow(sp, "sp") < 1):
                        sp.dma_start(block_row[:, :], tile_block["dst"]).then_inc(max_blocks_in.handle, 16)

                        def body(t, first):
                            if not first:
                                sp.wait_ge(max_steps.handle, 5 * t + 1)
                                sp.sem_inc(waits_passed.handle, 1)
                            sp.dma_start(record[:, :, :], list_v[:, bass.ds(t, 1), :]).then_inc(max_record_in.handle, 16)

                        turns(sp, KT, body)

                @block.gpsimd
                def _(pool):
                    with pool.If(narrow(pool, "pool") < 1):
                        def body(t, first):
                            pool.wait_ge(max_record_in.handle, 16 * t + 16)
                            pool.sem_inc(waits_passed.handle, 1)
                            pool.indirect_dma_start(
                                out=got[:, :], out_offset=None, in_=v["rows_gat"],
                                in_offset=bass.IndirectOffsetOnAxis(ap=record[:, 0, 0:1], axis=0),
                                bounds_check=N - 1, oob_is_err=False).then_inc(max_gathered.handle, 16)

                        turns(pool, KT, body)

                @block.tensor
                def _(pe):
                    with pe.If(narrow(pe, "pe") < 1):
                        def body(t, first):
                            pe.wait_ge(max_steps.handle, 5 * t + 4)
                            for h in range(HEADS):
                                ins = pe.transpose(bank[0][:, h * P:(h + 1) * P], spread_el[:, h, :], ident[:, :])
                            ins.then_inc(max_turned.handle, 1)

                        turns(pe, KT, body)

                @block.vector
                def _(dve):
                    with dve.If(narrow(dve, "dve") < 1):
                        block_reg = dve.alloc_register("max_block")
                        dve.memset(target[:, :, 0:HEADS], LOW).then_inc(max_steps.handle, 1)
                        dve.wait_ge(max_blocks_in.handle, 16)

                        def body(t, first):
                            dve.load(block_reg, block_row[0:1, bass.ds(t, 1)])
                            b = dve.snap(block_reg, min_val=0, max_val=NB - 1)
                            dve.wait_ge(max_gathered.handle, 16 * t + 16)
                            dve.tensor_scalar(hot[:, :], iota[:, :], record[:, 0, 1:2].bitcast(F32), None,
                                              ALU.is_equal).then_inc(max_steps.handle, 1)
                            dve.wait_ge(max_steps.handle, 5 * t + 2)
                            dve.tensor_scalar(outside[:, :], hot[:, :], -LOW, LOW, ALU.mult, ALU.add).then_inc(max_steps.handle, 1)
                            dve.wait_ge(max_steps.handle, 5 * t + 3)
                            for h in range(HEADS):
                                ins = dve.scalar_tensor_tensor(out=spread_el[:, h, :], in0=hot[:, :], scalar=got[:, HID + h:HID + h + 1],
                                                               in1=outside[:, :], op0=ALU.mult, op1=ALU.add)
                            ins.then_inc(max_steps.handle, 1)
                            dve.wait_ge(max_turned.handle, t + 1)
                            dve.tensor_reduce(tile_max[:, :], bank[0][:, :].rearrange("p (h e) -> p h e", h=HEADS), AX.X,
                                              ALU.max).then_inc(max_steps.handle, 1)
                            dve.wait_ge(max_steps.handle, 5 * t + 5)
                            place = target[:, bass.ds(b, 1), 0:HEADS]
                            dve.tensor_tensor(place, place, tile_max[:, :].unsqueeze(1), ALU.max).then_inc(max_steps.handle, 1)
                            dve.wait_ge(max_steps.handle, 5 * t + 6)

                        turns(dve, KT, body)

    def gat_out_loop():
        with ExitStack() as scope:
            hT = sb("hT", [P, KC, 2 * P], F32, scope)
            gate = {k: sb(f"gate_{k}", [P, KC, 2 * P], F32, scope) for k in ("r", "z", "n")}
            state = sb("state", [P, KC, 2 * P], F32, scope)
            share = [sb(f"share{j}", [P, HEADS], F32, scope) for j in range(2)]
            attended = signal("attended")
            attended_turned = signal("attended_turned")
            attended_kept = signal("attended_kept")
            gate_sum = signal("gate_sum")
            rz_set = signal("rz_set")
            n_in = signal("n_in")
            n_set = signal("n_set")
            state_set = signal("state_set")
            result = signal("result")
            nodes_set = signal("nodes_set")
            attend_steps = signal("attend_steps")
            add_steps = signal("add_steps")

            with nc.Block() as block:
                @block.vector
                def _(dve):
                    attend_links = Chain(dve, attend_steps, 2 * 3)
                    add_links = Chain(dve, add_steps, 2 * 2)

                    def attend(t, first):
                        attend_links.turn(t)
                        for j in range(2):
                            b = t * 2 + j
                            w = work[j]
                            attend_links.link(dve.tensor_scalar(share[j][:, :], sums_gat[:, bass.ds(b, 1), HID:].rearrange("p a w -> p (a w)"),
                                                                1e-30, None, ALU.max))
                            attend_links.link(dve.reciprocal(share[j][:, :], share[j][:, :]))
                            if not first:
                                dve.wait_ge(attended_turned.handle, attended_turned.at(t * 2 + j - 1))
                            attend_links.link(dve.tensor_tensor(w[:, :].rearrange("p (h d) -> p h d", h=HEADS),
                                                                sums_gat[:, bass.ds(b, 1), 0:HID].rearrange("p a (h d) -> p (a h) d", h=HEADS),
                                                                share[j][:, :].unsqueeze(2).to_broadcast([P, HEADS, DH]), ALU.mult))
                            dve.tensor_tensor(w[:, :], w[:, :], v["bias_gat_row"][:, :], ALU.add).then_inc(attended.handle, 1)

                    def new_gate(t, first):
                        dve.wait_ge(rz_set.handle, rz_set.at(t * 2 + 1))
                        dve.wait_ge(gate_sum.handle, gate_sum.at(t * 3 + 3))
                        if not first:
                            dve.wait_ge(state_set.handle, state_set.at(t))
                        for c in range(KC):
                            ins = dve.scalar_tensor_tensor(out=gate["n"][:, c, :], in0=gate["r"][:, c, :], scalar=v["b_hid_n"][:, c:c + 1],
                                                           in1=bank[6][:, c * 2 * P:(c + 1) * 2 * P], op0=ALU.mult, op1=ALU.add)
                        ins.then_inc(n_in.handle, 1)

                    def new_state(t, first):
                        dve.wait_ge(rz_set.handle, rz_set.at(t * 2 + 2))
                        dve.wait_ge(n_set.handle, n_set.at(t + 1))
                        if not first:
                            dve.wait_ge(result.handle, result.at(t * 2))
                        dve.tensor_tensor(state[:, :, :], gate["z"][:, :, :], gate["n"][:, :, :], ALU.mult).then_inc(state_set.handle, 1)

                    def add_result(t, first):
                        add_links.turn(t)
                        for j in range(2):
                            b = t * 2 + j
                            dve.wait_ge(result.handle, result.at(t * 2 + j + 1))
                            add_links.link(dve.tensor_tensor(staged[j][:, 0:D], bank[3 + 4 * j][:, 0:D], v["b_out_row"][:, :], ALU.add))
                            add_links.link(dve.tensor_tensor(blk(nodes, b), blk(nodes, b), staged[j][:, 0:D], ALU.add))
                            ins = dve.bn_stats(blk(stats, b), blk(nodes, b))
                        ins.then_inc(nodes_set.handle, 1)

                    lagged_turns(dve, [(attend, 0), (add_result, 3), (new_state, 2), (new_gate, 1)])

                @block.tensor
                def _(pe):
                    def turn_attended(t, first):
                        for j in range(2):
                            pe.wait_ge(attended.handle, attended.at(t * 2 + j + 1))
                            if not first:
                                pe.wait_ge(attended_kept.handle, attended_kept.at(t * 2 + j - 1))
                            for c in range(KC):
                                ins = pe.transpose(bank[j][:, c * P:(c + 1) * P], work[j][:, c * P:(c + 1) * P], ident[:, :])
                            ins.then_inc(attended_turned.handle, 1)

                    def gates(t, first):
                        pe.wait_ge(attended_kept.handle, attended_kept.at(t * 2 + 2))
                        if not first:
                            pe.wait_ge(rz_set.handle, rz_set.at(t * 2))
                        for g in range(3):
                            if g == 2 and not first:
                                pe.wait_ge(n_in.handle, n_in.at(t))
                            for c in range(KC):
                                for k in range(KC):
                                    row = (g * KC + c) * P
                                    ins = pe.matmul(bank[4 + g][:, c * 2 * P:(c + 1) * 2 * P], v["w_ihT"][:, k, row:row + P],
                                                    hT[:, k, :], start=(k == 0), stop=(k == KC - 1))
                            ins.then_inc(gate_sum.handle, 1)

                    def project(t, first):
                        pe.wait_ge(state_set.handle, state_set.at(t + 1))
                        if not first:
                            pe.wait_ge(nodes_set.handle, nodes_set.at(t))
                        for j in range(2):
                            for k in range(KC):
                                ins = pe.matmul(bank[3 + 4 * j][:, 0:D], state[:, k, j * P:(j + 1) * P], v["w_outT"][:, k, :],
                                                start=(k == 0), stop=(k == KC - 1))
                            ins.then_inc(result.handle, 1)

                    lagged_turns(pe, [(project, 3), (gates, 1), (turn_attended, 0)])

                @block.scalar
                def _(act):
                    def keep_attended(t, first):
                        for j in range(2):
                            act.wait_ge(attended_turned.handle, attended_turned.at(t * 2 + j + 1))
                            if not first:
                                act.wait_ge(gate_sum.handle, gate_sum.at(t * 3))
                            act.copy(hT[:, :, j * P:(j + 1) * P],
                                     bank[j][:, 0:KC * P].rearrange("p (c n) -> p c n", c=KC)).then_inc(attended_kept.handle, 1)

                    def sigmoids(t, first):
                        if not first:
                            act.wait_ge(n_in.handle, n_in.at(t))
                            act.wait_ge(state_set.handle, state_set.at(t))
                        for n, k in enumerate("rz"):
                            act.wait_ge(gate_sum.handle, gate_sum.at(t * 3 + n + 1))
                            for c in range(KC):
                                ins = act.activation(gate[k][:, c, :], bank[4 + n][:, c * 2 * P:(c + 1) * 2 * P], ACT.Sigmoid,
                                                     bias=v["b_gate"][:, n * KC + c:n * KC + c + 1], scale=(1.0, -1.0)[n])
                            ins.then_inc(rz_set.handle, 1)

                    def tanh(t, first):
                        act.wait_ge(n_in.handle, n_in.at(t + 1))
                        for c in range(KC):
                            ins = act.activation(gate["n"][:, c, :], gate["n"][:, c, :], ACT.Tanh,
                                                 bias=v["b_gate"][:, 2 * KC + c:2 * KC + c + 1])
                        ins.then_inc(n_set.handle, 1)

                    lagged_turns(act, [(keep_attended, 1), (tanh, 2), (sigmoids, 1)])

    def write_out():
        parts = 7
        size = NB // parts
        with nc.Block() as block:
            @block.vector
            def _(dve):
                links = Chain(dve, chain, parts)
                links.turn(0)
                for q in range(parts):
                    here = nodes[:, q * size:(q + 1) * size, :]
                    links.link(dve.tensor_tensor(here, here, mean[:, q * size:(q + 1) * size].unsqueeze(2).to_broadcast([P, size, D]),
                                                 ALU.subtract))
                    dve.tensor_tensor(here, here, rstd[:, q * size:(q + 1) * size].unsqueeze(2).to_broadcast([P, size, D]),
                                      ALU.mult).then_inc(block_staged.handle, 1)

            @block.sync
            def _(sp):
                for q in range(parts):
                    sp.wait_ge(block_staged.handle, block_staged.at(q + 1))
                    b0, b1 = q * size, min((q + 1) * size, NB - 1)
                    sp.dma_start(out[b0 * P:b1 * P, :].rearrange("(b p) d -> p b d", p=P), nodes[:, b0:b1, :]).then_inc(stored[0].handle, 16)
                sp.dma_start(out[FULL:N, :], nodes[0:LAST, NB - 1, :]).then_inc(stored[0].handle, 16)
                sp.wait_ge(stored[0].handle, stored[0].at(16 * (parts + 1)))
        block_staged.phase_over(parts)
        stored[0].phase_over(16 * (parts + 1))
        chain.phase_over(parts)

    load_x()
    first_rows()
    walk("conv1", "dst", v["rows_conv"][0], D, "conv")
    over_nodes("between", conv_rows_loop)
    walk("conv2", "dst", v["rows_conv"][1], D, "conv")
    over_nodes("conv_out", conv_out_loop)
    normalise_scales()
    if v.get("stop") == 1:
        return write_out()
    over_nodes("msg_rows", table_loop, "msg")
    walk("msg", "dst", v["rows_msg"], D, "msg")
    msg_out()
    normalise_scales()
    if v.get("stop") == 2:
        return write_out()
    over_nodes("cos_rows", table_loop, "cos")
    walk("cos", "src", v["rows_cos"], W_COS, "cos")
    cos_out()
    normalise_scales()
    if v.get("stop") == 3:
        return write_out()
    over_nodes("gat_rows", table_loop, "gat")
    gat_shift()
    walk("gat", "dst", v["rows_gat"], W_GAT, "gat")
    over_nodes("gat_out", gat_out_loop)
    normalise_scales()
    write_out()


_INS = {"x": "x", "src": "src", "dst": "dst", "edge_weight": "edge_weight", "L0_gnn_W1": "W1", "L0_gnn_b1": "b1",
        "L0_gnn_W2": "W2", "L0_gnn_b2": "b2", "L0_gnn_gamma": "gamma", "L0_gnn_beta": "beta",
        "L0_gnn_run_mean": "run_mean", "L0_gnn_run_var": "run_var", "L1_gnn_W": "W_msg", "L1_gnn_b": "b_msg",
        "L2_gnn_kernel": "W_cos", "L3_gnn_W_fc": "W_fc", "L3_gnn_attn_l": "attn_l", "L3_gnn_attn_r": "attn_r",
        "L3_gnn_bias_gat": "bias_gat", "L3_gnn_W_ih": "W_ih", "L3_gnn_b_ih": "b_ih", "L3_gnn_b_hh": "b_hh",
        "L3_gnn_W_out": "W_out", "L3_gnn_b_out": "b_out"}


def kernel(**inputs):
    import numpy as _np
    import concourse.bacc as _bacc
    from concourse import mybir as _mybir
    from concourse.bass_utils import run_bass_kernel_spmd as _run

    nc = _bacc.Bacc("TRN2", target_bir_lowering=False, num_devices=1)
    arrays, args = {}, {}
    for name, short in _INS.items():
        a = _np.ascontiguousarray(inputs[name])
        arrays[f"in_{name}_dram"] = a
        args[short] = nc.dram_tensor(f"in_{name}_dram", a.shape, _mybir.dt.from_np(a.dtype), kind="ExternalInput").ap()
    args["out"] = nc.dram_tensor("out_0_dram", (N, D), F32, kind="ExternalOutput").ap()
    program(nc, **args)
    r = _run(nc, [arrays], core_ids=[0])
    return r.results[0]["out_0_dram"]
```
